# Optimizing a Trainium2 kernel written in Bass

```python
import numpy as np
import jax
import jax.numpy as jnp

def _softmax(x, axis=-1):
    return jax.nn.softmax(x, axis=axis)

def _gelu(x):
    return jax.nn.gelu(x, approximate=True)

def _silu(x):
    return jax.nn.silu(x)

def _sigmoid(x):
    return jax.nn.sigmoid(x)

def _layernorm(x, axis=-1, eps=1e-05):
    m = jnp.mean(x, axis=axis, keepdims=True)
    v = jnp.var(x, axis=axis, keepdims=True)
    return (x - m) / jnp.sqrt(v + eps)

def _scatter_add(tgt, idx, src, axis=0):
    return tgt.at[idx].add(src)

def _segment_sum(src, seg, n):
    return jax.ops.segment_sum(src, seg, n)
kernel_name = 'mk_gnn_ffn_d2_gnn_r32_d44595'

def setup_inputs(seed: int=0):
    np.random.seed(seed)
    _w = jnp.asarray

    def _rec_inputs():
        import jax
        import jax.numpy as jnp
        _gk = jax.random.key(seed)
        x = -0.0003713 + 1 * jax.random.normal(jax.random.fold_in(_gk, 1), (3125, 256), jnp.float32)
        _s = jax.random.randint(jax.random.fold_in(_gk, 2), (25000,), 0, 3125, jnp.int32)
        _d = jax.random.randint(jax.random.fold_in(_gk, 3), (25000,), 0, 3125, jnp.int32)
        _loop = jnp.arange(3125, dtype=jnp.int32)
        src = jnp.concatenate([_s, _d, _loop])
        dst = jnp.concatenate([_d, _s, _loop])
        _o = jnp.argsort(dst, stable=True)
        src = src[_o]
        dst = dst[_o]
        edge_attr_128 = 0.000167468 + 1.0002 * jax.random.normal(jax.random.fold_in(_gk, 11), (53125, 128), jnp.float32)
        edge_attr_3 = -1.09012e-05 + 0.99985 * jax.random.normal(jax.random.fold_in(_gk, 12), (53125, 3), jnp.float32)
        return (x, src, dst, edge_attr_128, edge_attr_3)
    x, src, dst, edge_attr_128, edge_attr_3 = _rec_inputs()

    def _L0_gnn_setup():
        import jax, jax.numpy as jnp
        import numpy as np
        N = 50000
        E = 12500
        IN = 256
        H = 8
        D = 32
        EF = 3
        key = jax.random.key(seed)
        ks = jax.random.split(key, 8)
        x = jax.random.normal(ks[0], (N, IN), dtype=jnp.float32)
        edge_index = jax.random.randint(ks[1], (2, E), 0, N, dtype=jnp.int64)
        edge_attr = jax.random.normal(ks[2], (E, EF), dtype=jnp.float32)
        W = jax.random.normal(ks[3], (H * D, IN), dtype=jnp.float32) * np.float32(np.sqrt(2.0 / (IN + H * D)))
        a_src = jax.random.normal(ks[4], (H, D), dtype=jnp.float32) * np.float32(np.sqrt(2.0 / (H + D)))
        a_dst = jax.random.normal(ks[5], (H, D), dtype=jnp.float32) * np.float32(np.sqrt(2.0 / (H + D)))
        edge_W = jax.random.normal(ks[6], (H * D, EF), dtype=jnp.float32) * np.float32(np.sqrt(2.0 / (EF + H * D)))
        edge_b = jnp.zeros((H * D,), dtype=jnp.float32)
        bias = jnp.zeros((H * D,), dtype=jnp.float32)
        return {'x': x, 'W': W, 'a_src': a_src, 'a_dst': a_dst, 'edge_W': edge_W, 'edge_b': edge_b, 'bias': bias, 'edge_attr': edge_attr, 'edge_index': edge_index}
    _L0_gnn_all = _L0_gnn_setup()
    _L0_gnn_in = {k: v for k, v in _L0_gnn_all.items() if k in ('W', 'a_src', 'a_dst', 'edge_W', 'edge_b', 'bias')}
    del _L0_gnn_all

    def _L0_ffn_setup():
        import jax, jax.numpy as jnp
        import numpy as np
        B, S, D, H, E, K = (8, 256, 256, 1024, 8, 2)
        key = jax.random.key(seed)
        ks = jax.random.split(key, 7)
        s_in = 1.0 / np.sqrt(D)
        s_hid = 1.0 / np.sqrt(H)
        return {'x': jax.random.normal(ks[0], (B, S, D), dtype=jnp.float32), 'Wg': jax.random.uniform(ks[1], (E, D), jnp.float32, -s_in, s_in), 'bg': jax.random.uniform(ks[2], (E,), jnp.float32, -s_in, s_in), 'W1': jax.random.uniform(ks[3], (E, H, D), jnp.float32, -s_in, s_in), 'b1': jax.random.uniform(ks[4], (E, H), jnp.float32, -s_in, s_in), 'W2': jax.random.uniform(ks[5], (E, D, H), jnp.float32, -s_hid, s_hid), 'b2': jax.random.uniform(ks[6], (E, D), jnp.float32, -s_hid, s_hid)}
    _L0_ffn_all = _L0_ffn_setup()
    _L0_ffn_in = {k: v for k, v in _L0_ffn_all.items() if k in ('Wg', 'bg', 'W1', 'b1', 'W2', 'b2')}
    del _L0_ffn_all

    def _L1_gnn_setup():
        import jax, jax.numpy as jnp
        import numpy as np
        N = 625
        E = 10000
        D = 256
        ED = 128
        L = 5
        BN_EPS = 1e-05
        key = jax.random.key(seed)
        ks = jax.random.split(key, 12)
        inp = {'input_feature': jax.random.normal(ks[0], (N, D), jnp.float32), 'edge_index': jax.random.randint(ks[1], (2, E), 0, N, jnp.int64) if jax.config.jax_enable_x64 else jax.random.randint(ks[1], (2, E), 0, N, jnp.int32), 'edge_attr': jax.random.normal(ks[2], (E, ED), jnp.float32), 'W': jax.random.normal(ks[3], (L, D, D), jnp.float32) * (1.0 / np.sqrt(D)), 'b': jax.random.normal(ks[4], (L, D), jnp.float32) * 0.02, 'root': jax.random.normal(ks[5], (L, D), jnp.float32) * 0.02, 'We': jax.random.normal(ks[6], (L, ED, D), jnp.float32) * (1.0 / np.sqrt(ED)), 'be': jax.random.normal(ks[7], (L, D), jnp.float32) * 0.02, 'gamma': jnp.ones((L, D), jnp.float32), 'beta': jnp.zeros((L, D), jnp.float32)}
        return inp
    _L1_gnn_all = _L1_gnn_setup()
    _L1_gnn_in = {k: v for k, v in _L1_gnn_all.items() if k in ('W', 'b', 'root', 'We', 'be', 'gamma', 'beta')}
    del _L1_gnn_all

    def _L1_ffn_setup():
        import math
        import jax, jax.numpy as jnp
        import numpy as np
        CAPACITY_FACTOR = 1.25
        key = jax.random.key(seed)
        ks = jax.random.split(key, 5)
        B, L, D, F, E = (8, 256, 256, 1024, 8)
        h = jax.random.normal(ks[0], (B, L, D), dtype=jnp.float32)
        gate_w = jax.random.normal(ks[1], (D, E), dtype=jnp.float32) * 0.02
        gate_b = jnp.zeros((E,), dtype=jnp.float32)
        w1 = jax.random.normal(ks[2], (E, D, F), dtype=jnp.float32) * (1.0 / math.sqrt(D))
        b1 = jnp.zeros((E, F), dtype=jnp.float32)
        w2 = jax.random.normal(ks[3], (E, F, D), dtype=jnp.float32) * (1.0 / math.sqrt(F))
        b2 = jnp.zeros((E, D), dtype=jnp.float32)
        return {'h': h, 'gate_w': gate_w, 'gate_b': gate_b, 'w1': w1, 'b1': b1, 'w2': w2, 'b2': b2}
    _L1_ffn_all = _L1_ffn_setup()
    _L1_ffn_in = {k: v for k, v in _L1_ffn_all.items() if k in ('gate_w', 'gate_b', 'w1', 'b1', 'w2', 'b2')}
    del _L1_ffn_all
    return {'x': x, 'src': src, 'dst': dst, 'edge_attr_128': edge_attr_128, 'edge_attr_3': edge_attr_3, 'L0_gnn_W': _L0_gnn_in['W'], 'L0_gnn_a_src': _L0_gnn_in['a_src'], 'L0_gnn_a_dst': _L0_gnn_in['a_dst'], 'L0_gnn_edge_W': _L0_gnn_in['edge_W'], 'L0_gnn_edge_b': _L0_gnn_in['edge_b'], 'L0_gnn_bias': _L0_gnn_in['bias'], 'L0_ffn_Wg': _L0_ffn_in['Wg'], 'L0_ffn_bg': _L0_ffn_in['bg'], 'L0_ffn_W1': _L0_ffn_in['W1'], 'L0_ffn_b1': _L0_ffn_in['b1'], 'L0_ffn_W2': _L0_ffn_in['W2'], 'L0_ffn_b2': _L0_ffn_in['b2'], 'L1_gnn_W': _L1_gnn_in['W'], 'L1_gnn_b': _L1_gnn_in['b'], 'L1_gnn_root': _L1_gnn_in['root'], 'L1_gnn_We': _L1_gnn_in['We'], 'L1_gnn_be': _L1_gnn_in['be'], 'L1_gnn_gamma': _L1_gnn_in['gamma'], 'L1_gnn_beta': _L1_gnn_in['beta'], 'L1_ffn_gate_w': _L1_ffn_in['gate_w'], 'L1_ffn_gate_b': _L1_ffn_in['gate_b'], 'L1_ffn_w1': _L1_ffn_in['w1'], 'L1_ffn_b1': _L1_ffn_in['b1'], 'L1_ffn_w2': _L1_ffn_in['w2'], 'L1_ffn_b2': _L1_ffn_in['b2']}

def reference(x, src, dst, edge_attr_128, edge_attr_3, L0_gnn_W, L0_gnn_a_src, L0_gnn_a_dst, L0_gnn_edge_W, L0_gnn_edge_b, L0_gnn_bias, L0_ffn_Wg, L0_ffn_bg, L0_ffn_W1, L0_ffn_b1, L0_ffn_W2, L0_ffn_b2, L1_gnn_W, L1_gnn_b, L1_gnn_root, L1_gnn_We, L1_gnn_be, L1_gnn_gamma, L1_gnn_beta, L1_ffn_gate_w, L1_ffn_gate_b, L1_ffn_w1, L1_ffn_b1, L1_ffn_w2, L1_ffn_b2):
    import jax
    import jax.numpy as jnp

    def _L0_gnn_ref(x, W, a_src, a_dst, edge_W, edge_b, bias, edge_attr, edge_index):
        import jax, jax.numpy as jnp
        import numpy as np
        N = 50000
        E = 12500
        IN = 256
        H = 8
        D = 32
        EF = 3
        n = x.shape[0]
        h = (x @ W.T).reshape(n, H, D)
        src, dst = (edge_index[0], edge_index[1])
        h_src = h[src]
        h_dst = h[dst]
        alpha = jnp.einsum('ehd,hd->eh', h_src, a_src) + jnp.einsum('ehd,hd->eh', h_dst, a_dst)
        enc = jax.nn.relu(edge_attr @ edge_W.T + edge_b).reshape(-1, H, D)
        alpha = alpha + jnp.sum(enc * h_dst, axis=-1)
        alpha = jnp.where(alpha >= 0, alpha, 0.2 * alpha)
        amax = jax.ops.segment_max(alpha, dst, num_segments=n)
        ex = jnp.exp(alpha - amax[dst])
        denom = jax.ops.segment_sum(ex, dst, num_segments=n)
        attn = ex / jnp.maximum(denom[dst], 1e-10)
        out = jax.ops.segment_sum(h_src * attn[..., None], dst, num_segments=n)
        return out.reshape(n, H * D) + bias

    def _L0_ffn_ref(x, Wg, bg, W1, b1, W2, b2):
        import jax, jax.numpy as jnp
        import numpy as np
        B, S, D, H, E, K = (8, 256, 256, 1024, 8, 2)
        gate_scores = jnp.einsum('bsd,ed->bse', x, Wg) + bg
        topk_scores, topk_idx = jax.lax.top_k(gate_scores, K)
        topk_probs = jax.nn.softmax(topk_scores, axis=-1)
        combine = jnp.sum(topk_probs[..., None] * jax.nn.one_hot(topk_idx, E, dtype=x.dtype), axis=-2)
        out = jnp.zeros_like(x)
        for e in range(E):
            h = jax.nn.relu(jnp.einsum('bsd,hd->bsh', x, W1[e]) + b1[e])
            y = jnp.einsum('bsh,dh->bsd', h, W2[e]) + b2[e]
            out = out + combine[..., e:e + 1] * y
        return out

    def _L1_gnn_ref(input_feature, edge_index, edge_attr, W, b, root, We, be, gamma, beta):
        import jax, jax.numpy as jnp
        import numpy as np
        N = 625
        E = 10000
        D = 256
        ED = 128
        L = 5
        BN_EPS = 1e-05
        row, col = (edge_index[0], edge_index[1])
        n = input_feature.shape[0]
        deg = jnp.zeros((n,), input_feature.dtype).at[row].add(1.0) + 1.0
        dinv = deg ** (-0.5)
        norm = (dinv[row] * dinv[col])[:, None]
        h = input_feature
        for l in range(L):
            xl = h @ W[l] + b[l]
            ee = edge_attr @ We[l] + be[l]
            msg = norm * jax.nn.relu(xl[row] + ee)
            agg = jnp.zeros_like(xl).at[col].add(msg)
            conv = agg + jax.nn.relu(xl + root[l]) / deg[:, None]
            mean = conv.mean(axis=0)
            var = conv.var(axis=0)
            hbn = (conv - mean) * jax.lax.rsqrt(var + BN_EPS) * gamma[l] + beta[l]
            if l < L - 1:
                hbn = jax.nn.relu(hbn)
            h = hbn + h
        return h

    def _L1_ffn_ref(h, gate_w, gate_b, w1, b1, w2, b2):
        import math
        import jax, jax.numpy as jnp
        import numpy as np
        CAPACITY_FACTOR = 1.25
        B, L, D = h.shape
        E = gate_w.shape[1]
        T = B * L
        C = max(1, math.ceil(CAPACITY_FACTOR * T / E))
        x = h.reshape(T, D)
        logits = x @ gate_w + gate_b
        probs = jax.nn.softmax(logits, axis=-1)
        idx = jnp.argmax(probs, axis=-1)
        prb = jnp.take_along_axis(probs, idx[:, None], axis=1)[:, 0]
        one_hot = jax.nn.one_hot(idx, E, dtype=jnp.float32)
        pos = (jnp.cumsum(one_hot, axis=0) * one_hot).sum(-1).astype(jnp.int32) - 1
        kept = pos < C
        pos_safe = jnp.where(kept, pos, C)
        buf = jnp.zeros((E, C, D), dtype=h.dtype).at[idx, pos_safe].set(x, mode='drop')
        hmid = jax.nn.relu(jnp.einsum('ecd,edf->ecf', buf, w1) + b1[:, None, :])
        ybuf = jnp.einsum('ecf,efd->ecd', hmid, w2) + b2[:, None, :]
        pos_g = jnp.minimum(pos, C - 1)
        y_tok = ybuf[idx, pos_g] * (prb * kept)[:, None]
        y = y_tok.reshape(B, L, D)
        y = jnp.nan_to_num(y, nan=0.0, posinf=10000.0, neginf=-10000.0)
        return y
    edge_index = jnp.stack([src, dst])
    x = x + _L0_gnn_ref(_layernorm(x, axis=-1), L0_gnn_W, L0_gnn_a_src, L0_gnn_a_dst, L0_gnn_edge_W, L0_gnn_edge_b, L0_gnn_bias, edge_attr_3, edge_index)
    x = x + _L0_ffn_ref(_layernorm(x, axis=-1)[None], L0_ffn_Wg, L0_ffn_bg, L0_ffn_W1, L0_ffn_b1, L0_ffn_W2, L0_ffn_b2)[0]
    x = x + _L1_gnn_ref(_layernorm(x, axis=-1), edge_index, edge_attr_128, L1_gnn_W, L1_gnn_b, L1_gnn_root, L1_gnn_We, L1_gnn_be, L1_gnn_gamma, L1_gnn_beta)
    x = x + _L1_ffn_ref(_layernorm(x, axis=-1)[None], L1_ffn_gate_w, L1_ffn_gate_b, L1_ffn_w1, L1_ffn_b1, L1_ffn_w2, L1_ffn_b2)[0]
    return x

_drawn_inputs = setup_inputs


def setup_inputs(seed=0):
    import zlib

    import numpy as np

    out = dict(_drawn_inputs(seed))
    spreads = {'L0_gnn_edge_b': (0.0, 0.1),
     'L0_gnn_bias': (0.0, 0.1),
     'L1_gnn_gamma': (1.0, 0.2),
     'L1_gnn_beta': (0.0, 0.1),
     'L1_ffn_gate_b': (0.0, 0.378),
     'L1_ffn_b1': (0.0, 0.8),
     'L1_ffn_b2': (0.0, 0.8)}
    factors = {'L0_ffn_b1': 6.798,
     'L0_ffn_b2': 5.444,
     'L1_gnn_b': 8.0,
     'L1_gnn_root': 29.098,
     'L1_gnn_be': 8.0}
    for name, (base, spread) in spreads.items():
        noise = np.random.default_rng([zlib.crc32(name.encode()), seed]).standard_normal(out[name].shape)
        drawn = base * np.exp(spread * noise) if base else spread * noise
        out[name] = jnp.asarray(drawn.astype(out[name].dtype))
    for name, factor in factors.items():
        out[name] = (out[name] * factor).astype(out[name].dtype)
    return out
```

```python
from contextlib import ExitStack

import numpy as np

import concourse.bass as bass
from concourse import mybir

F32 = mybir.dt.float32
BF16 = mybir.dt.bfloat16
I32 = mybir.dt.int32
U8 = mybir.dt.uint8
ALU = mybir.AluOpType
ACT = mybir.ActivationFunctionType
AX = mybir.AxisListType.X

P = 128
N = 3125
NT = -(-N // P)
NP = NT * P
E = 53125
BODY = 16
HALF = 8
ET = -(-E // (P * BODY)) * BODY
EP = ET * P
ITERS = ET // BODY
D = 256
K = D // P
HEADS = 8
HD = D // HEADS
HROW = HEADS * (HD + 1)
GROW = HROW + HEADS
ACC = NP + P
LAYERS = 5
XROW = D + 1
ED = 128
EX = 8
F = 1024
M = F // P
STEP = 5
NSTEP = NT // STEP
CAP = -(-5 * N // (4 * EX))
NEG = -1.0e30
EPS = 1e-5
FMAX = 3.4028234663852886e38


def makers(k, c, tag):
    return (lambda n: k.sem(f"{tag}_{n}"),
            lambda n, s, d=F32: c.enter_context(k.nc.sbuf_tensor(f"{tag}_{n}", s, d)),
            lambda n: c.enter_context(k.nc.psum_tensor(f"{tag}_{n}", [P, 512], F32)))


class Kernel:

    def __init__(self, nc, a, ctx):
        self.nc, self.a, self.ctx = nc, a, ctx
        self.sems, self.live = ctx.enter_context(ExitStack()), []
        sb = lambda n, s, d=F32: ctx.enter_context(nc.sbuf_tensor(n, s, d))
        dr = lambda n, s, d=F32: nc.dram_tensor(n, s, d, kind="Internal").ap()
        self.x = sb("x_res", [P, NT, D])
        self.ident = sb("ident", [P, P])
        self.iota_row = sb("iota_row", [P, P])
        self.base_row = sb("base_row", [1, ET], I32)
        self.dst_rel = sb("dst_rel", [P, ET])
        self.mean = sb("mean", [P, NT])
        self.rstd = sb("rstd", [P, NT])
        self.eps = sb("eps", [P, 1])
        self.agg = sb("agg", [P, K, ACC])
        self.h = sb("h", [P, K, NP])
        self.dinv_row = sb("dinv_row", [P, NP])
        self.floor = sb("floor", [P, LAYERS])
        self.logits = sb("logits", [P, NT, EX])
        self.weight = sb("weight", [P, 2, NT])
        self.write_row = sb("write_row", [P, 2, NT], I32)
        self.read_row = sb("read_row", [P, 2, NT], I32)
        self.group_expert = sb("group_expert", [1, 64], I32)
        self.h_table = dr("h_table", [ACC, GROW])
        self.h_src = dr("h_src", [EP, HROW])
        self.alpha_d = dr("alpha_d", [EP, HEADS])
        self.attn_d = dr("attn_d", [EP, HEADS])
        self.deg_d = dr("deg_d", [NT, P])
        self.xl_table = dr("xl_table", [NP, XROW])
        self.slots = {m.layer: m.groups * m.rows for m in FFN}
        self.x_buf = {l: dr(f"x_buf{l}", [self.slots[l], D]) for l in (0, 1)}
        self.y_buf = {l: dr(f"y_buf{l}", [self.slots[l], D]) for l in (0, 1)}


    def sem(self, name):
        s = self.sems.enter_context(self.nc.semaphore(name))
        self.live.append(s)
        return s

    def pool_sem(self, name):
        return self.ctx.enter_context(self.nc.semaphore(name))

    def recycle(self):
        live, self.live = self.live, []
        with self.nc.Block() as block:
            @block.gpsimd
            def _(pool):
                for s in live:
                    pool.sem_clear(s)
        self.sems.close()


def load_bases(k, engine, regs, tile):
    engine.load(regs, k.base_row[0:1, bass.ds(tile, len(regs))])
    return [engine.snap(r, min_val=0, max_val=N) for r in regs]


def tile_rows(dram, t0, n, c0=0, c1=None):
    v = dram[bass.ds(t0 * P, n * P), :] if c1 is None else dram[bass.ds(t0 * P, n * P), c0:c1]
    return v.rearrange("(b p) c -> p b c", p=P)


def constants(k):
    nc, a = k.nc, k.a
    with ExitStack() as c:
        sem, sb, bank = makers(k, c, "k")
        dst = sb("dst_cols", [P, ET], I32)
        basb = sb("base_bcast", [P, ET], I32)
        zeros = sb("zeros", [P, 4 * D])
        iota_i = sb("iota_i", [P, P], I32)
        loaded, made, ints, zeroed, cleared = sem("k_loaded"), sem("k_made"), sem("k_ints"), sem("k_zeroed"), sem("k_cleared")
        block = c.enter_context(nc.Block())

        @block.sync
        def _(sp):
            sp.dma_start(k.x[:], a["x"].rearrange("(t p) d -> p t d", p=P)).then_inc(loaded, 16)
            sp.dma_start(k.base_row[:], a["dst_first"]).then_inc(loaded, 16)
            sp.dma_start(dst[:], a["dst_cols"]).then_inc(loaded, 16)
            sp.dma_start(basb[:], a["dst_first"].broadcast_to([P, ET])).then_inc(loaded, 16)
            sp.wait_ge(zeroed, 1)
            n = 0
            for l in (0, 1):
                for s in range(0, k.slots[l], 4 * P):
                    sp.dma_start(k.x_buf[l][s:s + 4 * P, :].rearrange("(b p) d -> p b d", p=P),
                                 zeros[:].rearrange("p (b d) -> p b d", d=D)).then_inc(cleared, 16)
                    n += 1
            sp.dma_start(k.h_table[NP:ACC, :], zeros[:, 0:GROW]).then_inc(cleared, 16)
            sp.wait_ge(loaded, 64)
            sp.wait_ge(cleared, 16 * (n + 1))

        @block.gpsimd
        def _(pool):
            nc.gpsimd.iota(k.iota_row[:], [[1, P]], base=0, channel_multiplier=0,
                           allow_small_or_imprecise_dtypes=True).then_inc(made, 1)
            nc.gpsimd.memset(k.ident[:], 0.0).then_inc(ints, 1)
            pool.wait_ge(ints, 1)
            nc.gpsimd.affine_select(out=k.ident[:], in_=k.ident[:], compare_op=ALU.not_equal, fill=1.0, base=0,
                                    pattern=[[-1, P]], channel_multiplier=1).then_inc(made, 1)

        @block.vector
        def _(dve):
            nc.vector.memset(zeros[:], 0.0).then_inc(zeroed, 1)
            nc.vector.memset(k.eps[:], EPS).then_inc(made, 1)
            nc.vector.memset(k.floor[:, 0:LAYERS - 1], 0.0).then_inc(made, 1)
            nc.vector.memset(k.floor[:, LAYERS - 1:], -FMAX).then_inc(made, 1)
            dve.wait_ge(loaded, 64)
            nc.vector.tensor_tensor(k.dst_rel[:], dst[:], basb[:], ALU.subtract).then_inc(made, 1)


def layer_stats(k, tag):
    nc = k.nc
    with ExitStack() as c:
        sem, sb, bank = makers(k, c, tag)
        st = sb("st", [P, NT, 6])
        diff, var = sb("diff", [P, NT]), sb("var", [P, NT])
        stats, step, root = sem("stats"), sem("step"), sem("root")
        block = c.enter_context(nc.Block())

        @block.vector
        def _(dve):
            with dve.Fori(0, NSTEP) as it:
                for j in range(STEP):
                    nc.vector.bn_stats(st[:, bass.ds(it * STEP + j, 1), :].rearrange("p a s -> p (a s)"),
                                       k.x[:, bass.ds(it * STEP + j, 1), :].rearrange("p a s -> p (a s)")
                                       ).then_inc(stats, 1)
            dve.wait_ge(stats, NT)
            nc.vector.tensor_tensor(k.mean[:], st[:, :, 1], st[:, :, 4], ALU.add).then_inc(step, 1)
            nc.vector.tensor_tensor(diff[:], st[:, :, 1], st[:, :, 4], ALU.subtract).then_inc(step, 1)
            nc.vector.tensor_tensor(var[:], st[:, :, 2], st[:, :, 5], ALU.add).then_inc(step, 1)
            dve.wait_ge(step, 3)
            nc.vector.tensor_scalar(k.mean[:], k.mean[:], 0.5, None, ALU.mult).then_inc(step, 1)
            nc.vector.tensor_tensor(diff[:], diff[:], diff[:], ALU.mult).then_inc(step, 1)
            dve.wait_ge(step, 5)
            nc.vector.scalar_tensor_tensor(out=var[:], in0=diff[:], scalar=D / 4.0, in1=var[:],
                                           op0=ALU.mult, op1=ALU.add).then_inc(step, 1)
            dve.wait_ge(root, 1)
            nc.vector.reciprocal(k.rstd[:], k.rstd[:]).then_inc(step, 1)
            dve.wait_ge(step, 7)

        @block.scalar
        def _(act):
            act.wait_ge(step, 6)
            nc.scalar.activation(k.rstd[:], var[:], ACT.Sqrt, bias=k.eps[:, 0:1], scale=1.0 / D).then_inc(root, 1)


def normalise(k, out, t):
    return k.nc.vector.tensor_scalar(out, k.x[:, bass.ds(t, 1), :].rearrange("p a d -> p (a d)"),
                                     k.mean[:, bass.ds(t, 1)], k.rstd[:, bass.ds(t, 1)], ALU.subtract, ALU.mult)


def head_cols(ap):
    return ap.rearrange("p (h c) -> p h c", h=HEADS)[:, :, 0:HD]


def attention_tables(k):
    nc, a = k.nc, k.a
    BANKS = 2
    with ExitStack() as c:
        sem, sb, bank = makers(k, c, "tab")
        w = sb("gat_w", [P, K, D])
        asrc, adst = sb("asrc_b", [P, D]), sb("adst_b", [P, D])
        xn = sb("xn", [P, STEP, D])
        xt = sb("xt", [P, STEP, K * P])
        row = sb("h_rows", [P, STEP, GROW])
        prod = sb("prod", [P, 2, STEP, D])
        tp = [bank(f"tp{i}") for i in range(BANKS)]
        hp = [bank(f"hp{i}") for i in range(BANKS)]
        weights, xn_ready, turned, xt_ready, h_ready, h_copied, scored, stored, rows_free, mul = map(sem, (
            "weights", "xn_ready", "turned", "xt_ready", "h_ready", "h_copied", "scored", "stored", "rows_free", "mul"))
        block = c.enter_context(nc.Block())

        @block.sync
        def _(sp):
            sp.dma_start(w[:], a["gat_w"]).then_inc(weights, 16)
            sp.dma_start(asrc[:], a["gat_asrc"].broadcast_to([P, D])).then_inc(weights, 16)
            sp.dma_start(adst[:], a["gat_adst"].broadcast_to([P, D])).then_inc(weights, 16)
            sp.sem_inc(rows_free, 1)
            with sp.Fori(0, NSTEP) as it:
                rows = tile_rows(k.h_table, it * STEP, STEP)
                sp.wait_ge(scored, it * STEP + STEP)
                sp.dma_start(rows, row[:]).then_inc(stored, 16)
                sp.wait_ge(stored, it * 16 + 16)
                sp.sem_inc(rows_free, 1)

        @block.vector
        def _(dve):
            dve.wait_ge(weights, 48)
            with dve.Fori(0, NSTEP) as it:
                dve.wait_ge(turned, it * STEP + BANKS)
                for j in range(STEP):
                    normalise(k, xn[:, j, :], it * STEP + j).then_inc(xn_ready, 1)
                for j in range(STEP):
                    dve.wait_ge(h_copied, it * STEP + j + 1 + BANKS)
                    for n, vec in enumerate((asrc, adst)):
                        nc.vector.tensor_tensor(prod[:, n, j, :].rearrange("p (h c) -> p h c", h=HEADS),
                                                head_cols(row[:, j, 0:HROW]),
                                                vec[:].rearrange("p (h c) -> p h c", h=HEADS),
                                                ALU.mult).then_inc(mul, 1)
                for j in range(STEP):
                    dve.wait_ge(mul, it * 2 * STEP + 2 * j + 2)
                    nc.vector.tensor_reduce(row[:, j, HROW:GROW],
                                            prod[:, 0, j, :].rearrange("p (h c) -> p h c", h=HEADS), AX, ALU.add)
                    nc.vector.tensor_reduce(row[:, j, 0:HROW].rearrange("p (h c) -> p h c", h=HEADS)[:, :, HD],
                                            prod[:, 1, j, :].rearrange("p (h c) -> p h c", h=HEADS),
                                            AX, ALU.add).then_inc(scored, 1)

        @block.tensor
        def _(pe):
            pe.wait_ge(weights, 48)
            pe.sem_inc(turned, BANKS)
            with pe.Fori(0, NSTEP) as it:
                for j in range(STEP + 1):
                    if j < STEP:
                        pe.wait_ge(xn_ready, it * STEP + j + 1)
                        pe.wait_ge(xt_ready, it * STEP + j + 1)
                        for b in range(K):
                            last = nc.tensor.transpose(tp[j % BANKS][:, b * P:(b + 1) * P],
                                                       xn[:, j, b * P:(b + 1) * P], k.ident[:])
                        last.then_inc(turned, 1)
                    if j > 0:
                        i = j - 1
                        pe.wait_ge(xt_ready, it * STEP + i + 1 + BANKS)
                        pe.wait_ge(h_copied, it * STEP + i + 1)
                        for b in range(K):
                            last = nc.tensor.matmul(hp[i % BANKS][:, 0:D], xt[:, i, b * P:(b + 1) * P], w[:, b, :],
                                                    start=(b == 0), stop=(b == K - 1))
                        last.then_inc(h_ready, 1)

        @block.scalar
        def _(act):
            act.sem_inc(xt_ready, BANKS)
            act.sem_inc(h_copied, BANKS)
            with act.Fori(0, NSTEP) as it:
                for j in range(STEP + 1):
                    if j < STEP:
                        act.wait_ge(turned, it * STEP + j + 1 + BANKS)
                        nc.scalar.copy(xt[:, j, :], tp[j % BANKS][:, 0:D]).then_inc(xt_ready, 1)
                    if j > 0:
                        i = j - 1
                        if i == 0:
                            act.wait_ge(rows_free, it + 1)
                        act.wait_ge(h_ready, it * STEP + i + 1)
                        nc.scalar.copy(head_cols(row[:, i, 0:HROW]),
                                       hp[i % BANKS][:, 0:D].rearrange("p (h c) -> p h c", h=HEADS)
                                       ).then_inc(h_copied, 1)


def edge_scores(k):
    nc, a = k.nc, k.a
    BANKS = 4
    with ExitStack() as c:
        sem, sb, bank = makers(k, c, "sc")
        ew = sb("ew", [4, D])
        idx = sb("idx", [P, 2, HALF], I32)
        ea = sb("ea", [4, 2, HALF * P])
        dstb = sb("dstb", [P, 2, HALF * P], I32)
        win = sb("win", [P, BODY, HROW])
        g = sb("g", [P, BODY, GROW])
        onehot = sb("onehot", [P, BODY, P])
        enc = sb("enc", [P, BODY, HROW])
        prod = sb("prod", [P, BODY, HROW])
        dots, alpha = sb("dots", [P, BODY, HEADS]), sb("alpha", [P, BODY, HEADS])
        node_i = sb("node_i", [P, ET], I32)
        basb = sb("basb", [P, ET], I32)
        node = sb("node", [P, ET])
        pe_e = [bank(f"pe_e{i}") for i in range(BANKS)]
        pe_h = [bank(f"pe_h{i}") for i in range(BANKS)]
        idx_in, ea_in, dst_in = ([sem(f"{n}{q}") for q in range(2)] for n in ("idx_in", "ea_in", "dst_in"))
        win_in = [sem(f"win_in{j}") for j in range(BODY)]
        src_in = [k.pool_sem(f"sc_src_in{j}") for j in range(BODY)]
        hs_out, al_out = ([sem(f"{n}{q}") for q in range(2)] for n in ("hs_out", "al_out"))
        const, consts, begun, encoded, relu, hot, expanded, multiplied, summed, scored = map(sem, (
            "const", "consts", "begun", "encoded", "relu", "hot", "expanded", "multiplied", "summed", "scored"))
        block = c.enter_context(nc.Block())

        @block.sync
        def _(sp):
            base_regs = [sp.alloc_register(f"sc_base{i}") for i in range(HALF)]
            sp.dma_start(ew[:], a["gat_ew"]).then_inc(const, 16)
            sp.dma_start(basb[:], a["dst_first"].broadcast_to([P, ET])).then_inc(const, 16)

            def places(q, it):
                cols = bass.ds(it * (BODY * P) + q * HALF * P, HALF * P)
                return (a["src_halves"][bass.ds(it * 2 + q, 1)].rearrange("a p j -> (a p) j"), a["ea3"][:, cols],
                        a["dst_row"][:, cols].broadcast_to([P, HALF * P]))

            def load(q, it, of_idx, of_ea, of_dst):
                sp.dma_start(idx[:, q, :], of_idx).then_inc(idx_in[q], 16)
                sp.dma_start(ea[:, q, :], of_ea).then_inc(ea_in[q], 16)
                sp.dma_start(dstb[:, q, :], of_dst).then_inc(dst_in[q], 16)
                bases = load_bases(k, sp, base_regs, it * BODY + q * HALF)
                for j, base in zip(range(q * HALF, q * HALF + HALF), bases):
                    sp.dma_start(win[:, j, :], k.h_table[bass.ds(base, P), 0:HROW]).then_inc(win_in[j], 16)

            def store(q, halves, rows):
                sp.wait_ge(scored, halves)
                sp.dma_start(rows, alpha[:, q * HALF:(q + 1) * HALF, :]).then_inc(al_out[q], 16)

            for q in range(2):
                load(q, 0, *places(q, 0))
            with sp.Fori(0, ITERS - 1) as it:
                nxt = sp.snap(it + 1)
                at = [places(q, nxt) for q in range(2)]
                stored = [(sp.snap(it * 2 + q + 1), tile_rows(k.alpha_d, it * BODY + q * HALF, HALF)) for q in range(2)]
                for q in range(2):
                    sp.wait_ge(scored, stored[q][0])
                    load(q, nxt, *at[q])
                    store(q, *stored[q])
            for q in range(2):
                store(q, ET // HALF - 1 + q, tile_rows(k.alpha_d, ET - BODY + q * HALF, HALF))
            for q in range(2):
                sp.wait_ge(al_out[q], ITERS * 16)

        @block.gpsimd
        def _(pool):
            nc.gpsimd.iota(node_i[:], [[0, ET]], base=0, channel_multiplier=1).then_inc(consts, 1)

            def gather(q, it, first):
                pool.wait_ge(idx_in[q], 16 if first else it * 16 + 16)
                if not first:
                    pool.wait_ge(hs_out[q], it * 16)
                    pool.wait_ge(scored, it * 2 - 1 + q)
                pool.sem_inc(begun, 1)
                for j in range(q * HALF, q * HALF + HALF):
                    nc.gpsimd.indirect_dma_start(
                        out=g[:, j, :], out_offset=None, in_=k.h_table[:, :],
                        in_offset=bass.IndirectOffsetOnAxis(ap=idx[:, q, j % HALF:j % HALF + 1], axis=0)
                    ).then_inc(src_in[j], 16)

            for q in range(2):
                gather(q, 0, True)
            with pool.Fori(1, ITERS) as it:
                for q in range(2):
                    gather(q, it, False)

        @block.tensor
        def _(pe):
            pe.wait_ge(const, 32)
            with pe.Fori(0, ITERS) as it:
                for j in range(BODY):
                    n = it * BODY + j
                    q = j // HALF
                    if j % HALF == 0:
                        pe.wait_ge(ea_in[q], it * 16 + 16)
                    pe.wait_ge(relu, n + 1)
                    nc.tensor.matmul(pe_e[j % BANKS][:, 0:D], ea[:, q, (j % HALF) * P:(j % HALF + 1) * P], ew[:],
                                     start=True, stop=True).then_inc(encoded, 1)
                    pe.wait_ge(win_in[j], it * 16 + 16)
                    pe.wait_ge(hot, n + 1)
                    pe.wait_ge(multiplied, n + 1)
                    nc.tensor.matmul(pe_h[j % BANKS][:, 0:HROW], onehot[:, j, :], win[:, j, :],
                                     start=True, stop=True).then_inc(expanded, 1)

        @block.scalar
        def _(act):
            act.sem_inc(relu, BANKS)
            act.wait_ge(consts, 2)

            with act.Fori(0, ITERS) as it:
                for j in range(BODY):
                    n = it * BODY + j
                    act.wait_ge(encoded, n + 1)
                    act.wait_ge(multiplied, n + 1)
                    nc.scalar.activation(head_cols(enc[:, j, :]),
                                         pe_e[j % BANKS][:, 0:D].rearrange("p (h c) -> p h c", h=HEADS),
                                         ACT.Relu).then_inc(relu, 1)
                    if j % HALF == HALF - 1:
                        q = j // HALF
                        rows = tile_rows(k.h_src, it * BODY + q * HALF, HALF)
                        for i in range(q * HALF, q * HALF + HALF):
                            act.wait_ge(src_in[i], it * 16 + 16)
                        act.dma_start(rows, g[:, q * HALF:(q + 1) * HALF, 0:HROW]).then_inc(hs_out[q], 16)
            for q in range(2):
                act.wait_ge(hs_out[q], ITERS * 16)

        @block.vector
        def _(dve):
            nc.vector.memset(enc[:], 1.0).then_inc(consts, 1)
            dve.wait_ge(const, 32)
            dve.wait_ge(consts, 2)
            nc.vector.tensor_tensor(node[:], node_i[:], basb[:], ALU.add).then_inc(consts, 1)
            dve.wait_ge(consts, 3)
            dve.sem_inc(multiplied, BANKS)

            def hot_tile(it, j):
                q = j // HALF
                if j % HALF == 0:
                    dve.wait_ge(dst_in[q], it * 16 + 16)
                nc.vector.tensor_scalar(onehot[:, j, :], dstb[:, q, (j % HALF) * P:(j % HALF + 1) * P],
                                        node[:, bass.ds(it * BODY + j, 1)], None, ALU.is_equal).then_inc(hot, 1)

            def sum_tile(it, j):
                dve.wait_ge(multiplied, it * BODY + j + 1 + BANKS)
                nc.vector.tensor_reduce(dots[:, j, :], prod[:, j, :].rearrange("p (h c) -> p h c", h=HEADS),
                                        AX, ALU.add).then_inc(summed, 1)

            def score_half(it, q, first):
                if not first:
                    dve.wait_ge(al_out[q], it * 16)
                for j in range(q * HALF, q * HALF + HALF):
                    dve.wait_ge(src_in[j], it * 16 + 16)
                dve.wait_ge(summed, it * BODY + HALF * (q + 1))
                nc.vector.tensor_tensor(alpha[:, q * HALF:(q + 1) * HALF, :], dots[:, q * HALF:(q + 1) * HALF, :],
                                        g[:, q * HALF:(q + 1) * HALF, HROW:GROW], ALU.add).then_inc(scored, 1)

            def body(it, first):
                hot_tile(it, 0)
                for j in range(BODY):
                    n = it * BODY + j
                    if j + 1 < BODY:
                        hot_tile(it, j + 1)
                    dve.wait_ge(relu, n + 1 + BANKS)
                    dve.wait_ge(expanded, n + 1)
                    nc.vector.tensor_tensor(prod[:, j, :], enc[:, j, :], pe_h[j % BANKS][:, 0:HROW],
                                            ALU.mult).then_inc(multiplied, 1)
                    if j > 0:
                        sum_tile(it, j - 1)
                    if j == HALF + 1:
                        score_half(it, 0, first)
                sum_tile(it, BODY - 1)
                score_half(it, 1, first)

            body(0, True)
            with dve.Fori(1, ITERS) as it:
                body(it, False)


def softmax_over_edges(k):
    nc, a = k.nc, k.a
    H = HEADS
    with ExitStack() as c:
        sem, sb, bank = makers(k, c, "sm")
        s = sb("s", [P, ET, H])
        f = sb("f", [P, ET, H])
        r = sb("r", [P, ET, H])
        dst = sb("dst", [P, ET], I32)
        same = sb("same", [P, ET])
        after = sb("after", [P, ET])
        gap, gap_after = sb("gap", [P, ET]), sb("gap_after", [P, ET])
        first, last = sb("first", [P, ET]), sb("last", [P, ET])
        firstp, lastp = sb("firstp", [P, ET]), sb("lastp", [P, ET])
        dstf, ends = sb("dstf", [P, ET]), sb("ends", [P, 2])
        heads_i, tails_i = sb("heads_i", [H, P], I32), sb("tails_i", [H, P], I32)
        joins = sb("joins", [H, P])
        onrun = sb("onrun", [H, P])
        wf, wb = sb("wf", [H, P]), sb("wb", [H, P])
        joinp, wfp, wbp = sb("joinp", [H, P]), sb("wfp", [H, P]), sb("wbp", [H, P])
        edge = sb("edge", [P, 2, H])
        edge_t = sb("edge_t", [H, 2, P])
        carry_t = sb("carry_t", [H, 2, P])
        carry = sb("carry", [P, 2, H])
        tot = sb("tot", [P, H])
        ps = [bank(f"ps{i}") for i in range(2)]
        loaded, done, turned, exped, out = map(sem, ("loaded", "done", "turned", "exped", "out"))
        count = [0]
        block = c.enter_context(nc.Block())
        PE_STEPS = []

        def by_head(t):
            return t[:].rearrange("p t h -> p h t")

        def bcast(v):
            return v[:].unsqueeze(2).broadcast_to([P, ET, H])

        @block.vector
        def _(dve):
            def do(ins):
                count[0] += 1
                ins.then_inc(done, 1)
                dve.wait_ge(done, count[0])

            def free(ins):
                count[0] += 1
                ins.then_inc(done, 1)

            v = nc.vector
            dve.wait_ge(loaded, 64)
            do(v.tensor_copy(dstf[:], dst[:]))
            free(v.memset(same[:, 0:1], 1.0))
            free(v.memset(after[:, ET - 1:ET], 1.0))
            free(v.tensor_copy(ends[:, 0:1], dstf[:, 0:1]))
            free(v.tensor_copy(ends[:, 1:2], dstf[:, ET - 1:ET]))
            free(v.tensor_tensor(same[:, 1:ET], dstf[:, 1:ET], dstf[:, 0:ET - 1], ALU.is_equal))
            do(v.tensor_tensor(after[:, 0:ET - 1], dstf[:, 1:ET], dstf[:, 0:ET - 1], ALU.is_equal))
            free(v.tensor_scalar(first[:], dstf[:], ends[:, 0:1], None, ALU.is_equal))
            do(v.tensor_scalar(last[:], dstf[:], ends[:, 1:2], None, ALU.is_equal))
            free(v.tensor_tensor(onrun[:], heads_i[:], tails_i[:], ALU.is_equal))
            free(v.memset(joins[:, 0:1], 0.0))
            do(v.tensor_tensor(joins[:, 1:P], heads_i[:, 1:P], tails_i[:, 0:P - 1], ALU.is_equal))
            free(v.memset(wf[:], 0.0))
            do(v.tensor_tensor(wb[:], onrun[:], joins[:], ALU.mult))
            do(v.tensor_tensor(wf[:, 0:P - 1], onrun[:, 0:P - 1], joins[:, 1:P], ALU.mult))
            for mask, pen in ((same, gap), (after, gap_after), (first, firstp), (last, lastp),
                              (joins, joinp), (wf, wfp), (wb, wbp)):
                do(v.tensor_scalar(pen[:], mask[:], -NEG, NEG, ALU.mult, ALU.add))

            def over_rows(weight_f, weight_b, join, op0, op1, neutral):
                turn = PE_STEPS
                turn.append(count[0])
                dve.wait_ge(turned, len(turn))
                do(v.tensor_copy(edge_t[:].rearrange("h a p -> h (a p)"), ps[0][0:H, 0:2 * P]))
                do(v.tensor_tensor(edge_t[:, 0, 0:P - 1], edge_t[:, 0, 0:P - 1], join[:, 1:P], op0))
                do(v.tensor_tensor(edge_t[:, 1, :], edge_t[:, 1, :], join[:], op0))
                do(v.memset(carry_t[:], neutral))
                do(v.tensor_tensor_scan(carry_t[:, 0, 1:P], weight_f[:, 0:P - 1], edge_t[:, 0, 0:P - 1], neutral,
                                        op0, op1))
                do(v.tensor_tensor_scan(carry_t[:, 1, 0:P - 1][:, ::-1], weight_b[:, 1:P][:, ::-1],
                                        edge_t[:, 1, 1:P][:, ::-1], neutral, op0, op1))
                turn.append(count[0])
                dve.wait_ge(turned, len(turn))
                do(v.tensor_copy(carry[:].rearrange("p a h -> p (a h)"), ps[1][:, 0:2 * H]))

            do(v.scalar_tensor_tensor(out=s[:], in0=s[:], scalar=0.2, in1=s[:], op0=ALU.mult, op1=ALU.max))
            for n, pen in enumerate((lastp, firstp)):
                do(v.tensor_tensor(r[:], s[:], bcast(pen), ALU.add))
                do(v.tensor_reduce(edge[:, n, :], by_head(r), AX, ALU.max))
            over_rows(wfp, wbp, joinp, ALU.add, ALU.max, NEG)
            for h in range(H):
                free(v.tensor_tensor_scan(f[:, :, h], gap[:], s[:, :, h], carry[:, 0, h:h + 1], ALU.add, ALU.max))
            dve.wait_ge(done, count[0])
            for h in range(H):
                free(v.tensor_tensor_scan(r[:, :, h][:, ::-1], gap_after[:][:, ::-1], f[:, :, h][:, ::-1],
                                          carry[:, 1, h:h + 1], ALU.add, ALU.max))
            dve.wait_ge(done, count[0])
            do(v.tensor_tensor(s[:], s[:], r[:], ALU.subtract))
            k.sm_exp_at = count[0]
            dve.wait_ge(exped, 1)
            for n, mask in enumerate((last, first)):
                do(v.tensor_tensor(r[:], s[:], bcast(mask), ALU.mult))
                do(v.tensor_reduce(edge[:, n, :], by_head(r), AX, ALU.add))
            over_rows(wf, wb, joins, ALU.mult, ALU.add, 0.0)
            for h in range(H):
                free(v.tensor_tensor_scan(f[:, :, h], same[:], s[:, :, h], carry[:, 0, h:h + 1], ALU.mult, ALU.add))
            dve.wait_ge(done, count[0])
            do(v.tensor_tensor(tot[:], f[:, ET - 1, :], carry[:, 1, :], ALU.add))
            for h in range(H):
                free(v.tensor_tensor_scan(r[:, :, h][:, ::-1], after[:][:, ::-1], f[:, :, h][:, ::-1],
                                          tot[:, h:h + 1], ALU.mult, ALU.max))
            dve.wait_ge(done, count[0])
            do(v.tensor_scalar(r[:], r[:], 1e-10, None, ALU.max))
            do(v.reciprocal(r[:], r[:]))
            do(v.tensor_tensor(s[:], s[:], r[:], ALU.mult))

        @block.sync
        def _(sp):
            sp.dma_start(s[:], k.alpha_d.rearrange("(p t) h -> p t h", p=P)).then_inc(loaded, 16)
            sp.dma_start(dst[:], a["dst_chunk"]).then_inc(loaded, 16)
            sp.dma_start(heads_i[:], a["dst_chunk_first"].broadcast_to([H, P])).then_inc(loaded, 16)
            sp.dma_start(tails_i[:], a["dst_chunk_last"].broadcast_to([H, P])).then_inc(loaded, 16)
            sp.wait_ge(done, count[0])
            sp.dma_start(k.attn_d.rearrange("(p t) h -> p t h", p=P), s[:]).then_inc(out, 16)
            sp.wait_ge(out, 16)

        @block.tensor
        def _(pe):
            for n, at in enumerate(PE_STEPS):
                pe.wait_ge(done, at)
                for m in range(2):
                    if n % 2 == 0:
                        ins = nc.tensor.transpose(ps[0][0:H, m * P:(m + 1) * P], edge[:, m, :], k.ident[:])
                    else:
                        ins = nc.tensor.transpose(ps[1][:, m * H:(m + 1) * H], carry_t[:, m, :], k.ident[0:H, 0:H])
                ins.then_inc(turned, 1)

        @block.scalar
        def _(act):
            act.wait_ge(done, k.sm_exp_at)
            nc.scalar.activation(s[:], s[:], ACT.Exp).then_inc(exped, 1)


def attention_sums(k):
    nc, a = k.nc, k.a
    BANKS = 4
    with ExitStack() as c:
        sem, sb, bank = makers(k, c, "at")
        hs = sb("hs", [P, BODY, HROW])
        attn = sb("attn", [P, BODY, HEADS])
        msg = sb("msg", [P, BODY, D])
        onehot = sb("onehot", [P, BODY, P])
        ps = [bank(f"ps{i}") for i in range(BANKS)]
        hs_in, attn_in = ([sem(f"{n}{q}") for q in range(2)] for n in ("hs_in", "attn_in"))
        cleared, weighted, hot, summed, added = map(sem, ("cleared", "weighted", "hot", "summed", "added"))
        block = c.enter_context(nc.Block())

        @block.sync
        def _(sp):
            def places(q, it):
                t = it * BODY + q * HALF
                return tile_rows(k.h_src, t, HALF), tile_rows(k.attn_d, t, HALF)

            def load(q, of_hs, of_attn):
                sp.dma_start(hs[:, q * HALF:(q + 1) * HALF, :], of_hs).then_inc(hs_in[q], 16)
                sp.dma_start(attn[:, q * HALF:(q + 1) * HALF, :], of_attn).then_inc(attn_in[q], 16)

            for q in range(2):
                load(q, *places(q, 0))
            with sp.Fori(0, ITERS - 1) as it:
                at = [places(q, it + 1) for q in range(2)]
                used = [sp.snap(it * BODY + HALF * (q + 1)) for q in range(2)]
                for q in range(2):
                    sp.wait_ge(weighted, used[q])
                    load(q, *at[q])

        @block.gpsimd
        def _(pool):
            with pool.Fori(0, ITERS) as it:
                for j in range(BODY):
                    q = j // HALF
                    if j % HALF == 0:
                        pool.wait_ge(hs_in[q], it * 16 + 16)
                        pool.wait_ge(attn_in[q], it * 16 + 16)
                    pool.wait_ge(summed, it * BODY + j + 1)
                    nc.gpsimd.tensor_tensor(msg[:, j, :].rearrange("p (h c) -> p h c", h=HEADS),
                                            head_cols(hs[:, j, :]),
                                            attn[:, j, :].unsqueeze(2).broadcast_to([P, HEADS, HD]),
                                            ALU.mult).then_inc(weighted, 1)

        @block.tensor
        def _(pe):
            pe.sem_inc(summed, BODY)
            with pe.Fori(0, ITERS) as it:
                for j in range(BODY):
                    n = it * BODY + j
                    pe.wait_ge(weighted, n + 1)
                    pe.wait_ge(hot, n + 1)
                    pe.wait_ge(added, n + 1)
                    for b in range(K):
                        last = nc.tensor.matmul(ps[j % BANKS][:, b * P:(b + 1) * P], msg[:, j, b * P:(b + 1) * P],
                                                onehot[:, j, :], start=True, stop=True)
                    last.then_inc(summed, 1)

        @block.vector
        def _(dve):
            nc.vector.memset(k.agg[:], 0.0).then_inc(cleared, 1)
            dve.sem_inc(added, BANKS)
            dve.wait_ge(cleared, 1)
            base_regs = [dve.alloc_register(f"at_base{i}") for i in range(BODY)]
            with dve.Fori(0, ITERS) as it:
                hot_and_add(k, dve, it, base_regs, onehot, hot, summed, added, ps, BANKS)
            dve.wait_ge(added, ET + BANKS)


def hot_and_add(k, dve, it, base_regs, onehot, hot, summed, added, ps, BANKS):
    nc = k.nc

    def hot_tile(j):
        dve.wait_ge(summed, it * BODY + j + 1)
        nc.vector.tensor_scalar(onehot[:, j, :], k.iota_row[:], k.dst_rel[:, bass.ds(it * BODY + j, 1)], None,
                                ALU.is_equal).then_inc(hot, 1)

    def add_tile(j, base):
        n = it * BODY + j
        window = k.agg[:, :, bass.ds(base, P)]
        dve.wait_ge(summed, n + 1 + BODY)
        dve.wait_ge(added, n + BANKS)
        nc.vector.tensor_tensor(window, window, ps[j % BANKS][:, 0:K * P].rearrange("p (b n) -> p b n", b=K),
                                ALU.add).then_inc(added, 1)

    LEAD = 2
    for j in range(LEAD):
        hot_tile(j)
    bases = load_bases(k, dve, base_regs, it * BODY)
    for j in range(BODY):
        if j + LEAD < BODY:
            hot_tile(j + LEAD)
        add_tile(j, bases[j])


def add_features_first(k, tag, src, bias):
    nc, a = k.nc, k.a
    BANKS = 2
    with ExitStack() as c:
        sem, sb, bank = makers(k, c, tag)
        col = sb("bias", [P, K])
        part = sb("part", [P, STEP, K * P])
        ps = [bank(f"ps{i}") for i in range(BANKS)]
        loaded, copied, turned, added = map(sem, ("loaded", "copied", "turned", "added"))
        block = c.enter_context(nc.Block())

        @block.sync
        def _(sp):
            if bias:
                sp.dma_start(col[:], a[bias]).then_inc(loaded, 16)

        @block.scalar
        def _(act):
            if bias:
                act.wait_ge(loaded, 16)
            with act.Fori(0, NSTEP) as it:
                for j in range(STEP):
                    act.wait_ge(turned, it * STEP + j + 1)
                    for b in range(K):
                        of = src[:, b, bass.ds((it * STEP + j) * P, P)]
                        to = part[:, j, b * P:(b + 1) * P]
                        ins = (nc.scalar.activation(to, of, ACT.Identity, bias=col[:, b:b + 1]) if bias
                               else nc.scalar.copy(to, of))
                    ins.then_inc(copied, 1)

        @block.tensor
        def _(pe):
            pe.sem_inc(turned, STEP)
            with pe.Fori(0, NSTEP) as it:
                for j in range(STEP):
                    pe.wait_ge(copied, it * STEP + j + 1)
                    pe.wait_ge(added, it * STEP + j + 1)
                    for b in range(K):
                        last = nc.tensor.transpose(ps[(j) % BANKS][:, b * P:(b + 1) * P],
                                                   part[:, j, b * P:(b + 1) * P], k.ident[:])
                    last.then_inc(turned, 1)

        @block.vector
        def _(dve):
            dve.sem_inc(added, 1)
            with dve.Fori(0, NSTEP) as it:
                for j in range(STEP):
                    row = k.x[:, bass.ds(it * STEP + j, 1), :].rearrange("p a d -> p (a d)")
                    dve.wait_ge(turned, it * STEP + j + 1 + STEP)
                    nc.vector.tensor_tensor(row, row, ps[j % BANKS][:, 0:D], ALU.add).then_inc(added, 1)
            dve.wait_ge(added, NT + 1)


class Experts:

    def __init__(self, layer, top, blocks, gate_w, gate_b, w1, b1, w2, b2):
        self.layer, self.top, self.blocks = layer, top, blocks
        self.rows = blocks * P
        self.groups = (N * top + EX * (self.rows - 1)) // self.rows if top > 1 else EX
        self.gate_w, self.gate_b, self.w1, self.b1, self.w2, self.b2 = gate_w, gate_b, w1, b1, w2, b2


FFN = (Experts(0, 2, 2, "f0_gate_w", "f0_gate_b", "f0_w1", "f0_b1", "f0_w2", "f0_b2"),
       Experts(1, 1, 4, "f1_gate_w", "f1_gate_b", "f1_w1", "f1_b1", "f1_w2", "f1_b2"))


def gate_logits(k, ffn):
    nc, a = k.nc, k.a
    BANKS = 2
    with ExitStack() as c:
        sem, sb, bank = makers(k, c, f"gl{ffn.layer}")
        w, bias = sb("w", [P, K, EX]), sb("b", [P, EX])
        xn, xt = sb("xn", [P, STEP, D]), sb("xt", [P, STEP, K * P])
        tp = [bank(f"tp{i}") for i in range(BANKS)]
        lp = [bank(f"lp{i}") for i in range(BANKS)]
        weights, xn_ready, turned, xt_ready, product, biased = map(sem, (
            "weights", "xn_ready", "turned", "xt_ready", "product", "biased"))
        block = c.enter_context(nc.Block())

        @block.sync
        def _(sp):
            sp.dma_start(w[:], a[ffn.gate_w]).then_inc(weights, 16)
            sp.dma_start(bias[:], a[ffn.gate_b].broadcast_to([P, EX])).then_inc(weights, 16)

        @block.vector
        def _(dve):
            dve.wait_ge(weights, 32)
            dve.sem_inc(biased, BANKS)
            with dve.Fori(0, NSTEP) as it:
                for j in range(STEP + 1):
                    if j < STEP:
                        dve.wait_ge(turned, it * STEP + j + 1)
                        normalise(k, xn[:, j, :], it * STEP + j).then_inc(xn_ready, 1)
                    if j > 0:
                        i = j - 1
                        dve.wait_ge(product, it * STEP + i + 1)
                        nc.vector.tensor_tensor(k.logits[:, bass.ds(it * STEP + i, 1), :].rearrange("p a e -> p (a e)"),
                                                lp[i % BANKS][:, 0:EX], bias[:], ALU.add).then_inc(biased, 1)
            dve.wait_ge(biased, NT + BANKS)

        @block.tensor
        def _(pe):
            pe.wait_ge(weights, 32)
            pe.sem_inc(turned, STEP)
            with pe.Fori(0, NSTEP) as it:
                for j in range(STEP + 1):
                    if j < STEP:
                        pe.wait_ge(xn_ready, it * STEP + j + 1)
                        pe.wait_ge(xt_ready, it * STEP + j + 1)
                        for b in range(K):
                            last = nc.tensor.transpose(tp[j % BANKS][:, b * P:(b + 1) * P],
                                                       xn[:, j, b * P:(b + 1) * P], k.ident[:])
                        last.then_inc(turned, 1)
                    if j > 0:
                        i = j - 1
                        pe.wait_ge(xt_ready, it * STEP + i + 1 + BANKS)
                        pe.wait_ge(biased, it * STEP + i + 1)
                        for b in range(K):
                            last = nc.tensor.matmul(lp[i % BANKS][:, 0:EX], xt[:, i, b * P:(b + 1) * P], w[:, b, :],
                                                    start=(b == 0), stop=(b == K - 1))
                        last.then_inc(product, 1)

        @block.scalar
        def _(act):
            act.sem_inc(xt_ready, BANKS)
            with act.Fori(0, NSTEP) as it:
                for j in range(STEP):
                    act.wait_ge(turned, it * STEP + j + 1 + STEP)
                    nc.scalar.copy(xt[:, j, :], tp[j % BANKS][:, 0:D]).then_inc(xt_ready, 1)


def route(k, ffn):
    nc, a = k.nc, k.a
    L, top = ffn.layer, ffn.top
    SH = [P, NT, EX]
    OUT = float(1 << 16)
    with ExitStack() as c:
        sem, sb, bank = makers(k, c, f"rt{L}")
        lg, eq, tmp = sb("lg", SH), sb("eq", SH), sb("tmp", SH)
        hot = [sb(f"hot{n}", SH) for n in range(top)]
        both, place, total, incl, excl = (sb(n, SH) for n in ("both", "place", "total", "incl", "excl"))
        rank = sb("rank", [P, EX])
        top_v = [sb(f"top{n}", [P, NT]) for n in range(top)]
        pick, node, out, slot = (sb(n, [P, NT]) for n in ("pick", "node", "out", "slot"))
        kept = sb("kept", [P, NT])
        upto, ones = sb("upto", [P, P]), sb("ones", [P, P])
        start, end = sb("start", [P, EX]), sb("end", [P, EX])
        count_i = sb("count_i", [P, EX], I32)
        groups = sb("groups", [1, ffn.groups, EX])
        group_f, group_n = sb("group_f", [1, ffn.groups]), sb("group_n", [1, ffn.groups])
        ps = [bank(f"ps{i}") for i in range(2)]
        made, done, counted, exped = map(sem, ("made", "done", "counted", "exped"))
        steps = [0]
        at = {}
        block = c.enter_context(nc.Block())
        flat = lambda t: t[:].rearrange("p t e -> p (t e)")
        over_e = lambda t: t[:].unsqueeze(2).broadcast_to(SH)
        over_t = lambda t: t[:].unsqueeze(1).broadcast_to(SH)

        @block.gpsimd
        def _(pool):
            g = nc.gpsimd
            g.iota(rank[:], [[-1, EX]], base=EX, channel_multiplier=0, allow_small_or_imprecise_dtypes=True
                   ).then_inc(made, 1)
            g.iota(node[:], [[P, NT]], base=0, channel_multiplier=1, allow_small_or_imprecise_dtypes=True
                   ).then_inc(made, 1)
            g.iota(group_n[:], [[1, ffn.groups]], base=0, channel_multiplier=0, allow_small_or_imprecise_dtypes=True
                   ).then_inc(made, 1)
            g.memset(ones[:], 1.0).then_inc(made, 1)
            pool.wait_ge(made, 4)
            g.affine_select(out=upto[:], in_=ones[:], compare_op=ALU.is_ge, fill=0.0, base=0, pattern=[[1, P]],
                            channel_multiplier=-1).then_inc(made, 1)

        @block.vector
        def _(dve):
            v = nc.vector

            def do(ins):
                steps[0] += 1
                ins.then_inc(done, 1)
                dve.wait_ge(done, steps[0])

            dve.wait_ge(made, 5)
            do(v.tensor_copy(flat(lg), k.logits[:].rearrange("p t e -> p (t e)")))
            for n in range(top):
                do(v.tensor_reduce(top_v[n][:], lg[:], AX, ALU.max))
                do(v.tensor_tensor(eq[:], lg[:], over_e(top_v[n]), ALU.is_equal))
                do(v.tensor_tensor(eq[:], eq[:], over_t(rank), ALU.mult))
                do(v.tensor_reduce(pick[:], eq[:], AX, ALU.max))
                do(v.tensor_tensor(hot[n][:], over_e(pick), over_t(rank), ALU.is_equal))
                if n + 1 < top:
                    do(v.scalar_tensor_tensor(out=flat(lg), in0=flat(hot[n]), scalar=NEG, in1=flat(lg),
                                              op0=ALU.mult, op1=ALU.add))
            do(v.tensor_scalar(out[:], node[:], float(N), None, ALU.is_ge))
            do(v.tensor_scalar(kept[:], out[:], -1.0, 1.0, ALU.mult, ALU.add))
            for n in range(top):
                do(v.tensor_tensor(hot[n][:], hot[n][:], over_e(kept), ALU.mult))
            if top == 2:
                do(v.tensor_tensor(both[:], hot[0][:], hot[1][:], ALU.add))
                do(v.tensor_tensor(pick[:], top_v[1][:], top_v[0][:], ALU.subtract))
                at["exp"] = steps[0]
                dve.wait_ge(exped, 1)
                do(v.tensor_scalar(k.weight[:, 0, :], pick[:], 1.0, None, ALU.add))
                do(v.reciprocal(k.weight[:, 0, :], k.weight[:, 0, :]))
                do(v.tensor_tensor(k.weight[:, 1, :], k.weight[:, 0, :], pick[:], ALU.mult))
            else:
                do(v.tensor_copy(flat(both), flat(hot[0])))
                do(v.tensor_tensor(lg[:], lg[:], over_e(top_v[0]), ALU.subtract))
                at["exp"] = steps[0]
                dve.wait_ge(exped, 1)
                do(v.tensor_reduce(k.weight[:, 0, :], lg[:], AX, ALU.add))
                do(v.reciprocal(k.weight[:, 0, :], k.weight[:, 0, :]))
            at["hot"] = steps[0]
            dve.wait_ge(counted, 1)
            do(v.tensor_copy(flat(total), ps[1][:, 0:NT * EX]))
            for e in range(EX):
                do(v.tensor_tensor_scan(incl[:, :, e], ones[:, 0:NT], total[:, :, e], 0.0, ALU.mult, ALU.add))
            do(v.tensor_tensor(excl[:], incl[:], total[:], ALU.subtract))
            do(v.tensor_tensor(flat(place), flat(excl), ps[0][:, 0:NT * EX], ALU.add))
            if top == 2:
                do(v.tensor_copy(count_i[:], incl[:, NT - 1, :]))
                do(v.tensor_scalar(count_i[:], count_i[:], float(ffn.rows - 1), None, ALU.add))
                do(v.tensor_scalar(count_i[:], count_i[:], ffn.rows.bit_length() - 1, None, ALU.arith_shift_right))
                do(v.tensor_copy(start[:], count_i[:]))
                do(v.tensor_tensor_scan(end[:], ones[:, 0:EX], start[:], 0.0, ALU.mult, ALU.add))
                do(v.tensor_tensor(start[:], end[:], start[:], ALU.subtract))
            else:
                do(v.tensor_scalar(start[:], rank[:], -1.0, float(EX), ALU.mult, ALU.add))
                do(v.tensor_scalar(end[:], start[:], 1.0, None, ALU.add))
            do(v.tensor_tensor(groups[:], group_n[:].unsqueeze(2).broadcast_to([1, ffn.groups, EX]),
                               end[0:1, :].unsqueeze(1).broadcast_to([1, ffn.groups, EX]), ALU.is_ge))
            do(v.tensor_reduce(group_f[:], groups[:], AX, ALU.add))
            do(v.tensor_scalar(group_f[:], group_f[:], float(EX - 1), None, ALU.min))
            do(v.tensor_copy(k.group_expert[:, 0:ffn.groups], group_f[:]))
            do(v.tensor_scalar(start[:], start[:], float(ffn.rows), -1.0, ALU.mult, ALU.add))
            for n in range(top):
                if top == 1:
                    do(v.tensor_tensor(tmp[:], place[:], hot[n][:], ALU.mult))
                    do(v.tensor_reduce(pick[:], tmp[:], AX, ALU.add))
                    do(v.tensor_scalar(kept[:], pick[:], float(CAP), None, ALU.is_le))
                    do(v.tensor_tensor(k.weight[:, 0, :], k.weight[:, 0, :], kept[:], ALU.mult))
                    do(v.tensor_scalar(pick[:], pick[:], float(CAP), None, ALU.is_gt))
                    do(v.tensor_tensor(out[:], out[:], pick[:], ALU.max))
                do(v.tensor_tensor(tmp[:], place[:], over_t(start), ALU.add))
                do(v.tensor_tensor(tmp[:], tmp[:], hot[n][:], ALU.mult))
                do(v.tensor_reduce(slot[:], tmp[:], AX, ALU.add))
                do(v.scalar_tensor_tensor(out=slot[:], in0=out[:], scalar=OUT, in1=slot[:], op0=ALU.mult, op1=ALU.add))
                do(v.tensor_copy(k.write_row[:, n, :], slot[:]))
                do(v.tensor_scalar(slot[:], slot[:], float(k.slots[L] - 1), None, ALU.min))
                do(v.tensor_copy(k.read_row[:, n, :], slot[:]))

        @block.scalar
        def _(act):
            act.wait_ge(done, at["exp"])
            t = pick[:] if top == 2 else flat(lg)
            nc.scalar.activation(t, t, ACT.Exp).then_inc(exped, 1)

        @block.tensor
        def _(pe):
            pe.wait_ge(made, 5)
            pe.wait_ge(done, at["hot"])
            nc.tensor.matmul(ps[0][:, 0:NT * EX], upto[:], flat(both), start=True, stop=True)
            nc.tensor.matmul(ps[1][:, 0:NT * EX], ones[:], flat(both), start=True, stop=True).then_inc(counted, 1)


def dispatch(k, ffn):
    nc = k.nc
    L, top = ffn.layer, ffn.top
    with ExitStack() as c:
        sem, sb, bank = makers(k, c, f"dp{L}")
        xn = sb("xn", [P, STEP, D])
        idx = sb("idx", [P, STEP, top], I32)
        ready, begun = sem("ready"), sem("begun")
        sent = [k.pool_sem(f"dp{L}_sent{j}") for j in range(STEP)]
        block = c.enter_context(nc.Block())

        @block.vector
        def _(dve):
            def step(it, first):
                for j in range(STEP):
                    if not first:
                        dve.wait_ge(sent[j], it * (16 * top))
                    normalise(k, xn[:, j, :], it * STEP + j).then_inc(ready, 1)
                    nc.vector.tensor_copy(idx[:, j, :], k.write_row[:, :, bass.ds(it * STEP + j, 1)]
                                          .rearrange("p n a -> p (n a)")[:, 0:top]).then_inc(ready, 1)

            step(0, True)
            with dve.Fori(1, NSTEP) as it:
                step(it, False)

        @block.gpsimd
        def _(pool):
            with pool.Fori(0, NSTEP) as it:
                for j in range(STEP):
                    pool.wait_ge(ready, it * (2 * STEP) + 2 * j + 2)
                    pool.sem_inc(begun, 1)
                    for n in range(top):
                        nc.gpsimd.indirect_dma_start(
                            out=k.x_buf[L][:, :], out_offset=bass.IndirectOffsetOnAxis(ap=idx[:, j, n:n + 1], axis=0),
                            in_=xn[:, j, :], in_offset=None, bounds_check=k.slots[L] - 1, oob_is_err=False
                        ).then_inc(sent[j], 16)
            for j in range(STEP):
                pool.wait_ge(sent[j], NSTEP * 16 * top)


def experts(k, ffn):
    nc, a = k.nc, k.a
    L, B, R = ffn.layer, ffn.blocks, ffn.rows
    HB = 3
    with ExitStack() as c:
        sem, sb, bank = makers(k, c, f"ex{L}")
        w1, w2 = sb("w1", [P, 2, K * F]), sb("w2", [P, 2, M * D])
        b1, b2 = sb("b1", [P, 2, M]), sb("b2", [1, 2, D])
        xb = sb("xb", [P, 2, B, D])
        xt = sb("xt", [P, K, R])
        hid = sb("hid", [P, M, R])
        y = sb("y", [P, 2, B, D])
        ones = sb("ones", [1, P])
        tp = [bank(f"tp{i}") for i in range(K)]
        hp = [bank(f"hp{i}") for i in range(HB)]
        yp = [bank(f"yp{i}") for i in range(2)]
        w_in, x_in = ([sem(f"{n}{s}") for s in range(2)] for n in ("w_in", "x_in"))
        made, turned, xt_ready, product, relu, summed, copied, y_free = map(sem, (
            "made", "turned", "xt_ready", "product", "relu", "summed", "copied", "y_free"))
        y_out = [k.pool_sem(f"ex{L}_y_out{s}") for s in range(2)]
        block = c.enter_context(nc.Block())
        PAIRS = ffn.groups // 2

        @block.sync
        def _(sp):
            def places(g):
                e = sp.value_load(k.group_expert[0:1, bass.ds(g, 1)], min_val=0, max_val=EX - 1)
                return (a[ffn.w1][bass.ds(e * P, P), :], a[ffn.w2][bass.ds(e * P, P), :],
                        a[ffn.b1][bass.ds(e * P, P), :], a[ffn.b2][bass.ds(e, 1), :], tile_rows(k.x_buf[L], g * B, B))

            def load(s, of_w1, of_w2, of_b1, of_b2, of_x):
                sp.dma_start(xb[:, s, :, :], of_x).then_inc(x_in[s], 16)
                sp.dma_start(w1[:, s, :], of_w1).then_inc(w_in[s], 16)
                sp.dma_start(b1[:, s, :], of_b1).then_inc(w_in[s], 16)
                sp.dma_start(w2[:, s, :], of_w2).then_inc(w_in[s], 16)
                sp.dma_start(b2[:, s, :], of_b2).then_inc(w_in[s], 16)

            for s in range(2):
                load(s, *places(s))
            with sp.Fori(0, PAIRS - 1) as it:
                at = [places(it * 2 + 2 + s) for s in range(2)]
                used = [sp.snap(it * (2 * B) + B * (s + 1)) for s in range(2)]
                for s in range(2):
                    sp.wait_ge(summed, used[s])
                    load(s, *at[s])

        @block.tensor
        def _(pe):
            pe.wait_ge(made, 1)
            with pe.Fori(0, PAIRS) as it:
                for s in range(2):
                    g = it * 2 + s
                    pe.wait_ge(x_in[s], it * 16 + 16)
                    pe.wait_ge(xt_ready, g * K + K)
                    for kk in range(K):
                        for b in range(B):
                            last = nc.tensor.transpose(tp[kk][:, b * P:(b + 1) * P], xb[:, s, b, kk * P:(kk + 1) * P],
                                                       k.ident[:])
                        last.then_inc(turned, 1)
                    pe.wait_ge(w_in[s], it * 64 + 64)
                    pe.wait_ge(xt_ready, g * K + 2 * K)
                    for m in range(M):
                        pe.wait_ge(relu, g * M + m + 1)
                        for kk in range(K):
                            last = nc.tensor.matmul(hp[m % HB][:, 0:R],
                                                    w1[:, s, kk * F + m * P:kk * F + (m + 1) * P], xt[:, kk, :],
                                                    start=(kk == 0), stop=(kk == K - 1))
                        last.then_inc(product, 1)
                    pe.wait_ge(relu, g * M + M + HB)
                    for b in range(B):
                        pe.wait_ge(copied, g * B + b + 1)
                        for m in range(M):
                            nc.tensor.matmul(yp[b % 2][:, 0:D], hid[:, m, b * P:(b + 1) * P],
                                             w2[:, s, m * D:(m + 1) * D], start=(m == 0), stop=False)
                        nc.tensor.matmul(yp[b % 2][:, 0:D], ones[:], b2[:, s, :], start=False, stop=True
                                         ).then_inc(summed, 1)

        @block.scalar
        def _(act):
            act.sem_inc(xt_ready, K)
            act.sem_inc(relu, HB)
            with act.Fori(0, PAIRS) as it:
                for s in range(2):
                    g = it * 2 + s
                    for kk in range(K):
                        act.wait_ge(turned, g * K + kk + 1)
                        nc.scalar.copy(xt[:, kk, :], tp[kk][:, 0:R]).then_inc(xt_ready, 1)
                    act.wait_ge(w_in[s], it * 64 + 64)
                    for m in range(M):
                        act.wait_ge(product, g * M + m + 1)
                        nc.scalar.activation(hid[:, m, :], hp[m % HB][:, 0:R], ACT.Relu, bias=b1[:, s, m:m + 1]
                                             ).then_inc(relu, 1)

        @block.vector
        def _(dve):
            nc.vector.memset(ones[:], 1.0).then_inc(made, 1)
            dve.sem_inc(copied, 2)

            def pair(it, first):
                for s in range(2):
                    if not first:
                        dve.wait_ge(y_out[s], it * 16)
                    for b in range(B):
                        dve.wait_ge(summed, it * (2 * B) + s * B + b + 1)
                        nc.vector.tensor_copy(y[:, s, b, :], yp[b % 2][:, 0:D]).then_inc(copied, 1)

            pair(0, True)
            with dve.Fori(1, PAIRS) as it:
                pair(it, False)

        @block.gpsimd
        def _(pool):
            with pool.Fori(0, PAIRS) as it:
                for s in range(2):
                    g = it * 2 + s
                    rows = tile_rows(k.y_buf[L], g * B, B)
                    pool.wait_ge(copied, g * B + B + 2)
                    pool.sem_inc(y_free, 1)
                    pool.dma_start(rows, y[:, s, :, :]).then_inc(y_out[s], 16)
            for s in range(2):
                pool.wait_ge(y_out[s], PAIRS * 16)


def combine(k, ffn):
    nc = k.nc
    L, top = ffn.layer, ffn.top
    with ExitStack() as c:
        sem, sb, bank = makers(k, c, f"cb{L}")
        idx = sb("idx", [P, STEP, top], I32)
        g = sb("g", [P, STEP, top, D])
        part = sb("part", [P, STEP, D])
        mask = [sb(f"mask{i}", [P, STEP, D], I32) for i in range(3)]
        sub = [sb(f"sub{i}", [P, STEP, D]) for i in range(3)]
        ready, begun, masked, added, scaled, fixed, begun_fix, made = map(sem, (
            "ready", "begun", "masked", "added", "scaled", "fixed", "begun_fix", "made"))
        got = [k.pool_sem(f"cb{L}_got{j}") for j in range(STEP)]
        block = c.enter_context(nc.Block())
        row = lambda t: k.x[:, bass.ds(t, 1), :].rearrange("p a d -> p (a d)")

        @block.gpsimd
        def _(pool):
            with pool.Fori(0, NSTEP) as it:
                for j in range(STEP):
                    pool.wait_ge(ready, it * STEP + j + 1)
                    pool.sem_inc(begun, 1)
                    for n in range(top):
                        nc.gpsimd.indirect_dma_start(
                            out=g[:, j, n, :], out_offset=None, in_=k.y_buf[L][:, :],
                            in_offset=bass.IndirectOffsetOnAxis(ap=idx[:, j, n:n + 1], axis=0)).then_inc(got[j], 16)

        @block.vector
        def _(dve):
            v = nc.vector
            for t, value in zip(sub, (0.0, 1e4, -1e4)):
                v.memset(t[:], value).then_inc(made, 1)
            dve.wait_ge(made, 3)

            def ask(it, j):
                v.tensor_copy(idx[:, j, :], k.read_row[:, :, bass.ds(it * STEP + j, 1)]
                              .rearrange("p n a -> p (n a)")[:, 0:top]).then_inc(ready, 1)

            for j in range(STEP):
                ask(0, j)

            def add_two(it):
                for j in range(STEP):
                    t = it * STEP + j
                    dve.wait_ge(got[j], it * 32 + 32)
                    for n in range(2):
                        if n:
                            dve.wait_ge(added, t * 2 + 1)
                        v.scalar_tensor_tensor(out=row(t), in0=g[:, j, n, :], scalar=k.weight[:, n, bass.ds(t, 1)],
                                               in1=row(t), op0=ALU.mult, op1=ALU.add).then_inc(added, 1)

            def add_one(it):
                for j in range(STEP):
                    dve.wait_ge(got[j], it * 16 + 16)
                    v.tensor_scalar(part[:, j, :], g[:, j, 0, :], k.weight[:, 0, bass.ds(it * STEP + j, 1)], None,
                                    ALU.mult).then_inc(scaled, 1)
                dve.wait_ge(scaled, it * STEP + STEP)
                v.tensor_tensor(mask[0][:], part[:], part[:], ALU.not_equal).then_inc(masked, 1)
                v.tensor_scalar(mask[1][:], part[:], FMAX, None, ALU.is_gt).then_inc(masked, 1)
                v.tensor_scalar(mask[2][:], part[:], -FMAX, None, ALU.is_lt).then_inc(masked, 1)
                for i in range(3):
                    dve.wait_ge(masked, it * 3 + 3)
                    if i:
                        dve.wait_ge(fixed, it * 3 + i)
                    dve.sem_inc(begun_fix, 1)
                    v.copy_predicated(part[:], mask[i][:], sub[i][:]).then_inc(fixed, 1)
                dve.wait_ge(fixed, it * 3 + 3)
                rows = k.x[:, bass.ds(it * STEP, STEP), :]
                v.tensor_tensor(rows, rows, part[:], ALU.add).then_inc(added, 1)

            add = add_two if top == 2 else add_one
            with dve.Fori(0, NSTEP - 1) as it:
                add(it)
                for j in range(STEP):
                    ask(it + 1, j)
            add(NSTEP - 1)
            dve.wait_ge(added, NT * 2 if top == 2 else NSTEP)


def mixture(k, ffn):
    layer_stats(k, f"ffn{ffn.layer}")
    gate_logits(k, ffn)
    route(k, ffn)
    dispatch(k, ffn)
    experts(k, ffn)
    combine(k, ffn)


def degrees(k):
    nc, a = k.nc, k.a
    with ExitStack() as c:
        sem, sb, bank = makers(k, c, "dg")
        src, hi, lo = (sb(n, [P, ET], I32) for n in ("src", "hi", "lo"))
        tile_hot = sb("tile_hot", [P, 2, BODY, NT], BF16)
        place_hot = sb("place_hot", [P, 2, BODY, P], BF16)
        deg = sb("deg", [NT, P])
        cols = sb("cols", [P, NT])
        ps = [bank(f"ps{i}") for i in range(3)]
        loaded, split, hot, counted, added, root, done, turned, stored = map(sem, (
            "loaded", "split", "hot", "counted", "added", "root", "done", "turned", "stored"))
        block = c.enter_context(nc.Block())

        @block.sync
        def _(sp):
            sp.dma_start(src[:], a["src_cols"]).then_inc(loaded, 16)
            sp.wait_ge(done, 1)
            sp.dma_start(k.deg_d, deg[:]).then_inc(stored, 16)
            sp.wait_ge(stored, 16)
            sp.dma_start(k.dinv_row[:], k.deg_d.rearrange("t p -> (t p)").unsqueeze(0).broadcast_to([P, NP])
                         ).then_inc(stored, 16)
            sp.wait_ge(turned, 2)
            with nc.allow_non_contiguous_dma(reason="one number for each row of the table"):
                sp.dma_start(k.xl_table[:, D:XROW].rearrange("(t p) c -> p t c", p=P), cols[:].unsqueeze(2)
                             ).then_inc(stored, 16)
            sp.wait_ge(stored, 48)

        @block.vector
        def _(dve):
            v = nc.vector
            dve.wait_ge(loaded, 16)
            v.tensor_scalar(hi[:], src[:], 7, None, ALU.arith_shift_right).then_inc(split, 1)
            v.tensor_scalar(lo[:], src[:], P - 1, None, ALU.bitwise_and).then_inc(split, 1)
            v.memset(deg[:], 1.0).then_inc(split, 1)
            dve.wait_ge(split, 3)
            dve.sem_inc(added, 2)
            with dve.Fori(0, ITERS // 2) as it:
                for s in range(2):
                    n = it * 2 + s
                    cols16 = bass.ds(n * BODY, BODY)
                    for src_of, of, width in ((hi, tile_hot, NT), (lo, place_hot, P)):
                        shape = [P, BODY, width]
                        v.tensor_tensor(of[:, s, :, :], k.iota_row[:, 0:width].unsqueeze(1).broadcast_to(shape),
                                        src_of[:, cols16].unsqueeze(2).broadcast_to(shape), ALU.is_equal
                                        ).then_inc(hot, 1)
                    dve.wait_ge(counted, n + 1)
                    dve.wait_ge(added, n + 2)
                    v.tensor_tensor(deg[:], deg[:], ps[s][0:NT, 0:P], ALU.add).then_inc(added, 1)
            dve.wait_ge(root, 1)
            v.reciprocal(deg[:], deg[:]).then_inc(done, 1)
            dve.wait_ge(turned, 1)
            v.tensor_copy(cols[:], ps[2][:, 0:NT]).then_inc(turned, 1)

        @block.tensor
        def _(pe):
            with pe.Fori(0, ITERS // 2) as it:
                for s in range(2):
                    n = it * 2 + s
                    pe.wait_ge(hot, n * 2 + 2)
                    pe.wait_ge(added, n + 1)
                    for j in range(BODY):
                        last = nc.tensor.matmul(ps[s][0:NT, 0:P], tile_hot[:, s, j, :], place_hot[:, s, j, :],
                                                start=(j == 0), stop=(j == BODY - 1))
                    last.then_inc(counted, 1)
            pe.wait_ge(done, 1)
            nc.tensor.transpose(ps[2][:, 0:NT], deg[:], k.ident[0:NT, 0:NT]).then_inc(turned, 1)

        @block.scalar
        def _(act):
            act.wait_ge(added, ITERS + 2)
            nc.scalar.activation(deg[:], deg[:], ACT.Sqrt).then_inc(root, 1)


def features_first(k):
    nc = k.nc
    BANKS = 4
    with ExitStack() as c:
        sem, sb, bank = makers(k, c, "ff")
        xn = sb("xn", [P, STEP, D])
        tp = [bank(f"tp{i}") for i in range(STEP)]
        xn_ready, turned, copied = map(sem, ("xn_ready", "turned", "copied"))
        block = c.enter_context(nc.Block())

        @block.vector
        def _(dve):
            with dve.Fori(0, NSTEP) as it:
                for j in range(STEP):
                    dve.wait_ge(turned, it * STEP + j + 1)
                    normalise(k, xn[:, j, :], it * STEP + j).then_inc(xn_ready, 1)

        @block.tensor
        def _(pe):
            pe.sem_inc(turned, STEP)
            with pe.Fori(0, NSTEP) as it:
                for j in range(STEP):
                    pe.wait_ge(xn_ready, it * STEP + j + 1)
                    pe.wait_ge(copied, it * STEP + j + 1)
                    for b in range(K):
                        last = nc.tensor.transpose(tp[j][:, b * P:(b + 1) * P], xn[:, j, b * P:(b + 1) * P],
                                                   k.ident[:])
                    last.then_inc(turned, 1)

        @block.scalar
        def _(act):
            act.sem_inc(copied, STEP)
            with act.Fori(0, NSTEP) as it:
                for j in range(STEP):
                    act.wait_ge(turned, it * STEP + j + 1 + STEP)
                    nc.scalar.copy(k.h[:, :, bass.ds((it * STEP + j) * P, P)],
                                   tp[j][:, 0:D].rearrange("p (b n) -> p b n", b=K)).then_inc(copied, 1)


CHUNK = 512
CHUNKS = [(i, min(CHUNK, NP - i)) for i in range(0, NP, CHUNK)]


def graph_layer_inputs(k, l):
    nc, a, g = k.nc, k.a, k.gl
    w, row, start = g.w, g.rows, g.start
    tb, fb = g.banks[0:4], g.banks[4:7]

    block = g.open()

    @block.sync
    def _(sp):
        sp.dma_start(w[:], a["g1_w"][bass.ds(l * P, P), :].rearrange("p (b d) -> p b d", b=K)).then_inc(g.weights, 16)
        sp.dma_start(g.bias[:], a["g1_bias"][bass.ds(l, 1), :].broadcast_to([P, 2 * D])).then_inc(g.weights, 16)
        sp.dma_start(g.cols[:], a["g1_cols"][bass.ds(l * P, P), :]).then_inc(g.weights, 16)
        sp.dma_start(g.we[:], a["g1_we"][bass.ds(l * P, P), :]).then_inc(g.weights, 16)
        for s in range(NSTEP):
            sp.wait_ge(g.biased, STEP * (s + 1))
            sp.dma_start(tile_rows(k.xl_table, s * STEP, STEP, 0, D), row[:, s % 2, :, :]).then_inc(g.stored[s % 2], 16)
        for s in range(2):
            sp.wait_ge(g.stored[s], 16 * ((NSTEP + 1 - s) // 2))

    @block.tensor
    def _(pe):
        pe.wait_ge(g.weights, 64)
        for t in range(NT):
            if t >= 4:
                pe.wait_ge(g.biased, t - 3)
            for kk in range(K):
                last = nc.tensor.matmul(tb[t % 4][:, 0:D], k.h[:, kk, t * P:(t + 1) * P], w[:, kk, :],
                                        start=(kk == 0), stop=(kk == K - 1))
            last.then_inc(g.xl_ready, 1)
        n = 0
        for at, width in CHUNKS:
            for b in range(K):
                if n >= 3:
                    pe.wait_ge(g.rooted, n - 2)
                for kk in range(K):
                    last = nc.tensor.matmul(fb[n % 3][:, 0:width], w[:, kk, b * P:(b + 1) * P],
                                            k.h[:, kk, at:at + width], start=(kk == 0), stop=(kk == K - 1))
                last.then_inc(g.xlt_ready, 1)
                n += 1

    @block.scalar
    def _(act):
        act.wait_ge(g.summed_bias, 2)
        n = 0
        for at, width in CHUNKS:
            for b in range(K):
                act.wait_ge(g.xlt_ready, n + 1)
                if n >= 2:
                    act.wait_ge(g.started, n - 1)
                nc.scalar.activation(start[:, n % 2, 0:width], fb[n % 3][:, 0:width], ACT.Relu,
                                     bias=g.rootb[:, b:b + 1]).then_inc(g.rooted, 1)
                n += 1

    @block.vector
    def _(dve):
        v = nc.vector
        dve.wait_ge(g.weights, 64)
        v.tensor_tensor(g.rowb[:], g.bias[:, 0:D], g.bias[:, D:2 * D], ALU.add).then_inc(g.summed_bias, 1)
        v.tensor_tensor(g.rootb[:], g.cols[:, 0:K], g.cols[:, K:2 * K], ALU.add).then_inc(g.summed_bias, 1)
        dve.wait_ge(g.summed_bias, 2)
        for t in range(NT):
            s = t // STEP
            if t % STEP == 0 and s >= 2:
                dve.wait_ge(g.stored[s % 2], 16 * (s // 2))
            dve.wait_ge(g.xl_ready, t + 1)
            v.tensor_tensor(row[:, s % 2, t % STEP, :], tb[t % 4][:, 0:D], g.rowb[:], ALU.add).then_inc(g.biased, 1)
        n = 0
        for at, width in CHUNKS:
            for b in range(K):
                dve.wait_ge(g.rooted, n + 1)
                v.tensor_tensor(k.agg[:, b, at:at + width], start[:, n % 2, 0:width], k.dinv_row[:, at:at + width],
                                ALU.mult).then_inc(g.started, 1)
                n += 1
        dve.wait_ge(g.started, n)

    g.close()


def graph_layer_edges(k, l):
    nc, a, g = k.nc, k.a, k.gl
    EB, SB = 3, 4
    ep, ps = g.banks[0:EB], g.banks[EB:EB + SB]
    block = g.open()

    @block.sync
    def _(sp):
        def places(q, it):
            cols = bass.ds(it * (BODY * P) + q * HALF * P, HALF * P)
            return a["src_halves"][bass.ds(it * 2 + q, 1)].rearrange("a p j -> (a p) j"), a["ea128"][:, cols]

        def load(q, of_idx, of_ea):
            sp.dma_start(g.idx[:, q, :], of_idx).then_inc(g.idx_in[q], 16)
            sp.dma_start(g.ea[:, q, :], of_ea).then_inc(g.ea_in[q], 16)

        for q in range(2):
            load(q, *places(q, 0))
        with sp.Fori(0, ITERS - 1) as it:
            at = [places(q, it + 1) for q in range(2)]
            used = [sp.snap(it * (BODY // 2) + HALF // 2 * (q + 1) + EB) for q in range(2)]
            for q in range(2):
                sp.wait_ge(g.raw, used[q])
                load(q, *at[q])

    @block.gpsimd
    def _(pool):
        def gather(q, it, first):
            pool.wait_ge(g.idx_in[q], 16 if first else it * 16 + 16)
            if not first:
                pool.wait_ge(g.raw, it * (BODY // 2) - BODY // 2 + HALF // 2 * (q + 1) + EB)
                pool.wait_ge(g.hot, it * BODY - BODY + HALF * (q + 1))
            pool.sem_inc(g.begun, 1)
            for j in range(q * HALF, q * HALF + HALF):
                nc.gpsimd.indirect_dma_start(
                    out=g.g[:, j, :], out_offset=None, in_=k.xl_table[:, :],
                    in_offset=bass.IndirectOffsetOnAxis(ap=g.idx[:, q, j % HALF:j % HALF + 1], axis=0)
                ).then_inc(g.src_in[j], 16)

        for q in range(2):
            gather(q, 0, True)
        with pool.Fori(1, ITERS) as it:
            for q in range(2):
                gather(q, it, False)

    @block.tensor
    def _(pe):
        pe.sem_inc(g.summed, BODY)
        with pe.Fori(0, ITERS) as it:
            def products(u):
                if u % (HALF // 2) == 0:
                    pe.wait_ge(g.ea_in[u // (HALF // 2)], it * 16 + 16)
                pe.wait_ge(g.raw, it * (BODY // 2) + u + 1)
                q, at = (2 * u) // HALF, (2 * u) % HALF
                bank = ep[u % EB]
                for i in range(2):
                    last = nc.tensor.matmul(bank[:, i * D:(i + 1) * D], g.ea[:, q, (at + i) * P:(at + i + 1) * P],
                                            g.we[:], start=True, stop=True)
                last.then_inc(g.product, 1)

            def sums(u):
                pe.wait_ge(g.relu, it * (BODY // 2) + u + 1)
                for j in (2 * u, 2 * u + 1):
                    n = it * BODY + j
                    pe.wait_ge(g.hot, n + 1)
                    pe.wait_ge(g.added, n + 1)
                    for b in range(K):
                        last = nc.tensor.matmul(ps[j % SB][:, b * P:(b + 1) * P], g.msg[:, j, b * P:(b + 1) * P],
                                                g.onehot[:, j, :], start=True, stop=True)
                    last.then_inc(g.summed, 1)

            products(0)
            products(1)
            for u in range(BODY // 2):
                if u + 2 < BODY // 2:
                    products(u + 2)
                sums(u)

    @block.scalar
    def _(act):
        with act.Fori(0, ITERS) as it:
            for u in range(BODY // 2):
                act.wait_ge(g.raw, it * (BODY // 2) + u + 1 + EB)
                m = g.msg[:, 2 * u:2 * u + 2, :].rearrange("p a d -> p (a d)")
                nc.scalar.activation(m, m, ACT.Relu).then_inc(g.relu, 1)

    @block.vector
    def _(dve):
        base_regs = [dve.alloc_register(f"g1_base{i}") for i in range(BODY)]
        dve.sem_inc(g.raw, EB)
        dve.sem_inc(g.added, SB)
        with dve.Fori(0, ITERS) as it:
            seen = it * 16 + l * (16 * ITERS) + 16

            def add_pair(u):
                dve.wait_ge(g.product, it * (BODY // 2) + u + 1)
                dve.wait_ge(g.src_in[2 * u], seen)
                dve.wait_ge(g.src_in[2 * u + 1], seen)
                dve.wait_ge(g.summed, it * BODY + 2 * u + 2)
                nc.vector.tensor_tensor(g.msg[:, 2 * u:2 * u + 2, :], g.g[:, 2 * u:2 * u + 2, 0:D],
                                        ep[u % EB][:, 0:2 * D].rearrange("p (a d) -> p a d", a=2), ALU.add
                                        ).then_inc(g.raw, 1)

            def hot_tile(j):
                nc.vector.tensor_scalar(g.onehot[:, j, :], k.iota_row[:], k.dst_rel[:, bass.ds(it * BODY + j, 1)],
                                        g.g[:, j, D:XROW], ALU.is_equal, ALU.mult).then_inc(g.hot, 1)

            def add_tile(j, base):
                n = it * BODY + j
                window = k.agg[:, :, bass.ds(base, P)]
                dve.wait_ge(g.summed, n + 1 + BODY)
                dve.wait_ge(g.added, n + SB)
                nc.vector.tensor_tensor(window, window, ps[j % SB][:, 0:K * P].rearrange("p (b n) -> p b n", b=K),
                                        ALU.add).then_inc(g.added, 1)

            bases = load_bases(k, dve, base_regs, it * BODY)
            for u in range(BODY // 2 + 1):
                if u < BODY // 2:
                    add_pair(u)
                    hot_tile(2 * u)
                    hot_tile(2 * u + 1)
                if u > 0:
                    for i in range(2):
                        add_tile(2 * u - 2 + i, bases[2 * u - 2 + i])
        dve.wait_ge(g.added, ET + SB)

    g.close()


def graph_layer_norm(k, l):
    nc, g = k.nc, k.gl
    stats, mv, s = g.stats, g.mv, g.scale
    parts = [(i, min(CHUNK, N - i)) for i in range(0, N, CHUNK)]
    block = g.open()

    @block.vector
    def _(dve):
        v = nc.vector
        for b in range(K):
            for n, (at, width) in enumerate(CHUNKS):
                v.tensor_tensor(k.agg[:, b, at:at + width], k.agg[:, b, at:at + width], k.dinv_row[:, at:at + width],
                                ALU.mult).then_inc(g.conv, 1)
        for b in range(K):
            for n, (at, width) in enumerate(parts):
                dve.wait_ge(g.conv, b * len(CHUNKS) + n + 1)
                v.bn_stats(stats[:, b, n, :], k.agg[:, b, at:at + width]).then_inc(g.stat, 1)
        for b in range(K):
            dve.wait_ge(g.stat, (b + 1) * len(parts))
            v.bn_aggr(mv[:, b, :], stats[:, b, :, :].rearrange("p n s -> p (n s)")).then_inc(g.stat, 1)
            dve.wait_ge(g.stat, (b + 1) * len(parts))
        dve.wait_ge(g.stat, K * len(parts) + K)
        dve.wait_ge(g.root, 1)
        v.reciprocal(s[:, 0, :], s[:, 0, :]).then_inc(g.step, 1)
        dve.wait_ge(g.step, 1)
        v.tensor_tensor(s[:, 0, :], s[:, 0, :], g.cols[:, 2 * K:3 * K], ALU.mult).then_inc(g.step, 1)
        dve.wait_ge(g.step, 2)
        v.tensor_tensor(s[:, 1, :], s[:, 0, :], mv[:, :, 0], ALU.mult).then_inc(g.step, 1)
        dve.wait_ge(g.step, 3)
        v.tensor_tensor(s[:, 1, :], g.cols[:, 3 * K:4 * K], s[:, 1, :], ALU.subtract).then_inc(g.step, 1)
        n = 0
        for b in range(K):
            for at, width in CHUNKS:
                dve.wait_ge(g.scaled, n + 1)
                v.scalar_tensor_tensor(out=k.h[:, b, at:at + width], in0=k.agg[:, b, at:at + width],
                                       scalar=k.floor[:, bass.ds(l, 1)], in1=k.h[:, b, at:at + width],
                                       op0=ALU.max, op1=ALU.add).then_inc(g.updated, 1)
                n += 1
        dve.wait_ge(g.updated, n)

    @block.scalar
    def _(act):
        act.wait_ge(g.stat, K * len(parts) + K)
        nc.scalar.activation(s[:, 0, :], mv[:, :, 1], ACT.Sqrt, bias=k.eps[:, 0:1]).then_inc(g.root, 1)
        act.wait_ge(g.step, 4)
        for b in range(K):
            for at, width in CHUNKS:
                nc.scalar.activation(k.agg[:, b, at:at + width], k.agg[:, b, at:at + width], ACT.Identity,
                                     bias=s[:, 1, b:b + 1], scale=s[:, 0, b:b + 1]).then_inc(g.scaled, 1)

    g.close()


class GraphLayers:

    def __init__(self, k, c):
        self.nc = nc = k.nc
        sem, sb, bank = makers(k, c, "g1")
        self.w, self.we = sb("w", [P, K, D]), sb("we", [P, D])
        self.bias, self.rowb = sb("bias", [P, 2 * D]), sb("rowb", [P, D])
        self.cols, self.rootb = sb("cols", [P, 4 * K]), sb("rootb", [P, K])
        self.rows = sb("rows", [P, 2, STEP, D])
        self.start = sb("start", [P, 2, CHUNK])
        self.idx, self.ea = sb("idx", [P, 2, HALF], I32), sb("ea", [P, 2, HALF * P])
        self.g, self.msg = sb("g", [P, BODY, XROW]), sb("msg", [P, BODY, D])
        self.onehot = sb("onehot", [P, BODY, P])
        self.stats, self.mv, self.scale = sb("stats", [P, K, -(-N // CHUNK), 6]), sb("mv", [P, K, 2]), sb("scale", [P, 2, K])
        self.banks = [bank(f"b{i}") for i in range(7)]
        self.src_in = [k.pool_sem(f"g1_src_in{j}") for j in range(BODY)]
        self.stored = [sem(f"stored{i}") for i in range(2)]
        self.idx_in = [sem(f"idx_in{i}") for i in range(2)]
        self.ea_in = [sem(f"ea_in{i}") for i in range(2)]
        (self.weights, self.xl_ready, self.xlt_ready, self.rooted, self.biased, self.started, self.summed_bias,
         self.begun, self.raw, self.product, self.hot, self.relu, self.summed, self.added,
         self.conv, self.stat, self.root, self.step, self.scaled, self.updated) = made = [sem(n) for n in (
             "weights", "xl_ready", "xlt_ready", "rooted", "biased", "started", "summed_bias",
             "begun", "raw", "product", "hot", "relu", "summed", "added",
             "conv", "stat", "root", "step", "scaled", "updated")]
        self.cleared = made + self.stored + self.idx_in + self.ea_in

    def open(self):
        self.stack = ExitStack()
        return self.stack.enter_context(self.nc.Block())

    def close(self):
        self.stack.close()


def graph_layers(k):
    nc = k.nc
    with ExitStack() as c:
        g = k.gl = GraphLayers(k, c)
        with nc.Fori(0, LAYERS) as l:
            graph_layer_inputs(k, l)
            graph_layer_edges(k, l)
            graph_layer_norm(k, l)
            with nc.Block() as block:
                @block.gpsimd
                def _(pool):
                    for s in g.cleared:
                        pool.sem_clear(s)


def finish(k):
    nc = k.nc
    whole, rest = N // P, N % P
    with nc.semaphore("written") as written, nc.Block() as block:
        @block.sync
        def _(sp):
            out = k.a["out"]
            sp.dma_start(out[0:whole * P, :].rearrange("(t p) d -> p t d", p=P), k.x[:, 0:whole, :]).then_inc(written, 16)
            sp.dma_start(out[whole * P:N, :], k.x[0:rest, whole, :]).then_inc(written, 16)
            sp.wait_ge(written, 32)


def host_arrays(inp):
    f = {n: np.asarray(v) for n, v in inp.items()}

    def pad(v, rows, fill=0):
        out = np.full((rows,) + v.shape[1:], fill, v.dtype)
        out[:v.shape[0]] = v
        return out

    def blocks(v, n):
        return v.reshape(n, P, v.shape[-1]).transpose(1, 0, 2)

    src, dst = pad(f["src"], EP, NP - 1), pad(f["dst"], EP, N)
    ea3 = np.ones((4, EP), np.float32)
    ea3[:3] = pad(f["edge_attr_3"], EP).T
    out = {
        "x": pad(f["x"], NP),
        "dst_cols": dst.reshape(ET, P).T,
        "dst_first": dst[::P][None],
        "src_halves": src.reshape(ET // HALF, HALF, P).transpose(0, 2, 1),
        "src_cols": src.reshape(ET, P).T,
        "dst_row": dst[None],
        "dst_chunk": dst.reshape(P, ET),
        "dst_chunk_first": dst[::ET][None],
        "dst_chunk_last": dst[ET - 1::ET][None],
        "ea3": ea3,
        "ea128": pad(f["edge_attr_128"], EP).T,
        "gat_w": blocks(f["L0_gnn_W"].T, K),
        "gat_asrc": f["L0_gnn_a_src"].reshape(1, D),
        "gat_adst": f["L0_gnn_a_dst"].reshape(1, D),
        "gat_ew": np.concatenate([f["L0_gnn_edge_W"].T, f["L0_gnn_edge_b"][None]]),
        "gat_bias": f["L0_gnn_bias"].reshape(K, P).T,
    }

    def first(w):
        return w.reshape(EX, K, P, F).transpose(0, 2, 1, 3).reshape(EX * P, K * F)

    def second(w):
        return w.reshape(EX, M, P, D).transpose(0, 2, 1, 3).reshape(EX * P, M * D)

    def hidden_bias(b):
        return b.reshape(EX, M, P).transpose(0, 2, 1).reshape(EX * P, M)

    out |= {
        "g1_w": f["L1_gnn_W"].reshape(LAYERS, K, P, D).transpose(0, 2, 1, 3).reshape(LAYERS * P, K * D),
        "g1_we": f["L1_gnn_We"].reshape(LAYERS * P, D),
        "g1_bias": np.concatenate([f["L1_gnn_b"], f["L1_gnn_be"]], 1),
        "g1_cols": np.concatenate([f[n].reshape(LAYERS, K, P).transpose(0, 2, 1).reshape(LAYERS * P, K) for n in
                                   ("L1_gnn_b", "L1_gnn_root", "L1_gnn_gamma", "L1_gnn_beta")], 1),
        "f0_gate_w": blocks(f["L0_ffn_Wg"].T, K), "f0_gate_b": f["L0_ffn_bg"][None],
        "f0_w1": first(f["L0_ffn_W1"].transpose(0, 2, 1)), "f0_b1": hidden_bias(f["L0_ffn_b1"]),
        "f0_w2": second(f["L0_ffn_W2"].transpose(0, 2, 1)), "f0_b2": f["L0_ffn_b2"],
        "f1_gate_w": blocks(f["L1_ffn_gate_w"], K), "f1_gate_b": f["L1_ffn_gate_b"][None],
        "f1_w1": first(f["L1_ffn_w1"]), "f1_b1": hidden_bias(f["L1_ffn_b1"]),
        "f1_w2": second(f["L1_ffn_w2"]), "f1_b2": f["L1_ffn_b2"],
    }
    return {n: np.ascontiguousarray(v) for n, v in out.items()}


STAGES = [
    constants,
    lambda k: layer_stats(k, "ln1"),
    attention_tables,
    edge_scores,
    softmax_over_edges,
    attention_sums,
    lambda k: add_features_first(k, "gat_out", k.agg, "gat_bias"),
    lambda k: mixture(k, FFN[0]),
    Kernel.recycle,
    degrees,
    lambda k: layer_stats(k, "ln3"),
    features_first,
    graph_layers,
    lambda k: add_features_first(k, "graph_out", k.h, None),
    lambda k: mixture(k, FFN[1]),
    finish,
]


def program(nc, a, stages=None, after=None):
    ctx = ExitStack()
    with ctx:
        k = Kernel(nc, a, ctx)
        for stage in STAGES[:stages]:
            stage(k)
        if after:
            after(k)


def kernel(**inputs):
    import concourse.bacc as bacc
    from concourse.bass_utils import run_bass_kernel_spmd

    nc = bacc.Bacc("TRN2", target_bir_lowering=False, num_devices=1)
    arrays = {f"in_{n}": v for n, v in host_arrays(inputs).items()}
    a = {n[3:]: nc.dram_tensor(n, v.shape, mybir.dt.from_np(v.dtype), kind="ExternalInput").ap()
         for n, v in arrays.items()}
    a["out"] = nc.dram_tensor("out", (N, D), F32, kind="ExternalOutput").ap()
    program(nc, a)
    return run_bass_kernel_spmd(nc, [arrays], core_ids=[0]).results[0]["out"]
```

```python
from contextlib import ExitStack

import numpy as np

import concourse.bass as bass
from concourse import mybir

F32 = mybir.dt.float32
BF16 = mybir.dt.bfloat16
I32 = mybir.dt.int32
U8 = mybir.dt.uint8
ALU = mybir.AluOpType
ACT = mybir.ActivationFunctionType
AX = mybir.AxisListType.X

P = 128
N = 3125
NT = -(-N // P)
NP = NT * P
E = 53125
BODY = 16
HALF = 8
ET = -(-E // (P * BODY)) * BODY
EP = ET * P
ITERS = ET // BODY
D = 256
K = D // P
HEADS = 8
HD = D // HEADS
HROW = HEADS * (HD + 1)
GROW = HROW + HEADS
ACC = NP + P
LAG = 4
LAYERS = 5
XROW = D + 2
PARTS = 3
EA = PARTS * PARTS * 4
ED = 128
EX = 8
F = 1024
M = F // P
STEP = 5
NSTEP = NT // STEP
CAP = -(-5 * N // (4 * EX))
NEG = -1.0e30
EPS = 1e-5
FMAX = 3.4028234663852886e38


def makers(k, c, tag):
    return (lambda n: k.sem(f"{tag}_{n}"),
            lambda n, s, d=F32: c.enter_context(k.nc.sbuf_tensor(f"{tag}_{n}", s, d)),
            lambda n: c.enter_context(k.nc.psum_tensor(f"{tag}_{n}", [P, 512], F32)))


class Kernel:

    def __init__(self, nc, a, ctx):
        self.nc, self.a, self.ctx = nc, a, ctx
        self.sems, self.live = ctx.enter_context(ExitStack()), []
        sb = lambda n, s, d=F32: ctx.enter_context(nc.sbuf_tensor(n, s, d))
        dr = lambda n, s, d=F32: nc.dram_tensor(n, s, d, kind="Internal").ap()
        self.x = sb("x_res", [P, NT, D])
        self.ident = sb("ident", [P, P])
        self.iota_row = sb("iota_row", [P, P])
        self.base_row = sb("base_row", [1, ET], I32)
        self.base_lag = sb("base_lag", [1, LAG + ET], I32)
        self.dst_rel = sb("dst_rel", [P, ET])
        self.mean = sb("mean", [P, NT])
        self.rstd = sb("rstd", [P, NT])
        self.eps = sb("eps", [P, 1])
        self.agg = sb("agg", [P, K, ACC])
        self.h = sb("h", [P, K, ACC])
        self.dinv_row = sb("dinv_row", [P, ACC])
        self.floor = sb("floor", [P, LAYERS])
        self.logits = sb("logits", [P, NT, EX])
        self.weight = sb("weight", [P, 2, NT])
        self.write_row = sb("write_row", [P, 2, NT], I32)
        self.read_row = sb("read_row", [P, 2, NT], I32)
        self.group_expert = sb("group_expert", [1, 64], I32)
        self.h_table = dr("h_table", [ACC, GROW])
        self.s_table = dr("s_table", [ACC, HEADS])
        self.ea_parts = dr("ea_parts", [EA, EP], BF16)
        self.ew_parts = sb("ew_parts", [EA, D], BF16)
        self.alpha_d = dr("alpha_d", [EP, HEADS])
        self.attn_d = dr("attn_d", [EP, HEADS])
        self.deg_d = dr("deg_d", [NT, P])
        self.xl_table = dr("xl_table", [NP, XROW])
        self.slots = {m.layer: m.groups * m.rows for m in FFN}
        self.x_buf = {l: dr(f"x_buf{l}", [self.slots[l], D]) for l in (0, 1)}
        self.y_buf = {l: dr(f"y_buf{l}", [self.slots[l], D]) for l in (0, 1)}


    def sem(self, name):
        s = self.sems.enter_context(self.nc.semaphore(name))
        self.live.append(s)
        return s

    def pool_sem(self, name):
        return self.ctx.enter_context(self.nc.semaphore(name))

    def recycle(self):
        live, self.live = self.live, []
        with self.nc.Block() as block:
            @block.gpsimd
            def _(pool):
                for s in live:
                    pool.sem_clear(s)
        self.sems.close()


def load_bases(k, engine, regs, tile):
    return read_bases(engine, regs, k.base_row, tile)


def lagging_bases(k, engine, regs, tile):
    return read_bases(engine, regs, k.base_lag, tile)


def read_bases(engine, regs, row, at):
    engine.load(regs, row[0:1, bass.ds(at, len(regs))])
    return [engine.snap(r, min_val=0, max_val=N) for r in regs]


def tile_rows(dram, t0, n, c0=0, c1=None):
    v = dram[bass.ds(t0 * P, n * P), :] if c1 is None else dram[bass.ds(t0 * P, n * P), c0:c1]
    return v.rearrange("(b p) c -> p b c", p=P)


def constants(k):
    nc, a = k.nc, k.a
    with ExitStack() as c:
        sem, sb, bank = makers(k, c, "k")
        dst = sb("dst_cols", [P, ET], I32)
        basb = sb("base_bcast", [P, ET], I32)
        loaded, made, ints, zeroed, cleared = (sem(n) for n in ("loaded", "made", "ints", "zeroed", "cleared"))
        block = c.enter_context(nc.Block())

        @block.sync
        def _(sp):
            sp.dma_start(k.x[:], a["x"].rearrange("(t p) d -> p t d", p=P)).then_inc(loaded, 16)
            sp.dma_start(k.base_row[:], a["dst_first"]).then_inc(loaded, 16)
            sp.dma_start(k.base_lag[:, LAG:], a["dst_first"]).then_inc(loaded, 16)
            sp.dma_start(dst[:], a["dst_cols"]).then_inc(loaded, 16)
            sp.dma_start(basb[:], a["dst_first"].broadcast_to([P, ET])).then_inc(loaded, 16)
            sp.wait_ge(zeroed, 1)
            sp.dma_start(k.h_table[NP:ACC, :], k.agg[:, 0, 0:GROW]).then_inc(cleared, 16)
            sp.dma_start(k.s_table[NP:ACC, :], k.agg[:, 0, 0:HEADS]).then_inc(cleared, 16)
            sp.wait_ge(loaded, 80)
            sp.wait_ge(cleared, 32)

        @block.gpsimd
        def _(pool):
            nc.gpsimd.iota(k.iota_row[:], [[1, P]], base=0, channel_multiplier=0,
                           allow_small_or_imprecise_dtypes=True).then_inc(made, 1)
            nc.gpsimd.memset(k.ident[:], 0.0).then_inc(ints, 1)
            pool.wait_ge(ints, 1)
            nc.gpsimd.affine_select(out=k.ident[:], in_=k.ident[:], compare_op=ALU.not_equal, fill=1.0, base=0,
                                    pattern=[[-1, P]], channel_multiplier=1).then_inc(made, 1)

        @block.vector
        def _(dve):
            nc.vector.memset(k.agg[:], 0.0).then_inc(zeroed, 1)
            nc.vector.memset(k.eps[:], EPS).then_inc(made, 1)
            nc.vector.memset(k.h[:, :, NP:ACC], 0.0).then_inc(made, 1)
            nc.vector.memset(k.dinv_row[:, NP:ACC], 0.0).then_inc(made, 1)
            nc.vector.memset(k.base_lag[:, 0:LAG], 0).then_inc(made, 1)
            nc.vector.memset(k.floor[:, 0:LAYERS - 1], 0.0).then_inc(made, 1)
            nc.vector.memset(k.floor[:, LAYERS - 1:], -FMAX).then_inc(made, 1)
            dve.wait_ge(loaded, 80)
            nc.vector.tensor_tensor(k.dst_rel[:], dst[:], basb[:], ALU.subtract).then_inc(made, 1)


def edge_feature_parts(k):
    nc, a = k.nc, k.a
    C = 4 * EP // P
    with ExitStack() as c:
        sem, sb, bank = makers(k, c, "ep")
        loaded, split, out = sem("loaded"), sem("split"), sem("out")
        ea, ew = sb("ea", [P, C]), sb("ew", [4, D])
        ea_part, ew_part = sb("ea_part", [P, PARTS, C], BF16), sb("ew_part", [4, PARTS, D], BF16)
        block = c.enter_context(nc.Block())

        @block.sync
        def _(sp):
            sp.dma_start(ea[:], a["ea3"].rearrange("f (q c) -> (f q) c", c=C)).then_inc(loaded, 16)
            sp.dma_start(ew[:], a["gat_ew"]).then_inc(loaded, 16)
            for i in range(PARTS):
                sp.wait_ge(split, 2 * (2 * i + 1))
                for j in range(PARTS):
                    at, of_w = (j * PARTS + i) * 4, (i * PARTS + j) * 4
                    sp.dma_start(k.ea_parts[at:at + 4, :].rearrange("f (q c) -> (f q) c", c=C), ea_part[:, i, :]
                                 ).then_inc(out, 16)
                    sp.dma_start(k.ew_parts[of_w:of_w + 4, :], ew_part[:, i, :]).then_inc(out, 16)
            sp.wait_ge(out, 2 * 16 * PARTS * PARTS)

        @block.vector
        def _(dve):
            v = nc.vector
            dve.wait_ge(loaded, 32)
            for i in range(PARTS):
                for whole, part in ((ea, ea_part), (ew, ew_part)):
                    v.tensor_copy(part[:, i, :], whole[:]).then_inc(split, 1)
                if i + 1 < PARTS:
                    dve.wait_ge(split, 2 * (2 * i + 1))
                    for whole, part in ((ea, ea_part), (ew, ew_part)):
                        v.tensor_tensor(whole[:], whole[:], part[:, i, :], ALU.subtract).then_inc(split, 1)
                    dve.wait_ge(split, 2 * (2 * i + 2))


def layer_stats(k, tag):
    nc = k.nc
    with ExitStack() as c:
        sem, sb, bank = makers(k, c, tag)
        st = sb("st", [P, NT, 6])
        diff, var = sb("diff", [P, NT]), sb("var", [P, NT])
        stats, step, root = sem("stats"), sem("step"), sem("root")
        block = c.enter_context(nc.Block())

        @block.vector
        def _(dve):
            with dve.Fori(0, NSTEP) as it:
                for j in range(STEP):
                    nc.vector.bn_stats(st[:, bass.ds(it * STEP + j, 1), :].rearrange("p a s -> p (a s)"),
                                       k.x[:, bass.ds(it * STEP + j, 1), :].rearrange("p a s -> p (a s)")
                                       ).then_inc(stats, 1)
            dve.wait_ge(stats, NT)
            nc.vector.tensor_tensor(k.mean[:], st[:, :, 1], st[:, :, 4], ALU.add).then_inc(step, 1)
            nc.vector.tensor_tensor(diff[:], st[:, :, 1], st[:, :, 4], ALU.subtract).then_inc(step, 1)
            nc.vector.tensor_tensor(var[:], st[:, :, 2], st[:, :, 5], ALU.add).then_inc(step, 1)
            dve.wait_ge(step, 3)
            nc.vector.tensor_scalar(k.mean[:], k.mean[:], 0.5, None, ALU.mult).then_inc(step, 1)
            nc.vector.tensor_tensor(diff[:], diff[:], diff[:], ALU.mult).then_inc(step, 1)
            dve.wait_ge(step, 5)
            nc.vector.scalar_tensor_tensor(out=var[:], in0=diff[:], scalar=D / 4.0, in1=var[:],
                                           op0=ALU.mult, op1=ALU.add).then_inc(step, 1)
            dve.wait_ge(root, 1)
            nc.vector.reciprocal(k.rstd[:], k.rstd[:]).then_inc(step, 1)
            dve.wait_ge(step, 7)

        @block.scalar
        def _(act):
            act.wait_ge(step, 6)
            nc.scalar.activation(k.rstd[:], var[:], ACT.Sqrt, bias=k.eps[:, 0:1], scale=1.0 / D).then_inc(root, 1)


def normalise(k, out, t):
    return k.nc.vector.tensor_scalar(out, k.x[:, bass.ds(t, 1), :].rearrange("p a d -> p (a d)"),
                                     k.mean[:, bass.ds(t, 1)], k.rstd[:, bass.ds(t, 1)], ALU.subtract, ALU.mult)


def head_cols(ap):
    return ap.rearrange("p (h c) -> p h c", h=HEADS)[:, :, 0:HD]


def attention_tables(k):
    nc, a = k.nc, k.a
    BANKS = 2
    with ExitStack() as c:
        sem, sb, bank = makers(k, c, "tab")
        w = sb("gat_w", [P, K, D])
        asrc, adst = sb("asrc_b", [P, D]), sb("adst_b", [P, D])
        xn = sb("xn", [P, STEP, D])
        xt = sb("xt", [P, STEP, K * P])
        row = sb("h_rows", [P, STEP, GROW])
        prod = sb("prod", [P, 2, STEP, D])
        tp = [bank(f"tp{i}") for i in range(BANKS)]
        hp = [bank(f"hp{i}") for i in range(BANKS)]
        weights, xn_ready, turned, xt_ready, h_ready, h_copied, scored, stored, rows_free, mul = map(sem, (
            "weights", "xn_ready", "turned", "xt_ready", "h_ready", "h_copied", "scored", "stored", "rows_free", "mul"))
        block = c.enter_context(nc.Block())

        @block.sync
        def _(sp):
            sp.dma_start(w[:], a["gat_w"]).then_inc(weights, 16)
            sp.dma_start(asrc[:], a["gat_asrc"].broadcast_to([P, D])).then_inc(weights, 16)
            sp.dma_start(adst[:], a["gat_adst"].broadcast_to([P, D])).then_inc(weights, 16)
            sp.sem_inc(rows_free, 1)
            with sp.Fori(0, NSTEP) as it:
                rows, scores = tile_rows(k.h_table, it * STEP, STEP), tile_rows(k.s_table, it * STEP, STEP)
                sp.wait_ge(scored, it * STEP + STEP)
                sp.dma_start(rows, row[:]).then_inc(stored, 16)
                sp.dma_start(scores, row[:, :, HROW:GROW]).then_inc(stored, 16)
                sp.wait_ge(stored, it * 32 + 32)
                sp.sem_inc(rows_free, 1)

        @block.vector
        def _(dve):
            dve.wait_ge(weights, 48)
            with dve.Fori(0, NSTEP) as it:
                dve.wait_ge(turned, it * STEP + BANKS)
                for j in range(STEP):
                    normalise(k, xn[:, j, :], it * STEP + j).then_inc(xn_ready, 1)
                for j in range(STEP):
                    dve.wait_ge(h_copied, it * STEP + j + 1 + BANKS)
                    for n, vec in enumerate((asrc, adst)):
                        nc.vector.tensor_tensor(prod[:, n, j, :].rearrange("p (h c) -> p h c", h=HEADS),
                                                head_cols(row[:, j, 0:HROW]),
                                                vec[:].rearrange("p (h c) -> p h c", h=HEADS),
                                                ALU.mult).then_inc(mul, 1)
                for j in range(STEP):
                    dve.wait_ge(mul, it * 2 * STEP + 2 * j + 2)
                    nc.vector.tensor_reduce(row[:, j, HROW:GROW],
                                            prod[:, 0, j, :].rearrange("p (h c) -> p h c", h=HEADS), AX, ALU.add)
                    nc.vector.tensor_reduce(row[:, j, 0:HROW].rearrange("p (h c) -> p h c", h=HEADS)[:, :, HD],
                                            prod[:, 1, j, :].rearrange("p (h c) -> p h c", h=HEADS),
                                            AX, ALU.add).then_inc(scored, 1)

        @block.tensor
        def _(pe):
            pe.wait_ge(weights, 48)
            pe.sem_inc(turned, BANKS)
            with pe.Fori(0, NSTEP) as it:
                for j in range(STEP + 1):
                    if j < STEP:
                        pe.wait_ge(xn_ready, it * STEP + j + 1)
                        pe.wait_ge(xt_ready, it * STEP + j + 1)
                        for b in range(K):
                            last = nc.tensor.transpose(tp[j % BANKS][:, b * P:(b + 1) * P],
                                                       xn[:, j, b * P:(b + 1) * P], k.ident[:])
                        last.then_inc(turned, 1)
                    if j > 0:
                        i = j - 1
                        pe.wait_ge(xt_ready, it * STEP + i + 1 + BANKS)
                        pe.wait_ge(h_copied, it * STEP + i + 1)
                        for b in range(K):
                            last = nc.tensor.matmul(hp[i % BANKS][:, 0:D], xt[:, i, b * P:(b + 1) * P], w[:, b, :],
                                                    start=(b == 0), stop=(b == K - 1))
                        last.then_inc(h_ready, 1)

        @block.scalar
        def _(act):
            act.sem_inc(xt_ready, BANKS)
            act.sem_inc(h_copied, BANKS)
            with act.Fori(0, NSTEP) as it:
                for j in range(STEP + 1):
                    if j < STEP:
                        act.wait_ge(turned, it * STEP + j + 1 + BANKS)
                        nc.scalar.copy(xt[:, j, :], tp[j % BANKS][:, 0:D]).then_inc(xt_ready, 1)
                    if j > 0:
                        i = j - 1
                        if i == 0:
                            act.wait_ge(rows_free, it + 1)
                        act.wait_ge(h_ready, it * STEP + i + 1)
                        nc.scalar.copy(head_cols(row[:, i, 0:HROW]),
                                       hp[i % BANKS][:, 0:D].rearrange("p (h c) -> p h c", h=HEADS)
                                       ).then_inc(h_copied, 1)


def edge_scores(k):
    nc, a = k.nc, k.a
    BANKS = 4
    with ExitStack() as c:
        sem, sb, bank = makers(k, c, "sc")
        idx = sb("idx", [P, 2, HALF], I32)
        ea = sb("ea", [EA, 2, HALF * P], BF16)
        dstb = sb("dstb", [P, 2, HALF * P], I32)
        win = sb("win", [P, BODY, HROW])
        g = sb("g", [P, BODY, HEADS])
        onehot = sb("onehot", [P, BODY, P])
        enc = sb("enc", [P, BODY, HROW])
        prod = sb("prod", [P, BODY, HROW])
        dots, alpha = sb("dots", [P, BODY, HEADS]), sb("alpha", [P, BODY, HEADS])
        node_i = sb("node_i", [P, ET], I32)
        basb = sb("basb", [P, ET], I32)
        node = sb("node", [P, ET])
        pe_e = [bank(f"pe_e{i}") for i in range(BANKS)]
        pe_h = [bank(f"pe_h{i}") for i in range(BANKS)]
        idx_in, ea_in, dst_in = ([sem(f"{n}{q}") for q in range(2)] for n in ("idx_in", "ea_in", "dst_in"))
        win_in = [sem(f"win_in{j}") for j in range(BODY)]
        src_in = [k.pool_sem(f"sc_src_in{j}") for j in range(BODY)]
        al_out = [sem(f"al_out{q}") for q in range(2)]
        const, consts, begun, encoded, relu, hot, expanded, multiplied, summed, scored = map(sem, (
            "const", "consts", "begun", "encoded", "relu", "hot", "expanded", "multiplied", "summed", "scored"))
        block = c.enter_context(nc.Block())

        @block.sync
        def _(sp):
            base_regs = [sp.alloc_register(f"sc_base{i}") for i in range(HALF)]
            sp.dma_start(basb[:], a["dst_first"].broadcast_to([P, ET])).then_inc(const, 16)

            def places(q, it):
                cols = bass.ds(it * (BODY * P) + q * HALF * P, HALF * P)
                return (a["src_halves"][bass.ds(it * 2 + q, 1)].rearrange("a p j -> (a p) j"), k.ea_parts[:, cols],
                        a["dst_row"][:, cols].broadcast_to([P, HALF * P]))

            def load(q, it, of_idx, of_ea, of_dst):
                sp.dma_start(idx[:, q, :], of_idx).then_inc(idx_in[q], 16)
                sp.dma_start(ea[:, q, :], of_ea).then_inc(ea_in[q], 16)
                sp.dma_start(dstb[:, q, :], of_dst).then_inc(dst_in[q], 16)
                bases = load_bases(k, sp, base_regs, it * BODY + q * HALF)
                for j, base in zip(range(q * HALF, q * HALF + HALF), bases):
                    sp.dma_start(win[:, j, :], k.h_table[bass.ds(base, P), 0:HROW]).then_inc(win_in[j], 16)

            def store(q, halves, rows):
                sp.wait_ge(scored, halves)
                sp.dma_start(rows, alpha[:, q * HALF:(q + 1) * HALF, :]).then_inc(al_out[q], 16)

            for q in range(2):
                load(q, 0, *places(q, 0))
            with sp.Fori(0, ITERS - 1) as it:
                nxt = sp.snap(it + 1)
                at = [places(q, nxt) for q in range(2)]
                stored = [(sp.snap(it * 2 + q + 1), tile_rows(k.alpha_d, it * BODY + q * HALF, HALF)) for q in range(2)]
                for q in range(2):
                    sp.wait_ge(scored, stored[q][0])
                    load(q, nxt, *at[q])
                    store(q, *stored[q])
            for q in range(2):
                store(q, ET // HALF - 1 + q, tile_rows(k.alpha_d, ET - BODY + q * HALF, HALF))
            for q in range(2):
                sp.wait_ge(al_out[q], ITERS * 16)

        @block.gpsimd
        def _(pool):
            nc.gpsimd.iota(node_i[:], [[0, ET]], base=0, channel_multiplier=1).then_inc(consts, 1)

            def gather(q, it, first):
                pool.wait_ge(idx_in[q], 16 if first else it * 16 + 16)
                if not first:
                    pool.wait_ge(scored, it * 2 - 1 + q)
                pool.sem_inc(begun, 1)
                for j in range(q * HALF, q * HALF + HALF):
                    nc.gpsimd.indirect_dma_start(
                        out=g[:, j, :], out_offset=None, in_=k.s_table[:, :],
                        in_offset=bass.IndirectOffsetOnAxis(ap=idx[:, q, j % HALF:j % HALF + 1], axis=0)
                    ).then_inc(src_in[j], 16)

            for q in range(2):
                gather(q, 0, True)
            with pool.Fori(1, ITERS) as it:
                for q in range(2):
                    gather(q, it, False)

        @block.tensor
        def _(pe):
            with pe.Fori(0, ITERS) as it:
                for j in range(BODY):
                    n = it * BODY + j
                    q = j // HALF
                    if j % HALF == 0:
                        pe.wait_ge(ea_in[q], it * 16 + 16)
                    pe.wait_ge(relu, n + 1)
                    nc.tensor.matmul(pe_e[j % BANKS][:, 0:D], ea[:, q, (j % HALF) * P:(j % HALF + 1) * P],
                                     k.ew_parts[:],
                                     start=True, stop=True).then_inc(encoded, 1)
                    pe.wait_ge(win_in[j], it * 16 + 16)
                    pe.wait_ge(hot, n + 1)
                    pe.wait_ge(multiplied, n + 1)
                    nc.tensor.matmul(pe_h[j % BANKS][:, 0:HROW], onehot[:, j, :], win[:, j, :],
                                     start=True, stop=True).then_inc(expanded, 1)

        @block.scalar
        def _(act):
            act.sem_inc(relu, BANKS)
            act.wait_ge(consts, 2)

            with act.Fori(0, ITERS) as it:
                for j in range(BODY):
                    n = it * BODY + j
                    act.wait_ge(encoded, n + 1)
                    act.wait_ge(multiplied, n + 1)
                    nc.scalar.activation(head_cols(enc[:, j, :]),
                                         pe_e[j % BANKS][:, 0:D].rearrange("p (h c) -> p h c", h=HEADS),
                                         ACT.Relu).then_inc(relu, 1)

        @block.vector
        def _(dve):
            nc.vector.memset(enc[:], 1.0).then_inc(consts, 1)
            dve.wait_ge(const, 16)
            dve.wait_ge(consts, 2)
            nc.vector.tensor_tensor(node[:], node_i[:], basb[:], ALU.add).then_inc(consts, 1)
            dve.wait_ge(consts, 3)
            dve.sem_inc(multiplied, BANKS)

            def hot_tile(it, j):
                q = j // HALF
                if j % HALF == 0:
                    dve.wait_ge(dst_in[q], it * 16 + 16)
                nc.vector.tensor_scalar(onehot[:, j, :], dstb[:, q, (j % HALF) * P:(j % HALF + 1) * P],
                                        node[:, bass.ds(it * BODY + j, 1)], None, ALU.is_equal).then_inc(hot, 1)

            def sum_tile(it, j):
                dve.wait_ge(multiplied, it * BODY + j + 1 + BANKS)
                nc.vector.tensor_reduce(dots[:, j, :], prod[:, j, :].rearrange("p (h c) -> p h c", h=HEADS),
                                        AX, ALU.add).then_inc(summed, 1)

            def score_half(it, q, first):
                if not first:
                    dve.wait_ge(al_out[q], it * 16)
                for j in range(q * HALF, q * HALF + HALF):
                    dve.wait_ge(src_in[j], it * 16 + 16)
                dve.wait_ge(summed, it * BODY + HALF * (q + 1))
                nc.vector.tensor_tensor(alpha[:, q * HALF:(q + 1) * HALF, :], dots[:, q * HALF:(q + 1) * HALF, :],
                                        g[:, q * HALF:(q + 1) * HALF, :], ALU.add).then_inc(scored, 1)

            def body(it, first):
                hot_tile(it, 0)
                for j in range(BODY):
                    n = it * BODY + j
                    if j + 1 < BODY:
                        hot_tile(it, j + 1)
                    dve.wait_ge(relu, n + 1 + BANKS)
                    dve.wait_ge(expanded, n + 1)
                    nc.vector.tensor_tensor(prod[:, j, :], enc[:, j, :], pe_h[j % BANKS][:, 0:HROW],
                                            ALU.mult).then_inc(multiplied, 1)
                    if j > 0:
                        sum_tile(it, j - 1)
                    if j == HALF + 1:
                        score_half(it, 0, first)
                sum_tile(it, BODY - 1)
                score_half(it, 1, first)

            body(0, True)
            with dve.Fori(1, ITERS) as it:
                body(it, False)


def softmax_over_edges(k):
    nc, a = k.nc, k.a
    H = HEADS
    with ExitStack() as c:
        sem, sb, bank = makers(k, c, "sm")
        s = sb("s", [P, ET, H])
        f = sb("f", [P, ET, H])
        r = sb("r", [P, ET, H])
        dst = sb("dst", [P, ET], I32)
        same = sb("same", [P, ET])
        after = sb("after", [P, ET])
        gap, gap_after = sb("gap", [P, ET]), sb("gap_after", [P, ET])
        first, last = sb("first", [P, ET]), sb("last", [P, ET])
        firstp, lastp = sb("firstp", [P, ET]), sb("lastp", [P, ET])
        dstf, ends = sb("dstf", [P, ET]), sb("ends", [P, 2])
        heads_i, tails_i = sb("heads_i", [H, P], I32), sb("tails_i", [H, P], I32)
        joins = sb("joins", [H, P])
        onrun = sb("onrun", [H, P])
        wf, wb = sb("wf", [H, P]), sb("wb", [H, P])
        joinp, wfp, wbp = sb("joinp", [H, P]), sb("wfp", [H, P]), sb("wbp", [H, P])
        edge = sb("edge", [P, 2, H])
        edge_t = sb("edge_t", [H, 2, P])
        carry_t = sb("carry_t", [H, 2, P])
        carry = sb("carry", [P, 2, H])
        tot = sb("tot", [P, H])
        ps = [bank(f"ps{i}") for i in range(2)]
        loaded, done, turned, exped, out, clears = map(sem, ("loaded", "done", "turned", "exped", "out", "clears"))
        count = [0]
        block = c.enter_context(nc.Block())
        PE_STEPS = []

        def by_head(t):
            return t[:].rearrange("p t h -> p h t")

        def bcast(v):
            return v[:].unsqueeze(2).broadcast_to([P, ET, H])

        @block.vector
        def _(dve):
            def do(ins):
                count[0] += 1
                ins.then_inc(done, 1)
                dve.wait_ge(done, count[0])

            def free(ins):
                count[0] += 1
                ins.then_inc(done, 1)

            v = nc.vector
            dve.wait_ge(loaded, 64)
            do(v.tensor_copy(dstf[:], dst[:]))
            free(v.memset(same[:, 0:1], 1.0))
            free(v.memset(after[:, ET - 1:ET], 1.0))
            free(v.tensor_copy(ends[:, 0:1], dstf[:, 0:1]))
            free(v.tensor_copy(ends[:, 1:2], dstf[:, ET - 1:ET]))
            free(v.tensor_tensor(same[:, 1:ET], dstf[:, 1:ET], dstf[:, 0:ET - 1], ALU.is_equal))
            do(v.tensor_tensor(after[:, 0:ET - 1], dstf[:, 1:ET], dstf[:, 0:ET - 1], ALU.is_equal))
            free(v.tensor_scalar(first[:], dstf[:], ends[:, 0:1], None, ALU.is_equal))
            do(v.tensor_scalar(last[:], dstf[:], ends[:, 1:2], None, ALU.is_equal))
            free(v.tensor_tensor(onrun[:], heads_i[:], tails_i[:], ALU.is_equal))
            free(v.memset(joins[:, 0:1], 0.0))
            do(v.tensor_tensor(joins[:, 1:P], heads_i[:, 1:P], tails_i[:, 0:P - 1], ALU.is_equal))
            free(v.memset(wf[:], 0.0))
            do(v.tensor_tensor(wb[:], onrun[:], joins[:], ALU.mult))
            do(v.tensor_tensor(wf[:, 0:P - 1], onrun[:, 0:P - 1], joins[:, 1:P], ALU.mult))
            for mask, pen in ((same, gap), (after, gap_after), (first, firstp), (last, lastp),
                              (joins, joinp), (wf, wfp), (wb, wbp)):
                do(v.tensor_scalar(pen[:], mask[:], -NEG, NEG, ALU.mult, ALU.add))

            def over_rows(weight_f, weight_b, join, op0, op1, neutral):
                turn = PE_STEPS
                turn.append(count[0])
                dve.wait_ge(turned, len(turn))
                do(v.tensor_copy(edge_t[:].rearrange("h a p -> h (a p)"), ps[0][0:H, 0:2 * P]))
                do(v.tensor_tensor(edge_t[:, 0, 0:P - 1], edge_t[:, 0, 0:P - 1], join[:, 1:P], op0))
                do(v.tensor_tensor(edge_t[:, 1, :], edge_t[:, 1, :], join[:], op0))
                do(v.memset(carry_t[:], neutral))
                do(v.tensor_tensor_scan(carry_t[:, 0, 1:P], weight_f[:, 0:P - 1], edge_t[:, 0, 0:P - 1], neutral,
                                        op0, op1))
                do(v.tensor_tensor_scan(carry_t[:, 1, 0:P - 1][:, ::-1], weight_b[:, 1:P][:, ::-1],
                                        edge_t[:, 1, 1:P][:, ::-1], neutral, op0, op1))
                turn.append(count[0])
                dve.wait_ge(turned, len(turn))
                do(v.tensor_copy(carry[:].rearrange("p a h -> p (a h)"), ps[1][:, 0:2 * H]))

            do(v.scalar_tensor_tensor(out=s[:], in0=s[:], scalar=0.2, in1=s[:], op0=ALU.mult, op1=ALU.max))
            for n, pen in enumerate((lastp, firstp)):
                do(v.tensor_tensor(r[:], s[:], bcast(pen), ALU.add))
                do(v.tensor_reduce(edge[:, n, :], by_head(r), AX, ALU.max))
            over_rows(wfp, wbp, joinp, ALU.add, ALU.max, NEG)
            for h in range(H):
                free(v.tensor_tensor_scan(f[:, :, h], gap[:], s[:, :, h], carry[:, 0, h:h + 1], ALU.add, ALU.max))
            dve.wait_ge(done, count[0])
            for h in range(H):
                free(v.tensor_tensor_scan(r[:, :, h][:, ::-1], gap_after[:][:, ::-1], f[:, :, h][:, ::-1],
                                          carry[:, 1, h:h + 1], ALU.add, ALU.max))
            dve.wait_ge(done, count[0])
            do(v.tensor_tensor(s[:], s[:], r[:], ALU.subtract))
            k.sm_exp_at = count[0]
            dve.wait_ge(exped, 1)
            for n, mask in enumerate((last, first)):
                do(v.tensor_tensor(r[:], s[:], bcast(mask), ALU.mult))
                do(v.tensor_reduce(edge[:, n, :], by_head(r), AX, ALU.add))
            over_rows(wf, wb, joins, ALU.mult, ALU.add, 0.0)
            for h in range(H):
                free(v.tensor_tensor_scan(f[:, :, h], same[:], s[:, :, h], carry[:, 0, h:h + 1], ALU.mult, ALU.add))
            dve.wait_ge(done, count[0])
            do(v.tensor_tensor(tot[:], f[:, ET - 1, :], carry[:, 1, :], ALU.add))
            for h in range(H):
                free(v.tensor_tensor_scan(r[:, :, h][:, ::-1], after[:][:, ::-1], f[:, :, h][:, ::-1],
                                          tot[:, h:h + 1], ALU.mult, ALU.max))
            dve.wait_ge(done, count[0])
            do(v.tensor_scalar(r[:], r[:], 1e-10, None, ALU.max))
            do(v.reciprocal(r[:], r[:]))
            do(v.tensor_tensor(s[:], s[:], r[:], ALU.mult))

        @block.sync
        def _(sp):
            sp.dma_start(s[:], k.alpha_d.rearrange("(p t) h -> p t h", p=P)).then_inc(loaded, 16)
            sp.dma_start(dst[:], a["dst_chunk"]).then_inc(loaded, 16)
            sp.dma_start(heads_i[:], a["dst_chunk_first"].broadcast_to([H, P])).then_inc(loaded, 16)
            sp.dma_start(tails_i[:], a["dst_chunk_last"].broadcast_to([H, P])).then_inc(loaded, 16)
            cleared = 0
            for l in (0, 1):
                for at in range(0, k.slots[l], 4 * P):
                    sp.dma_start(k.x_buf[l][at:at + 4 * P, :].rearrange("(b p) d -> p b d", p=P),
                                 k.agg[:, 0, 0:4 * D].rearrange("p (b d) -> p b d", d=D)).then_inc(clears, 16)
                    cleared += 16
            sp.wait_ge(clears, cleared)
            sp.wait_ge(done, count[0])
            sp.dma_start(k.attn_d.rearrange("(p t) h -> p t h", p=P), s[:]).then_inc(out, 16)
            sp.wait_ge(out, 16)

        @block.tensor
        def _(pe):
            for n, at in enumerate(PE_STEPS):
                pe.wait_ge(done, at)
                for m in range(2):
                    if n % 2 == 0:
                        ins = nc.tensor.transpose(ps[0][0:H, m * P:(m + 1) * P], edge[:, m, :], k.ident[:])
                    else:
                        ins = nc.tensor.transpose(ps[1][:, m * H:(m + 1) * H], carry_t[:, m, :], k.ident[0:H, 0:H])
                ins.then_inc(turned, 1)

        @block.scalar
        def _(act):
            act.wait_ge(done, k.sm_exp_at)
            nc.scalar.activation(s[:], s[:], ACT.Exp).then_inc(exped, 1)


def attention_sums(k):
    nc, a = k.nc, k.a
    BANKS = 8
    with ExitStack() as c:
        sem, sb, bank = makers(k, c, "at")
        idx = sb("idx", [P, 2, HALF], I32)
        g = sb("g", [P, BODY, GROW])
        attn = sb("attn", [P, BODY, HEADS])
        msg = sb("msg", [P, BODY, D])
        onehot = sb("onehot", [P, BODY, P])
        ps = [bank(f"ps{i}") for i in range(BANKS)]
        idx_in, attn_in = ([sem(f"{n}{q}") for q in range(2)] for n in ("idx_in", "attn_in"))
        src_in = [k.pool_sem(f"at_src_in{j}") for j in range(BODY)]
        begun, weighted, hot, summed, added = map(sem, ("begun", "weighted", "hot", "summed", "added"))
        block = c.enter_context(nc.Block())

        @block.sync
        def _(sp):
            def places(q, it):
                return (a["src_halves"][bass.ds(it * 2 + q, 1)].rearrange("a p j -> (a p) j"),
                        tile_rows(k.attn_d, it * BODY + q * HALF, HALF))

            def load(q, of_idx, of_attn):
                sp.dma_start(idx[:, q, :], of_idx).then_inc(idx_in[q], 16)
                sp.dma_start(attn[:, q * HALF:(q + 1) * HALF, :], of_attn).then_inc(attn_in[q], 16)

            for q in range(2):
                load(q, *places(q, 0))
            with sp.Fori(0, ITERS - 1) as it:
                at = [places(q, it + 1) for q in range(2)]
                used = [sp.snap(it * BODY + HALF * (q + 1)) for q in range(2)]
                for q in range(2):
                    sp.wait_ge(weighted, used[q])
                    load(q, *at[q])

        @block.gpsimd
        def _(pool):
            def gather(q, it, first):
                pool.wait_ge(idx_in[q], 16 if first else it * 16 + 16)
                if not first:
                    pool.wait_ge(weighted, it * BODY - BODY + HALF * (q + 1))
                pool.sem_inc(begun, 1)
                for j in range(q * HALF, q * HALF + HALF):
                    nc.gpsimd.indirect_dma_start(
                        out=g[:, j, :], out_offset=None, in_=k.h_table[:, :],
                        in_offset=bass.IndirectOffsetOnAxis(ap=idx[:, q, j % HALF:j % HALF + 1], axis=0)
                    ).then_inc(src_in[j], 16)

            for q in range(2):
                gather(q, 0, True)
            with pool.Fori(1, ITERS) as it:
                for q in range(2):
                    gather(q, it, False)

        @block.tensor
        def _(pe):
            pe.sem_inc(summed, BODY)
            with pe.Fori(0, ITERS) as it:
                for j in range(BODY):
                    n = it * BODY + j
                    pe.wait_ge(weighted, n + 1)
                    pe.wait_ge(hot, n + 1)
                    pe.wait_ge(added, n + 1)
                    for b in range(K):
                        last = nc.tensor.matmul(ps[j % BANKS][:, b * P:(b + 1) * P], msg[:, j, b * P:(b + 1) * P],
                                                onehot[:, j, :], start=True, stop=True)
                    last.then_inc(summed, 1)

        @block.vector
        def _(dve):
            base_regs = [dve.alloc_register(f"at_base{i}") for i in range(BODY)]
            dve.sem_inc(added, BANKS)

            def weigh_tile(it, j):
                if j % HALF == 0:
                    dve.wait_ge(attn_in[j // HALF], it * 16 + 16)
                dve.wait_ge(src_in[j], it * 16 + 16)
                dve.wait_ge(summed, it * BODY + j + 1)
                nc.vector.tensor_tensor(msg[:, j, :].rearrange("p (h c) -> p h c", h=HEADS),
                                        head_cols(g[:, j, 0:HROW]),
                                        attn[:, j, :].unsqueeze(2).broadcast_to([P, HEADS, HD]),
                                        ALU.mult).then_inc(weighted, 1)

            def hot_tile(it, j):
                nc.vector.tensor_scalar(onehot[:, j, :], k.iota_row[:], k.dst_rel[:, bass.ds(it * BODY + j, 1)], None,
                                        ALU.is_equal).then_inc(hot, 1)

            def add_tile(n, bank, base):
                window = k.agg[:, :, bass.ds(base, P)]
                dve.wait_ge(summed, n + 1 + BODY)
                dve.wait_ge(added, n + BANKS)
                nc.vector.tensor_tensor(window, window, bank[:, 0:K * P].rearrange("p (b n) -> p b n", b=K),
                                        ALU.add).then_inc(added, 1)

            def body(it, first):
                for j in range(BODY):
                    weigh_tile(it, j)
                    if j == 0:
                        bases = lagging_bases(k, dve, base_regs, it * BODY)
                    if j >= LAG or not first:
                        add_tile(it * BODY + j - LAG, ps[(j - LAG) % BANKS], bases[j])
                    hot_tile(it, j)

            body(0, True)
            with dve.Fori(1, ITERS) as it:
                body(it, False)
            for i, base in enumerate(lagging_bases(k, dve, base_regs[0:LAG], ET)):
                add_tile(ET - LAG + i, ps[(BODY - LAG + i) % BANKS], base)
            dve.wait_ge(added, ET + BANKS)


def add_features_first(k, tag, src, bias):
    nc, a = k.nc, k.a
    BANKS = 2
    with ExitStack() as c:
        sem, sb, bank = makers(k, c, tag)
        col = sb("bias", [P, K])
        part = sb("part", [P, STEP, K * P])
        ps = [bank(f"ps{i}") for i in range(BANKS)]
        loaded, copied, turned, added = map(sem, ("loaded", "copied", "turned", "added"))
        block = c.enter_context(nc.Block())

        @block.sync
        def _(sp):
            if bias:
                sp.dma_start(col[:], a[bias]).then_inc(loaded, 16)

        @block.scalar
        def _(act):
            if bias:
                act.wait_ge(loaded, 16)
            with act.Fori(0, NSTEP) as it:
                for j in range(STEP):
                    act.wait_ge(turned, it * STEP + j + 1)
                    for b in range(K):
                        of = src[:, b, bass.ds((it * STEP + j) * P, P)]
                        to = part[:, j, b * P:(b + 1) * P]
                        ins = (nc.scalar.activation(to, of, ACT.Identity, bias=col[:, b:b + 1]) if bias
                               else nc.scalar.copy(to, of))
                    ins.then_inc(copied, 1)

        @block.tensor
        def _(pe):
            pe.sem_inc(turned, STEP)
            with pe.Fori(0, NSTEP) as it:
                for j in range(STEP):
                    pe.wait_ge(copied, it * STEP + j + 1)
                    pe.wait_ge(added, it * STEP + j + 1)
                    for b in range(K):
                        last = nc.tensor.transpose(ps[(j) % BANKS][:, b * P:(b + 1) * P],
                                                   part[:, j, b * P:(b + 1) * P], k.ident[:])
                    last.then_inc(turned, 1)

        @block.vector
        def _(dve):
            dve.sem_inc(added, 1)
            with dve.Fori(0, NSTEP) as it:
                for j in range(STEP):
                    row = k.x[:, bass.ds(it * STEP + j, 1), :].rearrange("p a d -> p (a d)")
                    dve.wait_ge(turned, it * STEP + j + 1 + STEP)
                    nc.vector.tensor_tensor(row, row, ps[j % BANKS][:, 0:D], ALU.add).then_inc(added, 1)
            dve.wait_ge(added, NT + 1)


class Experts:

    def __init__(self, layer, top, blocks, gate_w, gate_b, w1, b1, w2, b2):
        self.layer, self.top, self.blocks = layer, top, blocks
        self.rows = blocks * P
        self.groups = (N * top + EX * (self.rows - 1)) // self.rows if top > 1 else EX
        self.gate_w, self.gate_b, self.w1, self.b1, self.w2, self.b2 = gate_w, gate_b, w1, b1, w2, b2


FFN = (Experts(0, 2, 2, "f0_gate_w", "f0_gate_b", "f0_w1", "f0_b1", "f0_w2", "f0_b2"),
       Experts(1, 1, 4, "f1_gate_w", "f1_gate_b", "f1_w1", "f1_b1", "f1_w2", "f1_b2"))


def gate_logits(k, ffn):
    nc, a = k.nc, k.a
    BANKS = 2
    with ExitStack() as c:
        sem, sb, bank = makers(k, c, f"gl{ffn.layer}")
        w, bias = sb("w", [P, K, EX]), sb("b", [P, EX])
        xn, xt = sb("xn", [P, STEP, D]), sb("xt", [P, STEP, K * P])
        tp = [bank(f"tp{i}") for i in range(BANKS)]
        lp = [bank(f"lp{i}") for i in range(BANKS)]
        weights, xn_ready, turned, xt_ready, product, biased = map(sem, (
            "weights", "xn_ready", "turned", "xt_ready", "product", "biased"))
        block = c.enter_context(nc.Block())

        @block.sync
        def _(sp):
            sp.dma_start(w[:], a[ffn.gate_w]).then_inc(weights, 16)
            sp.dma_start(bias[:], a[ffn.gate_b].broadcast_to([P, EX])).then_inc(weights, 16)

        @block.vector
        def _(dve):
            dve.wait_ge(weights, 32)
            dve.sem_inc(biased, BANKS)
            with dve.Fori(0, NSTEP) as it:
                for j in range(STEP + 1):
                    if j < STEP:
                        dve.wait_ge(turned, it * STEP + j + 1)
                        normalise(k, xn[:, j, :], it * STEP + j).then_inc(xn_ready, 1)
                    if j > 0:
                        i = j - 1
                        dve.wait_ge(product, it * STEP + i + 1)
                        nc.vector.tensor_tensor(k.logits[:, bass.ds(it * STEP + i, 1), :].rearrange("p a e -> p (a e)"),
                                                lp[i % BANKS][:, 0:EX], bias[:], ALU.add).then_inc(biased, 1)
            dve.wait_ge(biased, NT + BANKS)

        @block.tensor
        def _(pe):
            pe.wait_ge(weights, 32)
            pe.sem_inc(turned, STEP)
            with pe.Fori(0, NSTEP) as it:
                for j in range(STEP + 1):
                    if j < STEP:
                        pe.wait_ge(xn_ready, it * STEP + j + 1)
                        pe.wait_ge(xt_ready, it * STEP + j + 1)
                        for b in range(K):
                            last = nc.tensor.transpose(tp[j % BANKS][:, b * P:(b + 1) * P],
                                                       xn[:, j, b * P:(b + 1) * P], k.ident[:])
                        last.then_inc(turned, 1)
                    if j > 0:
                        i = j - 1
                        pe.wait_ge(xt_ready, it * STEP + i + 1 + BANKS)
                        pe.wait_ge(biased, it * STEP + i + 1)
                        for b in range(K):
                            last = nc.tensor.matmul(lp[i % BANKS][:, 0:EX], xt[:, i, b * P:(b + 1) * P], w[:, b, :],
                                                    start=(b == 0), stop=(b == K - 1))
                        last.then_inc(product, 1)

        @block.scalar
        def _(act):
            act.sem_inc(xt_ready, BANKS)
            with act.Fori(0, NSTEP) as it:
                for j in range(STEP):
                    act.wait_ge(turned, it * STEP + j + 1 + STEP)
                    nc.scalar.copy(xt[:, j, :], tp[j % BANKS][:, 0:D]).then_inc(xt_ready, 1)


def route(k, ffn):
    nc, a = k.nc, k.a
    L, top = ffn.layer, ffn.top
    SH = [P, NT, EX]
    OUT = float(1 << 16)
    with ExitStack() as c:
        sem, sb, bank = makers(k, c, f"rt{L}")
        lg, eq, tmp = sb("lg", SH), sb("eq", SH), sb("tmp", SH)
        hot = [sb(f"hot{n}", SH) for n in range(top)]
        both, place, total, incl, excl = (sb(n, SH) for n in ("both", "place", "total", "incl", "excl"))
        rank = sb("rank", [P, EX])
        top_v = [sb(f"top{n}", [P, NT]) for n in range(top)]
        pick, node, out, slot = (sb(n, [P, NT]) for n in ("pick", "node", "out", "slot"))
        kept = sb("kept", [P, NT])
        upto, ones = sb("upto", [P, P]), sb("ones", [P, P])
        start, end = sb("start", [P, EX]), sb("end", [P, EX])
        count_i = sb("count_i", [P, EX], I32)
        groups = sb("groups", [1, ffn.groups, EX])
        group_f, group_n = sb("group_f", [1, ffn.groups]), sb("group_n", [1, ffn.groups])
        ps = [bank(f"ps{i}") for i in range(2)]
        made, done, counted, exped = map(sem, ("made", "done", "counted", "exped"))
        steps = [0]
        at = {}
        block = c.enter_context(nc.Block())
        flat = lambda t: t[:].rearrange("p t e -> p (t e)")
        over_e = lambda t: t[:].unsqueeze(2).broadcast_to(SH)
        over_t = lambda t: t[:].unsqueeze(1).broadcast_to(SH)

        @block.gpsimd
        def _(pool):
            g = nc.gpsimd
            g.iota(rank[:], [[-1, EX]], base=EX, channel_multiplier=0, allow_small_or_imprecise_dtypes=True
                   ).then_inc(made, 1)
            g.iota(node[:], [[P, NT]], base=0, channel_multiplier=1, allow_small_or_imprecise_dtypes=True
                   ).then_inc(made, 1)
            g.iota(group_n[:], [[1, ffn.groups]], base=0, channel_multiplier=0, allow_small_or_imprecise_dtypes=True
                   ).then_inc(made, 1)
            g.memset(ones[:], 1.0).then_inc(made, 1)
            pool.wait_ge(made, 4)
            g.affine_select(out=upto[:], in_=ones[:], compare_op=ALU.is_ge, fill=0.0, base=0, pattern=[[1, P]],
                            channel_multiplier=-1).then_inc(made, 1)

        @block.vector
        def _(dve):
            v = nc.vector

            def do(ins):
                steps[0] += 1
                ins.then_inc(done, 1)
                dve.wait_ge(done, steps[0])

            dve.wait_ge(made, 5)
            do(v.tensor_copy(flat(lg), k.logits[:].rearrange("p t e -> p (t e)")))
            for n in range(top):
                do(v.tensor_reduce(top_v[n][:], lg[:], AX, ALU.max))
                do(v.tensor_tensor(eq[:], lg[:], over_e(top_v[n]), ALU.is_equal))
                do(v.tensor_tensor(eq[:], eq[:], over_t(rank), ALU.mult))
                do(v.tensor_reduce(pick[:], eq[:], AX, ALU.max))
                do(v.tensor_tensor(hot[n][:], over_e(pick), over_t(rank), ALU.is_equal))
                if n + 1 < top:
                    do(v.scalar_tensor_tensor(out=flat(lg), in0=flat(hot[n]), scalar=NEG, in1=flat(lg),
                                              op0=ALU.mult, op1=ALU.add))
            do(v.tensor_scalar(out[:], node[:], float(N), None, ALU.is_ge))
            do(v.tensor_scalar(kept[:], out[:], -1.0, 1.0, ALU.mult, ALU.add))
            for n in range(top):
                do(v.tensor_tensor(hot[n][:], hot[n][:], over_e(kept), ALU.mult))
            if top == 2:
                do(v.tensor_tensor(both[:], hot[0][:], hot[1][:], ALU.add))
                do(v.tensor_tensor(pick[:], top_v[1][:], top_v[0][:], ALU.subtract))
                at["exp"] = steps[0]
                dve.wait_ge(exped, 1)
                do(v.tensor_scalar(k.weight[:, 0, :], pick[:], 1.0, None, ALU.add))
                do(v.reciprocal(k.weight[:, 0, :], k.weight[:, 0, :]))
                do(v.tensor_tensor(k.weight[:, 1, :], k.weight[:, 0, :], pick[:], ALU.mult))
            else:
                do(v.tensor_copy(flat(both), flat(hot[0])))
                do(v.tensor_tensor(lg[:], lg[:], over_e(top_v[0]), ALU.subtract))
                at["exp"] = steps[0]
                dve.wait_ge(exped, 1)
                do(v.tensor_reduce(k.weight[:, 0, :], lg[:], AX, ALU.add))
                do(v.reciprocal(k.weight[:, 0, :], k.weight[:, 0, :]))
            at["hot"] = steps[0]
            dve.wait_ge(counted, 1)
            do(v.tensor_copy(flat(total), ps[1][:, 0:NT * EX]))
            for e in range(EX):
                do(v.tensor_tensor_scan(incl[:, :, e], ones[:, 0:NT], total[:, :, e], 0.0, ALU.mult, ALU.add))
            do(v.tensor_tensor(excl[:], incl[:], total[:], ALU.subtract))
            do(v.tensor_tensor(flat(place), flat(excl), ps[0][:, 0:NT * EX], ALU.add))
            if top == 2:
                do(v.tensor_copy(count_i[:], incl[:, NT - 1, :]))
                do(v.tensor_scalar(count_i[:], count_i[:], float(ffn.rows - 1), None, ALU.add))
                do(v.tensor_scalar(count_i[:], count_i[:], ffn.rows.bit_length() - 1, None, ALU.arith_shift_right))
                do(v.tensor_copy(start[:], count_i[:]))
                do(v.tensor_tensor_scan(end[:], ones[:, 0:EX], start[:], 0.0, ALU.mult, ALU.add))
                do(v.tensor_tensor(start[:], end[:], start[:], ALU.subtract))
            else:
                do(v.tensor_scalar(start[:], rank[:], -1.0, float(EX), ALU.mult, ALU.add))
                do(v.tensor_scalar(end[:], start[:], 1.0, None, ALU.add))
            do(v.tensor_tensor(groups[:], group_n[:].unsqueeze(2).broadcast_to([1, ffn.groups, EX]),
                               end[0:1, :].unsqueeze(1).broadcast_to([1, ffn.groups, EX]), ALU.is_ge))
            do(v.tensor_reduce(group_f[:], groups[:], AX, ALU.add))
            do(v.tensor_scalar(group_f[:], group_f[:], float(EX - 1), None, ALU.min))
            do(v.tensor_copy(k.group_expert[:, 0:ffn.groups], group_f[:]))
            do(v.tensor_scalar(start[:], start[:], float(ffn.rows), -1.0, ALU.mult, ALU.add))
            for n in range(top):
                if top == 1:
                    do(v.tensor_tensor(tmp[:], place[:], hot[n][:], ALU.mult))
                    do(v.tensor_reduce(pick[:], tmp[:], AX, ALU.add))
                    do(v.tensor_scalar(kept[:], pick[:], float(CAP), None, ALU.is_le))
                    do(v.tensor_tensor(k.weight[:, 0, :], k.weight[:, 0, :], kept[:], ALU.mult))
                    do(v.tensor_scalar(pick[:], pick[:], float(CAP), None, ALU.is_gt))
                    do(v.tensor_tensor(out[:], out[:], pick[:], ALU.max))
                do(v.tensor_tensor(tmp[:], place[:], over_t(start), ALU.add))
                do(v.tensor_tensor(tmp[:], tmp[:], hot[n][:], ALU.mult))
                do(v.tensor_reduce(slot[:], tmp[:], AX, ALU.add))
                do(v.scalar_tensor_tensor(out=slot[:], in0=out[:], scalar=OUT, in1=slot[:], op0=ALU.mult, op1=ALU.add))
                do(v.tensor_copy(k.write_row[:, n, :], slot[:]))
                do(v.tensor_scalar(slot[:], slot[:], float(k.slots[L] - 1), None, ALU.min))
                do(v.tensor_copy(k.read_row[:, n, :], slot[:]))

        @block.scalar
        def _(act):
            act.wait_ge(done, at["exp"])
            t = pick[:] if top == 2 else flat(lg)
            nc.scalar.activation(t, t, ACT.Exp).then_inc(exped, 1)

        @block.tensor
        def _(pe):
            pe.wait_ge(made, 5)
            pe.wait_ge(done, at["hot"])
            nc.tensor.matmul(ps[0][:, 0:NT * EX], upto[:], flat(both), start=True, stop=True)
            nc.tensor.matmul(ps[1][:, 0:NT * EX], ones[:], flat(both), start=True, stop=True).then_inc(counted, 1)


def dispatch(k, ffn):
    nc = k.nc
    L, top = ffn.layer, ffn.top
    with ExitStack() as c:
        sem, sb, bank = makers(k, c, f"dp{L}")
        xn = sb("xn", [P, STEP, D])
        idx = sb("idx", [P, STEP, top], I32)
        ready, begun = sem("ready"), sem("begun")
        sent = [k.pool_sem(f"dp{L}_sent{j}") for j in range(STEP)]
        block = c.enter_context(nc.Block())

        @block.vector
        def _(dve):
            def step(it, first):
                for j in range(STEP):
                    if not first:
                        dve.wait_ge(sent[j], it * (16 * top))
                    normalise(k, xn[:, j, :], it * STEP + j).then_inc(ready, 1)
                    nc.vector.tensor_copy(idx[:, j, :], k.write_row[:, :, bass.ds(it * STEP + j, 1)]
                                          .rearrange("p n a -> p (n a)")[:, 0:top]).then_inc(ready, 1)

            step(0, True)
            with dve.Fori(1, NSTEP) as it:
                step(it, False)

        @block.gpsimd
        def _(pool):
            with pool.Fori(0, NSTEP) as it:
                for j in range(STEP):
                    pool.wait_ge(ready, it * (2 * STEP) + 2 * j + 2)
                    pool.sem_inc(begun, 1)
                    for n in range(top):
                        nc.gpsimd.indirect_dma_start(
                            out=k.x_buf[L][:, :], out_offset=bass.IndirectOffsetOnAxis(ap=idx[:, j, n:n + 1], axis=0),
                            in_=xn[:, j, :], in_offset=None, bounds_check=k.slots[L] - 1, oob_is_err=False
                        ).then_inc(sent[j], 16)
            for j in range(STEP):
                pool.wait_ge(sent[j], NSTEP * 16 * top)


def experts(k, ffn):
    nc, a = k.nc, k.a
    L, B, R = ffn.layer, ffn.blocks, ffn.rows
    HB = 3
    with ExitStack() as c:
        sem, sb, bank = makers(k, c, f"ex{L}")
        w1, w2 = sb("w1", [P, 2, K * F]), sb("w2", [P, 2, M * D])
        b1, b2 = sb("b1", [P, 2, M]), sb("b2", [P, 2, D])
        xb = sb("xb", [P, 2, B, D])
        xt = sb("xt", [P, 2, K, R])
        hid = sb("hid", [P, M, R])
        y = sb("y", [P, 2, B, D])
        tp = [bank(f"tp{i}") for i in range(K)]
        hp = [bank(f"hp{i}") for i in range(HB)]
        yp = [bank(f"yp{i}") for i in range(2)]
        w_in, x_in = ([sem(f"{n}{s}") for s in range(2)] for n in ("w_in", "x_in"))
        turned, xt_ready, product, relu, summed, copied, y_free = map(sem, (
            "turned", "xt_ready", "product", "relu", "summed", "copied", "y_free"))
        y_out = [k.pool_sem(f"ex{L}_y_out{s}") for s in range(2)]
        block = c.enter_context(nc.Block())
        PAIRS = ffn.groups // 2

        @block.sync
        def _(sp):
            def places(g):
                e = sp.value_load(k.group_expert[0:1, bass.ds(g, 1)], min_val=0, max_val=EX - 1)
                return (a[ffn.w1][bass.ds(e * P, P), :], a[ffn.w2][bass.ds(e * P, P), :],
                        a[ffn.b1][bass.ds(e * P, P), :], a[ffn.b2][bass.ds(e, 1), :].broadcast_to([P, D]),
                        tile_rows(k.x_buf[L], g * B, B))

            def load(s, of_w1, of_w2, of_b1, of_b2, of_x):
                sp.dma_start(xb[:, s, :, :], of_x).then_inc(x_in[s], 16)
                sp.dma_start(w1[:, s, :], of_w1).then_inc(w_in[s], 16)
                sp.dma_start(b1[:, s, :], of_b1).then_inc(w_in[s], 16)
                sp.dma_start(w2[:, s, :], of_w2).then_inc(w_in[s], 16)
                sp.dma_start(b2[:, s, :], of_b2).then_inc(w_in[s], 16)

            for s in range(2):
                load(s, *places(s))
            with sp.Fori(0, PAIRS - 1) as it:
                at = [places(it * 2 + 2 + s) for s in range(2)]
                used = [sp.snap(it * (2 * B) + B * (s + 1) + 2) for s in range(2)]
                for s in range(2):
                    sp.wait_ge(copied, used[s])
                    load(s, *at[s])

        @block.tensor
        def _(pe):
            def turn(g, s, turn_of):
                pe.wait_ge(x_in[s], turn_of * 16 + 16)
                pe.wait_ge(xt_ready, g * K + K)
                for kk in range(K):
                    for b in range(B):
                        last = nc.tensor.transpose(tp[kk][:, b * P:(b + 1) * P], xb[:, s, b, kk * P:(kk + 1) * P],
                                                   k.ident[:])
                    last.then_inc(turned, 1)

            def pair(it, final):
                for s in range(2):
                    g = it * 2 + s
                    pe.wait_ge(w_in[s], it * 64 + 64)
                    pe.wait_ge(xt_ready, g * K + 2 * K)
                    for m in range(M):
                        pe.wait_ge(relu, g * M + m + 1)
                        for kk in range(K):
                            last = nc.tensor.matmul(hp[m % HB][:, 0:R],
                                                    w1[:, s, kk * F + m * P:kk * F + (m + 1) * P], xt[:, s, kk, :],
                                                    start=(kk == 0), stop=(kk == K - 1))
                        last.then_inc(product, 1)
                    if not (final and s):
                        turn(g + 1, 1 - s, it + s)
                    pe.wait_ge(relu, g * M + M + HB)
                    for b in range(B):
                        pe.wait_ge(copied, g * B + b + 1)
                        for m in range(M):
                            last = nc.tensor.matmul(yp[b % 2][:, 0:D], hid[:, m, b * P:(b + 1) * P],
                                             w2[:, s, m * D:(m + 1) * D], start=(m == 0), stop=(m == M - 1))
                        last.then_inc(summed, 1)

            turn(0, 0, 0)
            with pe.Fori(0, PAIRS - 1) as it:
                pair(it, False)
            pair(PAIRS - 1, True)

        @block.scalar
        def _(act):
            act.sem_inc(xt_ready, K)
            act.sem_inc(relu, HB)

            def copy_turned(g, s):
                for kk in range(K):
                    act.wait_ge(turned, g * K + kk + 1)
                    nc.scalar.copy(xt[:, s, kk, :], tp[kk][:, 0:R]).then_inc(xt_ready, 1)

            def pair(it, final):
                for s in range(2):
                    g = it * 2 + s
                    act.wait_ge(w_in[s], it * 64 + 64)
                    for m in range(M):
                        act.wait_ge(product, g * M + m + 1)
                        nc.scalar.activation(hid[:, m, :], hp[m % HB][:, 0:R], ACT.Relu, bias=b1[:, s, m:m + 1]
                                             ).then_inc(relu, 1)
                    if not (final and s):
                        copy_turned(g + 1, 1 - s)

            copy_turned(0, 0)
            with act.Fori(0, PAIRS - 1) as it:
                pair(it, False)
            pair(PAIRS - 1, True)

        @block.vector
        def _(dve):
            dve.sem_inc(copied, 2)

            def pair(it, first):
                for s in range(2):
                    if not first:
                        dve.wait_ge(y_out[s], it * 16)
                    for b in range(B):
                        dve.wait_ge(summed, it * (2 * B) + s * B + b + 1)
                        nc.vector.tensor_tensor(y[:, s, b, :], yp[b % 2][:, 0:D], b2[:, s, :], ALU.add
                                                ).then_inc(copied, 1)

            pair(0, True)
            with dve.Fori(1, PAIRS) as it:
                pair(it, False)

        @block.gpsimd
        def _(pool):
            with pool.Fori(0, PAIRS) as it:
                for s in range(2):
                    g = it * 2 + s
                    rows = tile_rows(k.y_buf[L], g * B, B)
                    pool.wait_ge(copied, g * B + B + 2)
                    pool.sem_inc(y_free, 1)
                    pool.dma_start(rows, y[:, s, :, :]).then_inc(y_out[s], 16)
            for s in range(2):
                pool.wait_ge(y_out[s], PAIRS * 16)


def combine(k, ffn):
    nc = k.nc
    L, top = ffn.layer, ffn.top
    with ExitStack() as c:
        sem, sb, bank = makers(k, c, f"cb{L}")
        idx = sb("idx", [P, STEP, top], I32)
        g = sb("g", [P, STEP, top, D])
        part = sb("part", [P, STEP, D])
        mask = [sb(f"mask{i}", [P, STEP, D], I32) for i in range(3)]
        sub = [sb(f"sub{i}", [P, STEP, D]) for i in range(3)]
        ready, begun, masked, added, scaled, fixed, begun_fix, made = map(sem, (
            "ready", "begun", "masked", "added", "scaled", "fixed", "begun_fix", "made"))
        got = [k.pool_sem(f"cb{L}_got{j}") for j in range(STEP)]
        block = c.enter_context(nc.Block())
        row = lambda t: k.x[:, bass.ds(t, 1), :].rearrange("p a d -> p (a d)")

        @block.gpsimd
        def _(pool):
            with pool.Fori(0, NSTEP) as it:
                for j in range(STEP):
                    pool.wait_ge(ready, it * STEP + j + 1)
                    pool.sem_inc(begun, 1)
                    for n in range(top):
                        nc.gpsimd.indirect_dma_start(
                            out=g[:, j, n, :], out_offset=None, in_=k.y_buf[L][:, :],
                            in_offset=bass.IndirectOffsetOnAxis(ap=idx[:, j, n:n + 1], axis=0)).then_inc(got[j], 16)

        @block.vector
        def _(dve):
            v = nc.vector
            for t, value in zip(sub, (0.0, 1e4, -1e4)):
                v.memset(t[:], value).then_inc(made, 1)
            dve.wait_ge(made, 3)

            def ask(it, j):
                v.tensor_copy(idx[:, j, :], k.read_row[:, :, bass.ds(it * STEP + j, 1)]
                              .rearrange("p n a -> p (n a)")[:, 0:top]).then_inc(ready, 1)

            for j in range(STEP):
                ask(0, j)

            def add_two(it):
                for j in range(STEP):
                    t = it * STEP + j
                    dve.wait_ge(got[j], it * 32 + 32)
                    for n in range(2):
                        if n:
                            dve.wait_ge(added, t * 2 + 1)
                        v.scalar_tensor_tensor(out=row(t), in0=g[:, j, n, :], scalar=k.weight[:, n, bass.ds(t, 1)],
                                               in1=row(t), op0=ALU.mult, op1=ALU.add).then_inc(added, 1)

            def add_one(it):
                for j in range(STEP):
                    dve.wait_ge(got[j], it * 16 + 16)
                    v.tensor_scalar(part[:, j, :], g[:, j, 0, :], k.weight[:, 0, bass.ds(it * STEP + j, 1)], None,
                                    ALU.mult).then_inc(scaled, 1)
                dve.wait_ge(scaled, it * STEP + STEP)
                v.tensor_tensor(mask[0][:], part[:], part[:], ALU.not_equal).then_inc(masked, 1)
                v.tensor_scalar(mask[1][:], part[:], FMAX, None, ALU.is_gt).then_inc(masked, 1)
                v.tensor_scalar(mask[2][:], part[:], -FMAX, None, ALU.is_lt).then_inc(masked, 1)
                for i in range(3):
                    dve.wait_ge(masked, it * 3 + 3)
                    if i:
                        dve.wait_ge(fixed, it * 3 + i)
                    dve.sem_inc(begun_fix, 1)
                    v.copy_predicated(part[:], mask[i][:], sub[i][:]).then_inc(fixed, 1)
                dve.wait_ge(fixed, it * 3 + 3)
                rows = k.x[:, bass.ds(it * STEP, STEP), :]
                v.tensor_tensor(rows, rows, part[:], ALU.add).then_inc(added, 1)

            add = add_two if top == 2 else add_one
            with dve.Fori(0, NSTEP - 1) as it:
                add(it)
                for j in range(STEP):
                    ask(it + 1, j)
            add(NSTEP - 1)
            dve.wait_ge(added, NT * 2 if top == 2 else NSTEP)


def mixture(k, ffn):
    layer_stats(k, f"ffn{ffn.layer}")
    gate_logits(k, ffn)
    route(k, ffn)
    dispatch(k, ffn)
    experts(k, ffn)
    combine(k, ffn)


def degrees(k):
    nc, a = k.nc, k.a
    with ExitStack() as c:
        sem, sb, bank = makers(k, c, "dg")
        src, hi, lo = (sb(n, [P, ET], I32) for n in ("src", "hi", "lo"))
        tile_hot = sb("tile_hot", [P, 2, BODY, NT], BF16)
        place_hot = sb("place_hot", [P, 2, BODY, P], BF16)
        deg = sb("deg", [NT, P])
        cols = sb("cols", [P, NT, 2])
        ps = [bank(f"ps{i}") for i in range(2)]
        loaded, split, hot, counted, added, root, done, turned, stored = map(sem, (
            "loaded", "split", "hot", "counted", "added", "root", "done", "turned", "stored"))
        block = c.enter_context(nc.Block())

        @block.sync
        def _(sp):
            sp.dma_start(src[:], a["src_cols"]).then_inc(loaded, 16)
            sp.wait_ge(done, 1)
            sp.dma_start(k.deg_d, deg[:]).then_inc(stored, 16)
            sp.wait_ge(stored, 16)
            sp.dma_start(k.dinv_row[:, 0:NP], k.deg_d.rearrange("t p -> (t p)").unsqueeze(0).broadcast_to([P, NP])
                         ).then_inc(stored, 16)
            sp.wait_ge(turned, 3)
            with nc.allow_non_contiguous_dma(reason="two numbers for each row of the table"):
                sp.dma_start(k.xl_table[:, D:XROW].rearrange("(t p) c -> p t c", p=P), cols[:]
                             ).then_inc(stored, 16)
            sp.wait_ge(stored, 48)

        @block.vector
        def _(dve):
            v = nc.vector
            dve.wait_ge(loaded, 16)
            v.tensor_scalar(hi[:], src[:], 7, None, ALU.arith_shift_right).then_inc(split, 1)
            v.tensor_scalar(lo[:], src[:], P - 1, None, ALU.bitwise_and).then_inc(split, 1)
            v.memset(deg[:], 1.0).then_inc(split, 1)
            dve.wait_ge(split, 3)

            def pair(it, first):
                for s in range(2):
                    n = it * 2 + s
                    if not first:
                        dve.wait_ge(counted, n - 1)
                    cols16 = bass.ds(n * BODY, BODY)
                    for src_of, of, width in ((hi, tile_hot, NT), (lo, place_hot, P)):
                        shape = [P, BODY, width]
                        v.tensor_tensor(of[:, s, :, :], k.iota_row[:, 0:width].unsqueeze(1).broadcast_to(shape),
                                        src_of[:, cols16].unsqueeze(2).broadcast_to(shape), ALU.is_equal
                                        ).then_inc(hot, 1)

            pair(0, True)
            with dve.Fori(1, ITERS // 2) as it:
                pair(it, False)
            dve.wait_ge(counted, ITERS)
            v.tensor_tensor(deg[:], deg[:], ps[0][0:NT, 0:P], ALU.add).then_inc(added, 1)
            dve.wait_ge(root, 1)
            v.reciprocal(deg[:], deg[:]).then_inc(done, 1)
            dve.wait_ge(turned, 1)
            v.tensor_copy(cols[:, :, 0], ps[1][:, 0:NT]).then_inc(turned, 1)
            v.tensor_scalar(cols[:, :, 1], ps[1][:, 0:NT], -1.0, None, ALU.mult).then_inc(turned, 1)

        @block.tensor
        def _(pe):
            def pair(it, first=False, final=False):
                for s in range(2):
                    pe.wait_ge(hot, (it * 2 + s) * 2 + 2)
                    for j in range(BODY):
                        last = nc.tensor.matmul(ps[0][0:NT, 0:P], tile_hot[:, s, j, :], place_hot[:, s, j, :],
                                                start=(first and s == 0 and j == 0),
                                                stop=(final and s == 1 and j == BODY - 1))
                    last.then_inc(counted, 1)

            pair(0, first=True)
            with pe.Fori(1, ITERS // 2 - 1) as it:
                pair(it)
            pair(ITERS // 2 - 1, final=True)
            pe.wait_ge(done, 1)
            nc.tensor.transpose(ps[1][:, 0:NT], deg[:], k.ident[0:NT, 0:NT]).then_inc(turned, 1)

        @block.scalar
        def _(act):
            act.wait_ge(added, 1)
            nc.scalar.activation(deg[:], deg[:], ACT.Sqrt).then_inc(root, 1)


def features_first(k):
    nc = k.nc
    BANKS = 4
    with ExitStack() as c:
        sem, sb, bank = makers(k, c, "ff")
        xn = sb("xn", [P, STEP, D])
        tp = [bank(f"tp{i}") for i in range(STEP)]
        xn_ready, turned, copied = map(sem, ("xn_ready", "turned", "copied"))
        block = c.enter_context(nc.Block())

        @block.vector
        def _(dve):
            with dve.Fori(0, NSTEP) as it:
                for j in range(STEP):
                    dve.wait_ge(turned, it * STEP + j + 1)
                    normalise(k, xn[:, j, :], it * STEP + j).then_inc(xn_ready, 1)

        @block.tensor
        def _(pe):
            pe.sem_inc(turned, STEP)
            with pe.Fori(0, NSTEP) as it:
                for j in range(STEP):
                    pe.wait_ge(xn_ready, it * STEP + j + 1)
                    pe.wait_ge(copied, it * STEP + j + 1)
                    for b in range(K):
                        last = nc.tensor.transpose(tp[j][:, b * P:(b + 1) * P], xn[:, j, b * P:(b + 1) * P],
                                                   k.ident[:])
                    last.then_inc(turned, 1)

        @block.scalar
        def _(act):
            act.sem_inc(copied, STEP)
            with act.Fori(0, NSTEP) as it:
                for j in range(STEP):
                    act.wait_ge(turned, it * STEP + j + 1 + STEP)
                    nc.scalar.copy(k.h[:, :, bass.ds((it * STEP + j) * P, P)],
                                   tp[j][:, 0:D].rearrange("p (b n) -> p b n", b=K)).then_inc(copied, 1)


CHUNK = 512
CHUNKS = [(i, min(CHUNK, NP - i)) for i in range(0, NP, CHUNK)]


def graph_layer_inputs(k, l):
    nc, a, g = k.nc, k.a, k.gl
    w, row, tb = g.w, g.rows, g.banks[0:4]

    block = g.open()

    @block.sync
    def _(sp):
        sp.dma_start(w[:], a["g1_w"][bass.ds(l * P, P), :].rearrange("p (b d) -> p b d", b=K)).then_inc(g.weights, 16)
        sp.dma_start(g.bias[:], a["g1_bias"][bass.ds(l, 1), :].broadcast_to([P, 2 * D])).then_inc(g.weights, 16)
        sp.dma_start(g.cols[:], a["g1_cols"][bass.ds(l * P, P), :]).then_inc(g.weights, 16)
        sp.dma_start(g.we[:], a["g1_we"][bass.ds(l * P, P), :]).then_inc(g.weights, 16)
        for s in range(NSTEP):
            sp.wait_ge(g.biased, STEP * (s + 1))
            sp.dma_start(tile_rows(k.xl_table, s * STEP, STEP, 0, D), row[:, s % 2, :, :]).then_inc(g.stored[s % 2], 16)
        for s in range(2):
            sp.wait_ge(g.stored[s], 16 * ((NSTEP + 1 - s) // 2))

    @block.tensor
    def _(pe):
        pe.wait_ge(g.weights, 64)
        for t in range(NT):
            if t >= 4:
                pe.wait_ge(g.biased, t - 3)
            for kk in range(K):
                last = nc.tensor.matmul(tb[t % 4][:, 0:D], k.h[:, kk, t * P:(t + 1) * P], w[:, kk, :],
                                        start=(kk == 0), stop=(kk == K - 1))
            last.then_inc(g.xl_ready, 1)

    @block.gpsimd
    def _(pool):
        nc.gpsimd.memset(k.agg[:], 0.0).then_inc(g.cleared_agg, 1)
        pool.wait_ge(g.cleared_agg, 1)

    @block.vector
    def _(dve):
        v = nc.vector
        dve.wait_ge(g.weights, 64)
        v.tensor_tensor(g.rowb[:], g.bias[:, 0:D], g.bias[:, D:2 * D], ALU.add).then_inc(g.summed_bias, 1)
        v.tensor_tensor(g.rootb[:], g.cols[:, 0:K], g.cols[:, K:2 * K], ALU.add).then_inc(g.summed_bias, 1)
        dve.wait_ge(g.summed_bias, 2)
        for t in range(NT):
            s = t // STEP
            if t % STEP == 0 and s >= 2:
                dve.wait_ge(g.stored[s % 2], 16 * (s // 2))
            dve.wait_ge(g.xl_ready, t + 1)
            v.tensor_tensor(row[:, s % 2, t % STEP, :], tb[t % 4][:, 0:D], g.rowb[:], ALU.add).then_inc(g.biased, 1)

    g.close()


def graph_layer_edges(k, l):
    nc, a, g = k.nc, k.a, k.gl
    EB, SB = 2, 8
    START_AT = BODY - LAG
    ep, ps, rp = g.banks[0:EB], g.banks[EB:EB + SB // 2], g.banks[EB + SB // 2]
    start = g.start
    block = g.open()

    @block.sync
    def _(sp):
        def places(q, it):
            cols = bass.ds(it * (BODY * P) + q * HALF * P, HALF * P)
            return a["src_halves"][bass.ds(it * 2 + q, 1)].rearrange("a p j -> (a p) j"), a["ea128"][:, cols]

        def load(q, of_idx, of_ea):
            sp.dma_start(g.idx[:, q, :], of_idx).then_inc(g.idx_in[q], 16)
            sp.dma_start(g.ea[:, q, :], of_ea).then_inc(g.ea_in[q], 16)

        for q in range(2):
            load(q, *places(q, 0))
        with sp.Fori(0, ITERS - 1) as it:
            at = [places(q, it + 1) for q in range(2)]
            used = [sp.snap(it * (BODY // 2) + HALF // 2 * (q + 1) + EB) for q in range(2)]
            for q in range(2):
                sp.wait_ge(g.raw, used[q])
                load(q, *at[q])

    @block.gpsimd
    def _(pool):
        def gather(q, it, first):
            pool.wait_ge(g.idx_in[q], 16 if first else it * 16 + 16)
            if not first:
                pool.wait_ge(g.raw, it * (BODY // 2) - BODY // 2 + HALF // 2 * (q + 1) + EB)
                pool.wait_ge(g.hot, it * (BODY // 2) - BODY // 2 + HALF // 2 * (q + 1))
                pool.wait_ge(g.act_hot, it * (BODY // 2) - BODY // 2 + HALF // 2 * (q + 1) + 2)
            pool.sem_inc(g.begun, 1)
            for j in range(q * HALF, q * HALF + HALF):
                nc.gpsimd.indirect_dma_start(
                    out=g.g[:, j, :], out_offset=None, in_=k.xl_table[:, :],
                    in_offset=bass.IndirectOffsetOnAxis(ap=g.idx[:, q, j % HALF:j % HALF + 1], axis=0)
                ).then_inc(g.src_in[j], 16)

        for q in range(2):
            gather(q, 0, True)
        with pool.Fori(1, ITERS) as it:
            for q in range(2):
                gather(q, it, False)

    @block.tensor
    def _(pe):
        pe.sem_inc(g.summed, BODY)

        def products(it, u):
            if u % (HALF // 2) == 0:
                pe.wait_ge(g.ea_in[u // (HALF // 2)], it * 16 + 16)
            pe.wait_ge(g.raw, it * (BODY // 2) + u + 1)
            q, at = (2 * u) // HALF, (2 * u) % HALF
            for i in range(2):
                last = nc.tensor.matmul(ep[u % EB][:, i * D:(i + 1) * D], g.ea[:, q, (at + i) * P:(at + i + 1) * P],
                                        g.we[:], start=True, stop=True)
            last.then_inc(g.product, 1)

        def sums(it, u):
            pe.wait_ge(g.relu, it * (BODY // 2) + u + 1)
            pe.wait_ge(g.hot, it * (BODY // 2) + u + 1)
            pe.wait_ge(g.act_hot, it * (BODY // 2) + u + 1 + 2)
            pe.wait_ge(g.added, it * BODY + 2 * u + 2)
            for i in range(2):
                j = 2 * u + i
                for b in range(K):
                    at = i * D + b * P
                    last = nc.tensor.matmul(ps[u % (SB // 2)][:, at:at + P], g.msg[:, j, b * P:(b + 1) * P],
                                            g.onehot[:, j, :], start=True, stop=True)
            last.then_inc(g.summed, 2)

        def node_tile(it):
            pe.wait_ge(g.rooted, it * K + K)
            for b in range(K):
                for kk in range(K):
                    last = nc.tensor.matmul(rp[:, b * P:(b + 1) * P], g.w[:, kk, b * P:(b + 1) * P],
                                            k.h[:, kk, bass.ds(it * P, P)], start=(kk == 0), stop=(kk == K - 1))
            last.then_inc(g.xlt_ready, 1)

        def body(it, final):
            for u in range(BODY // 2):
                if u + 2 < BODY // 2:
                    products(it, u + 2)
                elif not final:
                    products(it + 1, u + 2 - BODY // 2)
                sums(it, u)
                if u == 1:
                    node_tile(it)

        products(0, 0)
        products(0, 1)
        with pe.Fori(0, ITERS - 1) as it:
            body(it, False)
        body(ITERS - 1, True)

    @block.scalar
    def _(act):
        act.sem_inc(g.rooted, K)
        act.sem_inc(g.act_hot, 2)

        def hot_tile(it, j, seen):
            n = it * (BODY // 2) + j // 2
            act.wait_ge(g.src_in[j], seen)
            act.wait_ge(g.summed, it * BODY + j + 1)
            act.wait_ge(g.act_hot, n + 1)
            nc.scalar.activation(g.away[:, j // 2 % 2, :], k.iota_row[:], ACT.Abs, bias=k.dst_rel[:, bass.ds(it * BODY + j, 1)],
                                 scale=-1.0).then_inc(g.distance, 1)
            act.wait_ge(g.distance, n + 1)
            nc.scalar.activation(g.onehot[:, j, :], g.away[:, j // 2 % 2, :], ACT.Relu, bias=g.g[:, j, D:D + 1],
                                 scale=g.g[:, j, D + 1:XROW]).then_inc(g.act_hot, 1)

        with act.Fori(0, ITERS) as it:
            seen = it * 16 + l * (16 * ITERS) + 16
            for u in range(BODY // 2):
                hot_tile(it, 2 * u + 1, seen)
                if u == 3:
                    act.wait_ge(g.xlt_ready, it + 1)
                    act.wait_ge(g.started, it * 2 + 2)
                    for b in range(K):
                        nc.scalar.activation(start[:, b, :], rp[:, b * P:(b + 1) * P], ACT.Relu,
                                             bias=g.rootb[:, b:b + 1]).then_inc(g.rooted, 1)
                act.wait_ge(g.raw, it * (BODY // 2) + u + 1 + EB)
                m = g.msg[:, 2 * u:2 * u + 2, :].rearrange("p a d -> p (a d)")
                nc.scalar.activation(m, m, ACT.Relu).then_inc(g.relu, 1)

    @block.vector
    def _(dve):
        base_regs = [dve.alloc_register(f"g1_base{i}") for i in range(BODY)]
        dve.sem_inc(g.raw, EB)
        dve.sem_inc(g.added, SB)
        dve.sem_inc(g.started, 2)

        def add_pair(it, u, seen):
            dve.wait_ge(g.product, it * (BODY // 2) + u + 1)
            dve.wait_ge(g.src_in[2 * u], seen)
            dve.wait_ge(g.src_in[2 * u + 1], seen)
            dve.wait_ge(g.summed, it * BODY + 2 * u + 2)
            nc.vector.tensor_tensor(g.msg[:, 2 * u:2 * u + 2, :], g.g[:, 2 * u:2 * u + 2, 0:D],
                                    ep[u % EB][:, 0:2 * D].rearrange("p (a d) -> p a d", a=2), ALU.add
                                    ).then_inc(g.raw, 1)

        def hot_tile(it, j):
            nc.vector.tensor_scalar(g.onehot[:, j, :], k.iota_row[:], k.dst_rel[:, bass.ds(it * BODY + j, 1)],
                                    g.g[:, j, D:D + 1], ALU.is_equal, ALU.mult).then_inc(g.hot, 1)

        def add_sums(n, u, i, base):
            dve.wait_ge(g.summed, n + 2 + BODY)
            window = k.agg[:, :, bass.ds(base, P)]
            dve.wait_ge(g.added, n + i + SB)
            nc.vector.tensor_tensor(window, window, ps[u % (SB // 2)][:, i * D:(i + 1) * D]
                                    .rearrange("p (b n) -> p b n", b=K), ALU.add).then_inc(g.added, 1)

        def start_tile(it, step):
            nodes = bass.ds(it * P, P)
            if step == 0:
                dve.wait_ge(g.rooted, it * K + 2 * K)
                nc.vector.tensor_tensor(start[:], start[:], k.dinv_row[:, nodes].unsqueeze(1).broadcast_to([P, K, P]),
                                        ALU.mult).then_inc(g.started, 1)
            else:
                dve.wait_ge(g.started, it * 2 + 3)
                dve.wait_ge(g.added, it * BODY + START_AT + SB)
                nc.vector.tensor_tensor(k.agg[:, :, nodes], k.agg[:, :, nodes], start[:], ALU.add
                                        ).then_inc(g.started, 1)
                dve.wait_ge(g.started, it * 2 + 4)

        def body(it, first):
            seen = it * 16 + l * (16 * ITERS) + 16
            for u in range(BODY // 2):
                add_pair(it, u, seen)
                if u == 0:
                    bases = lagging_bases(k, dve, base_regs, it * BODY)
                for i in range(2):
                    if 2 * u >= LAG or not first:
                        add_sums(it * BODY + 2 * u - LAG, u - LAG // 2, i, bases[2 * u + i])
                    if i == 0:
                        hot_tile(it, 2 * u)
                    if u == BODY // 2 - 2 + i and i == 0:
                        start_tile(it, 0)
                if u == BODY // 2 - 1:
                    start_tile(it, 1)

        body(0, True)
        with dve.Fori(1, ITERS) as it:
            body(it, False)
        for i, base in enumerate(lagging_bases(k, dve, base_regs[0:LAG], ET)):
            add_sums(ET - LAG + i // 2 * 2, (BODY - LAG + i) // 2, i % 2, base)
        dve.wait_ge(g.added, ET + SB)

    g.close()


def graph_layer_norm(k, l):
    nc, g = k.nc, k.gl
    stats, mv, s = g.stats, g.mv, g.scale
    parts = [(i, min(CHUNK, N - i)) for i in range(0, N, CHUNK)]
    block = g.open()

    @block.vector
    def _(dve):
        v = nc.vector
        for b in range(K):
            for n, (at, width) in enumerate(CHUNKS):
                v.tensor_tensor(k.agg[:, b, at:at + width], k.agg[:, b, at:at + width], k.dinv_row[:, at:at + width],
                                ALU.mult).then_inc(g.conv, 1)
        for b in range(K):
            for n, (at, width) in enumerate(parts):
                dve.wait_ge(g.conv, b * len(CHUNKS) + n + 1)
                v.bn_stats(stats[:, b, n, :], k.agg[:, b, at:at + width]).then_inc(g.stat, 1)
        for b in range(K):
            dve.wait_ge(g.stat, (b + 1) * len(parts))
            v.bn_aggr(mv[:, b, :], stats[:, b, :, :].rearrange("p n s -> p (n s)")).then_inc(g.stat, 1)
            dve.wait_ge(g.stat, (b + 1) * len(parts))
        dve.wait_ge(g.stat, K * len(parts) + K)
        dve.wait_ge(g.root, 1)
        v.reciprocal(s[:, 0, :], s[:, 0, :]).then_inc(g.step, 1)
        dve.wait_ge(g.step, 1)
        v.tensor_tensor(s[:, 0, :], s[:, 0, :], g.cols[:, 2 * K:3 * K], ALU.mult).then_inc(g.step, 1)
        dve.wait_ge(g.step, 2)
        v.tensor_tensor(s[:, 1, :], s[:, 0, :], mv[:, :, 0], ALU.mult).then_inc(g.step, 1)
        dve.wait_ge(g.step, 3)
        v.tensor_tensor(s[:, 1, :], g.cols[:, 3 * K:4 * K], s[:, 1, :], ALU.subtract).then_inc(g.step, 1)
        n = 0
        for b in range(K):
            for at, width in CHUNKS:
                dve.wait_ge(g.scaled, n + 1)
                v.scalar_tensor_tensor(out=k.h[:, b, at:at + width], in0=k.agg[:, b, at:at + width],
                                       scalar=k.floor[:, bass.ds(l, 1)], in1=k.h[:, b, at:at + width],
                                       op0=ALU.max, op1=ALU.add).then_inc(g.updated, 1)
                n += 1
        dve.wait_ge(g.updated, n)

    @block.scalar
    def _(act):
        act.wait_ge(g.stat, K * len(parts) + K)
        nc.scalar.activation(s[:, 0, :], mv[:, :, 1], ACT.Sqrt, bias=k.eps[:, 0:1]).then_inc(g.root, 1)
        act.wait_ge(g.step, 4)
        for b in range(K):
            for at, width in CHUNKS:
                nc.scalar.activation(k.agg[:, b, at:at + width], k.agg[:, b, at:at + width], ACT.Identity,
                                     bias=s[:, 1, b:b + 1], scale=s[:, 0, b:b + 1]).then_inc(g.scaled, 1)

    g.close()


class GraphLayers:

    def __init__(self, k, c):
        self.nc = nc = k.nc
        sem, sb, bank = makers(k, c, "g1")
        self.w, self.we = sb("w", [P, K, D]), sb("we", [P, D])
        self.bias, self.rowb = sb("bias", [P, 2 * D]), sb("rowb", [P, D])
        self.cols, self.rootb = sb("cols", [P, 4 * K]), sb("rootb", [P, K])
        self.rows = sb("rows", [P, 2, STEP, D])
        self.start = sb("start", [P, K, P])
        self.idx, self.ea = sb("idx", [P, 2, HALF], I32), sb("ea", [P, 2, HALF * P])
        self.g, self.msg = sb("g", [P, BODY, XROW]), sb("msg", [P, BODY, D])
        self.away = sb("away", [P, 2, P])
        self.onehot = sb("onehot", [P, BODY, P])
        self.stats, self.mv, self.scale = sb("stats", [P, K, -(-N // CHUNK), 6]), sb("mv", [P, K, 2]), sb("scale", [P, 2, K])
        self.banks = [bank(f"b{i}") for i in range(8)]
        self.src_in = [k.pool_sem(f"g1_src_in{j}") for j in range(BODY)]
        self.stored = [sem(f"stored{i}") for i in range(2)]
        self.idx_in = [sem(f"idx_in{i}") for i in range(2)]
        self.ea_in = [sem(f"ea_in{i}") for i in range(2)]
        (self.weights, self.xl_ready, self.xlt_ready, self.rooted, self.biased, self.started, self.summed_bias,
         self.begun, self.raw, self.product, self.hot, self.relu, self.summed, self.added,
         self.cleared_agg, self.act_hot, self.distance, self.conv, self.stat, self.root, self.step, self.scaled, self.updated) = made = [sem(n) for n in (
             "weights", "xl_ready", "xlt_ready", "rooted", "biased", "started", "summed_bias",
             "begun", "raw", "product", "hot", "relu", "summed", "added",
             "cleared_agg", "act_hot", "distance", "conv", "stat", "root", "step", "scaled", "updated")]
        self.cleared = made + self.stored + self.idx_in + self.ea_in

    def open(self):
        self.stack = ExitStack()
        return self.stack.enter_context(self.nc.Block())

    def close(self):
        self.stack.close()


def graph_layers(k):
    nc = k.nc
    with ExitStack() as c:
        g = k.gl = GraphLayers(k, c)
        with nc.Fori(0, LAYERS) as l:
            graph_layer_inputs(k, l)
            graph_layer_edges(k, l)
            graph_layer_norm(k, l)
            with nc.Block() as block:
                @block.gpsimd
                def _(pool):
                    for s in g.cleared:
                        pool.sem_clear(s)


def finish(k):
    nc = k.nc
    whole, rest = N // P, N % P
    with nc.semaphore("written") as written, nc.Block() as block:
        @block.sync
        def _(sp):
            out = k.a["out"]
            sp.dma_start(out[0:whole * P, :].rearrange("(t p) d -> p t d", p=P), k.x[:, 0:whole, :]).then_inc(written, 16)
            sp.dma_start(out[whole * P:N, :], k.x[0:rest, whole, :]).then_inc(written, 16)
            sp.wait_ge(written, 32)


def host_arrays(inp):
    f = {n: np.asarray(v) for n, v in inp.items()}

    def pad(v, rows, fill=0):
        out = np.full((rows,) + v.shape[1:], fill, v.dtype)
        out[:v.shape[0]] = v
        return out

    def blocks(v, n):
        return v.reshape(n, P, v.shape[-1]).transpose(1, 0, 2)

    src, dst = pad(f["src"], EP, NP - 1), pad(f["dst"], EP, N)
    ea3 = np.ones((4, EP), np.float32)
    ea3[:3] = pad(f["edge_attr_3"], EP).T
    out = {
        "x": pad(f["x"], NP),
        "dst_cols": dst.reshape(ET, P).T,
        "dst_first": dst[::P][None],
        "src_halves": src.reshape(ET // HALF, HALF, P).transpose(0, 2, 1),
        "src_cols": src.reshape(ET, P).T,
        "dst_row": dst[None],
        "dst_chunk": dst.reshape(P, ET),
        "dst_chunk_first": dst[::ET][None],
        "dst_chunk_last": dst[ET - 1::ET][None],
        "ea3": ea3,
        "ea128": pad(f["edge_attr_128"], EP).T,
        "gat_w": blocks(f["L0_gnn_W"].T, K),
        "gat_asrc": f["L0_gnn_a_src"].reshape(1, D),
        "gat_adst": f["L0_gnn_a_dst"].reshape(1, D),
        "gat_ew": np.concatenate([f["L0_gnn_edge_W"].T, f["L0_gnn_edge_b"][None]]),
        "gat_bias": f["L0_gnn_bias"].reshape(K, P).T,
    }

    def first(w):
        return w.reshape(EX, K, P, F).transpose(0, 2, 1, 3).reshape(EX * P, K * F)

    def second(w):
        return w.reshape(EX, M, P, D).transpose(0, 2, 1, 3).reshape(EX * P, M * D)

    def hidden_bias(b):
        return b.reshape(EX, M, P).transpose(0, 2, 1).reshape(EX * P, M)

    out |= {
        "g1_w": f["L1_gnn_W"].reshape(LAYERS, K, P, D).transpose(0, 2, 1, 3).reshape(LAYERS * P, K * D),
        "g1_we": f["L1_gnn_We"].reshape(LAYERS * P, D),
        "g1_bias": np.concatenate([f["L1_gnn_b"], f["L1_gnn_be"]], 1),
        "g1_cols": np.concatenate([f[n].reshape(LAYERS, K, P).transpose(0, 2, 1).reshape(LAYERS * P, K) for n in
                                   ("L1_gnn_b", "L1_gnn_root", "L1_gnn_gamma", "L1_gnn_beta")], 1),
        "f0_gate_w": blocks(f["L0_ffn_Wg"].T, K), "f0_gate_b": f["L0_ffn_bg"][None],
        "f0_w1": first(f["L0_ffn_W1"].transpose(0, 2, 1)), "f0_b1": hidden_bias(f["L0_ffn_b1"]),
        "f0_w2": second(f["L0_ffn_W2"].transpose(0, 2, 1)), "f0_b2": f["L0_ffn_b2"],
        "f1_gate_w": blocks(f["L1_ffn_gate_w"], K), "f1_gate_b": f["L1_ffn_gate_b"][None],
        "f1_w1": first(f["L1_ffn_w1"]), "f1_b1": hidden_bias(f["L1_ffn_b1"]),
        "f1_w2": second(f["L1_ffn_w2"]), "f1_b2": f["L1_ffn_b2"],
    }
    return {n: np.ascontiguousarray(v) for n, v in out.items()}


STAGES = [
    constants,
    edge_feature_parts,
    lambda k: layer_stats(k, "ln1"),
    attention_tables,
    edge_scores,
    softmax_over_edges,
    attention_sums,
    lambda k: add_features_first(k, "gat_out", k.agg, "gat_bias"),
    lambda k: mixture(k, FFN[0]),
    Kernel.recycle,
    degrees,
    lambda k: layer_stats(k, "ln3"),
    features_first,
    graph_layers,
    lambda k: add_features_first(k, "graph_out", k.h, None),
    lambda k: mixture(k, FFN[1]),
    finish,
]


def program(nc, a, stages=None, after=None):
    ctx = ExitStack()
    with ctx:
        k = Kernel(nc, a, ctx)
        for stage in STAGES[:stages]:
            stage(k)
        if after:
            after(k)


def kernel(**inputs):
    import concourse.bacc as bacc
    from concourse.bass_utils import run_bass_kernel_spmd

    nc = bacc.Bacc("TRN2", target_bir_lowering=False, num_devices=1)
    arrays = {f"in_{n}": v for n, v in host_arrays(inputs).items()}
    a = {n[3:]: nc.dram_tensor(n, v.shape, mybir.dt.from_np(v.dtype), kind="ExternalInput").ap()
         for n, v in arrays.items()}
    a["out"] = nc.dram_tensor("out", (N, D), F32, kind="ExternalOutput").ap()
    program(nc, a)
    return run_bass_kernel_spmd(nc, [arrays], core_ids=[0]).results[0]["out"]
```
